# Optimizing a Trainium2 kernel written in Bass

```python
import numpy as np
import jax
import jax.numpy as jnp

def _softmax(x, axis=-1):
    return jax.nn.softmax(x, axis=axis)

def _gelu(x):
    return jax.nn.gelu(x, approximate=True)

def _silu(x):
    return jax.nn.silu(x)

def _sigmoid(x):
    return jax.nn.sigmoid(x)

def _layernorm(x, axis=-1, eps=1e-05):
    m = jnp.mean(x, axis=axis, keepdims=True)
    v = jnp.var(x, axis=axis, keepdims=True)
    return (x - m) / jnp.sqrt(v + eps)

def _scatter_add(tgt, idx, src, axis=0):
    return tgt.at[idx].add(src)

def _segment_sum(src, seg, n):
    return jax.ops.segment_sum(src, seg, n)
kernel_name = 'mk_gnn_resnorm_d2_gnn_r32_e14e48'

def setup_inputs(seed: int=0):
    np.random.seed(seed)
    _w = jnp.asarray

    def _rec_inputs():
        import jax
        import jax.numpy as jnp
        _gk = jax.random.key(seed)
        x = -0.0005121 + 1.001 * jax.random.normal(jax.random.fold_in(_gk, 1), (3125, 64), jnp.float32)
        src = jax.random.randint(jax.random.fold_in(_gk, 2), (100000,), 0, 3125, jnp.int32)
        dst = jnp.minimum((3125 * jax.random.uniform(jax.random.fold_in(_gk, 3), (100000,)) ** 2.0).astype(jnp.int32), 99999)
        _o = jnp.argsort(dst, stable=True)
        src = src[_o]
        dst = dst[_o]
        edge_attr_3 = 0.000669165 + 0.999965 * jax.random.normal(jax.random.fold_in(_gk, 11), (100000, 3), jnp.float32)
        edge_weight1 = jax.random.uniform(jax.random.fold_in(_gk, 13), (100000, 1), jnp.float32, 0.0, 9.99999)
        return (x, src, dst, edge_attr_3, edge_weight1)
    x, src, dst, edge_attr_3, edge_weight1 = _rec_inputs()

    def _L0_gnn_setup():
        import jax, jax.numpy as jnp
        import numpy as np
        N, E, L, HEADS, HID = (50000, 18750, 4, 8, 128)
        IN_C, OUT_C = (64, 64)
        D_HEAD = HID // HEADS

        def _layer_norm(x, g, b, eps=1e-05):
            m = jnp.mean(x, axis=-1, keepdims=True)
            v = jnp.mean((x - m) ** 2, axis=-1, keepdims=True)
            return (x - m) * jax.lax.rsqrt(v + eps) * g + b

        def _transformer_conv(h, src, dst, Wq, bq, Wk, bk, Wv, bv, Ws, bs, Wbeta):
            n, f = h.shape
            q = (h @ Wq.T + bq)[dst].reshape(-1, HEADS, D_HEAD)
            k = (h @ Wk.T + bk)[src].reshape(-1, HEADS, D_HEAD)
            v = (h @ Wv.T + bv)[src].reshape(-1, HEADS, D_HEAD)
            alpha = jnp.sum(q * k, axis=-1) / float(np.sqrt(D_HEAD))
            amax = jax.ops.segment_max(alpha, dst, num_segments=n)
            ex = jnp.exp(alpha - amax[dst])
            denom = jax.ops.segment_sum(ex, dst, num_segments=n)
            a = ex / (denom[dst] + 1e-16)
            out = jax.ops.segment_sum((a[:, :, None] * v).reshape(-1, f), dst, num_segments=n)
            x_r = h @ Ws.T + bs
            beta = jax.nn.sigmoid(jnp.concatenate([out, x_r, out - x_r], axis=-1) @ Wbeta.T)
            return beta * x_r + (1.0 - beta) * out

        def _forward(x, src, dst, Wi, bi, Wq, bq, Wk, bk, Wv, bv, Ws, bs, Wbeta, ln_g, ln_b, W1, b1, W2, b2, Wo, bo):
            h = jax.nn.gelu(x @ Wi.T + bi, approximate=False)
            for i in range(L):
                res = h
                h = _transformer_conv(h, src, dst, Wq[i], bq[i], Wk[i], bk[i], Wv[i], bv[i], Ws[i], bs[i], Wbeta[i])
                h = _layer_norm(h + res, ln_g[i], ln_b[i])
                res = h
                f = jax.nn.gelu(h @ W1[i].T + b1[i], approximate=False) @ W2[i].T + b2[i]
                h = f + res
            return h @ Wo.T + bo
        key = jax.random.key(seed)
        ks = jax.random.split(key, 24)
        rn = lambda k, shp, s=0.05: jax.random.normal(k, shp, jnp.float32) * s
        x = jax.random.normal(ks[0], (N, IN_C), jnp.float32)
        edge_index = jax.random.randint(ks[1], (2, E), 0, N, dtype=jnp.int64)
        return {'x': x, 'edge_index': edge_index, 'Wi': rn(ks[2], (HID, IN_C)), 'bi': jnp.zeros((HID,), jnp.float32), 'Wq': rn(ks[3], (L, HID, HID)), 'bq': jnp.zeros((L, HID), jnp.float32), 'Wk': rn(ks[4], (L, HID, HID)), 'bk': jnp.zeros((L, HID), jnp.float32), 'Wv': rn(ks[5], (L, HID, HID)), 'bv': jnp.zeros((L, HID), jnp.float32), 'Ws': rn(ks[6], (L, HID, HID)), 'bs': jnp.zeros((L, HID), jnp.float32), 'Wbeta': rn(ks[7], (L, 1, 3 * HID)), 'ln_g': jnp.ones((L, HID), jnp.float32), 'ln_b': jnp.zeros((L, HID), jnp.float32), 'W1': rn(ks[8], (L, 4 * HID, HID)), 'b1': jnp.zeros((L, 4 * HID), jnp.float32), 'W2': rn(ks[9], (L, HID, 4 * HID)), 'b2': jnp.zeros((L, HID), jnp.float32), 'Wo': rn(ks[10], (OUT_C, HID)), 'bo': jnp.zeros((OUT_C,), jnp.float32)}
    _L0_gnn_all = _L0_gnn_setup()
    _L0_gnn_in = {k: v for k, v in _L0_gnn_all.items() if k in ('Wi', 'bi', 'Wq', 'bq', 'Wk', 'bk', 'Wv', 'bv', 'Ws', 'bs', 'Wbeta', 'ln_g', 'ln_b', 'W1', 'b1', 'W2', 'b2', 'Wo', 'bo')}
    del _L0_gnn_all

    def _L1_gnn_setup():
        import jax, jax.numpy as jnp
        import numpy as np
        N, E, DIN, DOUT, NB = (50000, 25000, 64, 64, 16)
        MAX_RADIUS = 10.0
        key = jax.random.key(seed)
        ks = jax.random.split(key, 16)
        x = jax.random.normal(ks[0], (N, DIN), dtype=jnp.float32)
        edge_index = jax.random.randint(ks[1], (2, E), 0, N, dtype=jnp.int64)
        edge_vec = jax.random.normal(ks[2], (E, 3), dtype=jnp.float32)
        edge_len = jax.random.uniform(ks[3], (E, 1), dtype=jnp.float32) * MAX_RADIUS

        def lin(k, fan_in, fan_out):
            b = 1.0 / np.sqrt(fan_in)
            kw, kb = jax.random.split(k)
            W = jax.random.uniform(kw, (fan_in, fan_out), minval=-b, maxval=b, dtype=jnp.float32)
            bias = jax.random.uniform(kb, (fan_out,), minval=-b, maxval=b, dtype=jnp.float32)
            return (W, bias)
        mw1, mb1 = lin(ks[4], 2 * DIN + NB, 2 * DOUT)
        mw2, mb2 = lin(ks[5], 2 * DOUT, DOUT)
        uw1, ub1 = lin(ks[6], DIN + DOUT, DOUT)
        uw2, ub2 = lin(ks[7], DOUT, DOUT)
        ln_g = jnp.ones((DOUT,), dtype=jnp.float32)
        ln_b = jnp.zeros((DOUT,), dtype=jnp.float32)
        return {'x': x, 'edge_index': edge_index, 'edge_vec': edge_vec, 'edge_len': edge_len, 'mw1': mw1, 'mb1': mb1, 'mw2': mw2, 'mb2': mb2, 'uw1': uw1, 'ub1': ub1, 'uw2': uw2, 'ub2': ub2, 'ln_g': ln_g, 'ln_b': ln_b}
    _L1_gnn_all = _L1_gnn_setup()
    _L1_gnn_in = {k: v for k, v in _L1_gnn_all.items() if k in ('mw1', 'mb1', 'mw2', 'mb2', 'uw1', 'ub1', 'uw2', 'ub2', 'ln_g', 'ln_b')}
    del _L1_gnn_all
    return {'x': x, 'src': src, 'dst': dst, 'edge_attr_3': edge_attr_3, 'edge_weight1': edge_weight1, 'L0_gnn_Wi': _L0_gnn_in['Wi'], 'L0_gnn_bi': _L0_gnn_in['bi'], 'L0_gnn_Wq': _L0_gnn_in['Wq'], 'L0_gnn_bq': _L0_gnn_in['bq'], 'L0_gnn_Wk': _L0_gnn_in['Wk'], 'L0_gnn_bk': _L0_gnn_in['bk'], 'L0_gnn_Wv': _L0_gnn_in['Wv'], 'L0_gnn_bv': _L0_gnn_in['bv'], 'L0_gnn_Ws': _L0_gnn_in['Ws'], 'L0_gnn_bs': _L0_gnn_in['bs'], 'L0_gnn_Wbeta': _L0_gnn_in['Wbeta'], 'L0_gnn_ln_g': _L0_gnn_in['ln_g'], 'L0_gnn_ln_b': _L0_gnn_in['ln_b'], 'L0_gnn_W1': _L0_gnn_in['W1'], 'L0_gnn_b1': _L0_gnn_in['b1'], 'L0_gnn_W2': _L0_gnn_in['W2'], 'L0_gnn_b2': _L0_gnn_in['b2'], 'L0_gnn_Wo': _L0_gnn_in['Wo'], 'L0_gnn_bo': _L0_gnn_in['bo'], 'L1_gnn_mw1': _L1_gnn_in['mw1'], 'L1_gnn_mb1': _L1_gnn_in['mb1'], 'L1_gnn_mw2': _L1_gnn_in['mw2'], 'L1_gnn_mb2': _L1_gnn_in['mb2'], 'L1_gnn_uw1': _L1_gnn_in['uw1'], 'L1_gnn_ub1': _L1_gnn_in['ub1'], 'L1_gnn_uw2': _L1_gnn_in['uw2'], 'L1_gnn_ub2': _L1_gnn_in['ub2'], 'L1_gnn_ln_g': _L1_gnn_in['ln_g'], 'L1_gnn_ln_b': _L1_gnn_in['ln_b']}

def reference(x, src, dst, edge_attr_3, edge_weight1, L0_gnn_Wi, L0_gnn_bi, L0_gnn_Wq, L0_gnn_bq, L0_gnn_Wk, L0_gnn_bk, L0_gnn_Wv, L0_gnn_bv, L0_gnn_Ws, L0_gnn_bs, L0_gnn_Wbeta, L0_gnn_ln_g, L0_gnn_ln_b, L0_gnn_W1, L0_gnn_b1, L0_gnn_W2, L0_gnn_b2, L0_gnn_Wo, L0_gnn_bo, L1_gnn_mw1, L1_gnn_mb1, L1_gnn_mw2, L1_gnn_mb2, L1_gnn_uw1, L1_gnn_ub1, L1_gnn_uw2, L1_gnn_ub2, L1_gnn_ln_g, L1_gnn_ln_b):
    import jax
    import jax.numpy as jnp

    def _L0_gnn_ref(x, edge_index, Wi, bi, Wq, bq, Wk, bk, Wv, bv, Ws, bs, Wbeta, ln_g, ln_b, W1, b1, W2, b2, Wo, bo):
        import jax, jax.numpy as jnp
        import numpy as np
        N, E, L, HEADS, HID = (50000, 18750, 4, 8, 128)
        IN_C, OUT_C = (64, 64)
        D_HEAD = HID // HEADS

        def _layer_norm(x, g, b, eps=1e-05):
            m = jnp.mean(x, axis=-1, keepdims=True)
            v = jnp.mean((x - m) ** 2, axis=-1, keepdims=True)
            return (x - m) * jax.lax.rsqrt(v + eps) * g + b

        def _transformer_conv(h, src, dst, Wq, bq, Wk, bk, Wv, bv, Ws, bs, Wbeta):
            n, f = h.shape
            q = (h @ Wq.T + bq)[dst].reshape(-1, HEADS, D_HEAD)
            k = (h @ Wk.T + bk)[src].reshape(-1, HEADS, D_HEAD)
            v = (h @ Wv.T + bv)[src].reshape(-1, HEADS, D_HEAD)
            alpha = jnp.sum(q * k, axis=-1) / float(np.sqrt(D_HEAD))
            amax = jax.ops.segment_max(alpha, dst, num_segments=n)
            ex = jnp.exp(alpha - amax[dst])
            denom = jax.ops.segment_sum(ex, dst, num_segments=n)
            a = ex / (denom[dst] + 1e-16)
            out = jax.ops.segment_sum((a[:, :, None] * v).reshape(-1, f), dst, num_segments=n)
            x_r = h @ Ws.T + bs
            beta = jax.nn.sigmoid(jnp.concatenate([out, x_r, out - x_r], axis=-1) @ Wbeta.T)
            return beta * x_r + (1.0 - beta) * out

        def _forward(x, src, dst, Wi, bi, Wq, bq, Wk, bk, Wv, bv, Ws, bs, Wbeta, ln_g, ln_b, W1, b1, W2, b2, Wo, bo):
            h = jax.nn.gelu(x @ Wi.T + bi, approximate=False)
            for i in range(L):
                res = h
                h = _transformer_conv(h, src, dst, Wq[i], bq[i], Wk[i], bk[i], Wv[i], bv[i], Ws[i], bs[i], Wbeta[i])
                h = _layer_norm(h + res, ln_g[i], ln_b[i])
                res = h
                f = jax.nn.gelu(h @ W1[i].T + b1[i], approximate=False) @ W2[i].T + b2[i]
                h = f + res
            return h @ Wo.T + bo
        src, dst = (edge_index[0], edge_index[1])
        return _forward(x, src, dst, Wi, bi, Wq, bq, Wk, bk, Wv, bv, Ws, bs, Wbeta, ln_g, ln_b, W1, b1, W2, b2, Wo, bo)

    def _L1_gnn_ref(x, edge_index, edge_vec, edge_len, mw1, mb1, mw2, mb2, uw1, ub1, uw2, ub2, ln_g, ln_b):
        import jax, jax.numpy as jnp
        import numpy as np
        N, E, DIN, DOUT, NB = (50000, 25000, 64, 64, 16)
        MAX_RADIUS = 10.0
        src, dst = (edge_index[0], edge_index[1])
        dist = edge_len[:, 0]
        centers = jnp.linspace(0.0, MAX_RADIUS, NB)
        width = (centers[1] - centers[0]) * 0.5
        rbf = jnp.exp(-(dist[:, None] - centers) ** 2 / (2.0 * width ** 2))
        msg_in = jnp.concatenate([x[src], x[dst], rbf], axis=-1)
        msg = jax.nn.silu(msg_in @ mw1 + mb1) @ mw2 + mb2
        agg = jax.ops.segment_sum(msg, dst, num_segments=x.shape[0])
        cnt = jax.ops.segment_sum(jnp.ones((dst.shape[0],), dtype=x.dtype), dst, num_segments=x.shape[0])
        agg = agg / jnp.maximum(cnt, 1.0)[:, None]
        upd_in = jnp.concatenate([x, agg], axis=-1)
        out = jax.nn.silu(upd_in @ uw1 + ub1) @ uw2 + ub2
        mu = out.mean(-1, keepdims=True)
        var = ((out - mu) ** 2).mean(-1, keepdims=True)
        out = (out - mu) * jax.lax.rsqrt(var + 1e-05) * ln_g + ln_b
        return out
    edge_index = jnp.stack([src, dst])
    x = _layernorm(x + _L0_gnn_ref(x, edge_index, L0_gnn_Wi, L0_gnn_bi, L0_gnn_Wq, L0_gnn_bq, L0_gnn_Wk, L0_gnn_bk, L0_gnn_Wv, L0_gnn_bv, L0_gnn_Ws, L0_gnn_bs, L0_gnn_Wbeta, L0_gnn_ln_g, L0_gnn_ln_b, L0_gnn_W1, L0_gnn_b1, L0_gnn_W2, L0_gnn_b2, L0_gnn_Wo, L0_gnn_bo), axis=-1)
    x = _layernorm(x + _L1_gnn_ref(x, edge_index, edge_attr_3, edge_weight1, L1_gnn_mw1, L1_gnn_mb1, L1_gnn_mw2, L1_gnn_mb2, L1_gnn_uw1, L1_gnn_ub1, L1_gnn_uw2, L1_gnn_ub2, L1_gnn_ln_g, L1_gnn_ln_b), axis=-1)
    return x

_drawn_inputs = setup_inputs


def setup_inputs(seed=0):
    import zlib

    import numpy as np

    out = dict(_drawn_inputs(seed))
    spreads = {'L0_gnn_bi': (0.0, 0.1),
     'L0_gnn_bq': (0.0, 0.8),
     'L0_gnn_bk': (0.0, 0.8),
     'L0_gnn_bv': (0.0, 0.1),
     'L0_gnn_bs': (0.0, 0.1),
     'L0_gnn_ln_g': (1.0, 0.2),
     'L0_gnn_ln_b': (0.0, 0.1),
     'L0_gnn_b1': (0.0, 0.1),
     'L0_gnn_b2': (0.0, 0.1),
     'L0_gnn_bo': (0.0, 0.1),
     'L1_gnn_ln_g': (1.0, 0.2),
     'L1_gnn_ln_b': (0.0, 0.1)}
    factors = {'edge_weight1': 8.0, 'L0_gnn_Wq': 2.845, 'L0_gnn_Wk': 2.912, 'L1_gnn_mb1': 5.833}
    for name, (base, spread) in spreads.items():
        noise = np.random.default_rng([zlib.crc32(name.encode()), seed]).standard_normal(out[name].shape)
        drawn = base * np.exp(spread * noise) if base else spread * noise
        out[name] = jnp.asarray(drawn.astype(out[name].dtype))
    for name, factor in factors.items():
        out[name] = (out[name] * factor).astype(out[name].dtype)
    return out
```

```python
from contextlib import ExitStack

import numpy as np

import concourse.bass as bass
from concourse import mybir

F32 = mybir.dt.float32
BF16 = mybir.dt.bfloat16
I32 = mybir.dt.int32
ALU = mybir.AluOpType
ACT = mybir.ActivationFunctionType
X = mybir.AxisListType.X

P = 128
N = 3125
E = 100000
L = 4
HEADS, DH = 8, 16
HID = HEADS * DH
NB = -(-N // P)
NPAD = NB * P
TILES = -(-E // P) + 2
SUPERS = (-(-E // P) + NB - 1 + NB) // 2 + 1
CH = 16
CHUNKS = 2 * (-(-2 * SUPERS // (2 * CH)))
V = CHUNKS * CH
VC = -(-V // P)
PAIRS = CHUNKS // 2
G = 4
NG = CH // G
VW = DH + 1
KVW = HID + HEADS * VW
BW = 5
NI = NB // BW
BIG = 1.0e30
START = NG + 1
NBASIS = 16
QS, BAND = 2 * HID, KVW
VEC0 = {"w0": 0, "w1": 128, "w2": 256, "g": 384, "b": 512, "b2": 640, "qs": 768, "kv": 1024}
VEC0_W = 1024 + KVW
VEC1 = {"bi": 0, "bo": 128, "mb1": 192, "mb2": 320, "ub1": 384, "ub2": 448, "g": 512, "b": 576}
VEC1_W = 640
assert NB % BW == 0 and V >= 2 * SUPERS


def build_program(nc, a, out):
    with ExitStack() as ctx:
        def sb(name, shape, dt=F32):
            return ctx.enter_context(nc.sbuf_tensor(name, shape, dt))

        def sem(name):
            return ctx.enter_context(nc.semaphore(name))

        def sems(name, n):
            return [sem(f"{name}{k}") for k in range(n)]

        bank = [ctx.enter_context(nc.psum_tensor(f"bank{k}", [P, 512], F32)) for k in range(8)]

        kv_table = nc.dram_tensor("kv_table", [NPAD, KVW], F32, kind="Internal").ap()
        src_table = nc.dram_tensor("src_table", [NPAD, HID], F32, kind="Internal").ap()
        flat_dst = nc.dram_tensor("flat_dst", [VC * P * P + P], F32, kind="Internal").ap()
        flat_rst = nc.dram_tensor("flat_rst", [VC * P * P + P], BF16, kind="Internal").ap()
        flat_len = nc.dram_tensor("flat_len", [VC * P * P], F32, kind="Internal").ap()
        flat_blk = nc.dram_tensor("flat_blk", [VC * P], I32, kind="Internal").ap()

        ident = sb("ident", [P, P])
        iota = sb("iota", [P, P])
        place = sb("place", [P, 2, VC])
        centers = sb("centers", [NBASIS, 1])
        ones = sb("ones", [P, P])
        h = sb("h", [P, NB, HID])
        xn = sb("xn", [P, NB, 64])
        qs = sb("qs", [P, NB, QS])
        acc = sb("acc", [P, NB, HEADS * VW])
        src_e = sb("src_e", [P, VC * P], I32)
        rel_e = sb("rel_e", [P, VC * P])
        blk = sb("blk", [1, VC * P], I32)
        rst = sb("rst", [P, CHUNKS, P], BF16)
        rst_b = sb("rst_b", [P, CHUNKS, P], BF16)
        rst_sum = sb("rst_sum", [P, CHUNKS, 2])
        cont = sb("cont", [1, CHUNKS])
        w_qs = sb("w_qs", [P, QS])
        w_kv = sb("w_kv", [P, BAND])
        w_1 = sb("w_1", [P, 4 * HID])
        b_1 = sb("b_1", [P, 4])
        w_2 = sb("w_2", [P, 4, HID])
        vec0 = sb("vec0", [P, VEC0_W])
        vec1 = sb("vec1", [P, VEC1_W])
        w_i = sb("w_i", [64, HID])
        w_o = sb("w_o", [P, 64])
        m_1 = sb("m_1", [64, 2 * HID])
        m_1c = sb("m_1c", [NBASIS, HID])
        m_2 = sb("m_2", [P, 64])
        u_1 = sb("u_1", [P, 64])
        u_2 = sb("u_2", [64, 64])
        slots = sb("slots", [P, 2, CH, KVW])
        flat_slots = slots[:, :, :, :].rearrange("p a c k -> p (a c k)")
        idx = sb("idx", [P, 2, CH], I32)
        oh = sb("oh", [P, 2, CH, P])
        ohT = sb("ohT", [P, 2, G, P])
        alpha = sb("alpha", [P, HEADS, CH])
        rcol = sb("rcol", [P, 2])
        fwd = sb("fwd", [P, P])
        bwd = sb("bwd", [P, P])
        ex = sb("ex", [P, P])
        f_in = sb("f_in", [1, 2, HEADS, CH + 1])
        b_in = sb("b_in", [1, 2, HEADS, CH + 1])
        f_out = sb("f_out", [1, HEADS, CH + 1])
        b_out = sb("b_out", [1, HEADS, CH + 1])
        c_row = sb("c_row", [1, 2, P])
        icol = sb("icol", [P, 2])
        gap = sb("gap", [1, HEADS])
        shift = sb("shift", [P, HEADS])
        scale = sb("scale", [P, HEADS])
        rbf = sb("rbf", [NBASIS, 2, CH * P])
        at = [0]

        def node_tile(width):
            s = at[0]
            at[0] += width
            assert at[0] <= 2 * CH * KVW
            return flat_slots[:, s:s + width]

        tsrc = node_tile(BW * P).rearrange("p (b k) -> p b k", b=BW)
        hT = node_tile(BW * P)
        kvst = node_tile(BW * KVW).rearrange("p (b k) -> p b k", b=BW)
        g1 = node_tile(4 * BW * P).rearrange("p (f k) -> p f k", f=4)
        at[0] = BW * P * 2
        o_t = node_tile(BW * P).rearrange("p (b k) -> p b k", b=BW)
        at[0] = BW * P * 2 + BW * KVW + 4 * BW * P
        t1 = node_tile(BW * P).rearrange("p (b k) -> p b k", b=BW)
        t2 = sb("t2", [P, BW, P])
        dx = sb("dx", [P, BW, P])
        den = sb("den", [P, BW, HEADS])
        rden = sb("rden", [P, BW, HEADS])
        st = [sb(f"st{k}", [P, BW]) for k in range(7)]
        su_f = flat_slots[:, 0:TILES]
        su_i = flat_slots[:, TILES:2 * TILES].bitcast(I32)
        su_o = flat_slots[:, 2 * TILES:3 * TILES]
        row = sb("row", [P, 12, NB + 1])
        rowi = sb("rowi", [P, 4, NB + 1], I32)
        vt = sb("vt", [P, 4, VC])
        vti = sb("vti", [P, 2, VC], I32)
        rows_i = flat_slots[:, 3000:3000 + VC * P].rearrange("p (c e) -> p c e", c=VC).bitcast(I32)
        rows_d = flat_slots[:, 4000:4000 + VC * P].rearrange("p (c e) -> p c e", c=VC).bitcast(I32)
        rows_l = flat_slots[:, 5000:5000 + VC * P].rearrange("p (c e) -> p c e", c=VC)
        rows_f = flat_slots[:, 6000:6000 + VC * P].rearrange("p (c e) -> p c e", c=VC)
        rst_r = flat_slots[:, 0:CHUNKS * P // 2].bitcast(BF16).rearrange("p (c e) -> p c e", c=CHUNKS)
        oh_f = oh[:, :, :, :].rearrange("p a c k -> p (a c k)")
        r_dst = oh_f[:, 0:VC * P].rearrange("p (c e) -> p c e", c=VC)
        r_rel = oh_f[:, 900:900 + VC * P].rearrange("p (c e) -> p c e", c=VC)
        r_ok = oh_f[:, 1800:1800 + VC * P].rearrange("p (c e) -> p c e", c=VC)
        r_prev = oh_f[:, 2700:2700 + VC * P].rearrange("p (c e) -> p c e", c=VC)
        r_bf = sb("r_bf", [P, VC, P], BF16)
        r_src = flat_slots[:, 7000:7000 + VC * P].rearrange("p (c e) -> p c e", c=VC)
        edge_word = sb("edge_word", [1, 2])
        edge_bf = sb("edge_bf", [1, 2], BF16)

        ld_const, ld_w1, ld_layer, ld_dst = sem("ld_const"), sem("ld_w1"), sem("ld_layer"), sem("ld_dst")
        su_step, su_count, su_idx, su_rows = sem("su_step"), sem("su_count"), sem("su_idx"), sem("su_rows")
        su_flat, su_prev, su_rst, su_tabs = sem("su_flat"), sem("su_prev"), sem("su_rst"), sem("su_tabs")
        su_turn, su_turned, su_taken, su_done = sem("su_turn"), sem("su_turned"), sem("su_taken"), sem("su_done")
        su_pool, su_len, su_rstd, su_dstd = sem("su_pool"), sem("su_len"), sem("su_rstd"), sem("su_dstd")
        t_in, t_ps, t_out = sem("t_in"), sem("t_ps"), sem("t_out")
        m_ps, m_ev, ffn_ps, ffn_act = sem("m_ps"), sem("m_ev"), sem("ffn_ps"), sem("ffn_act")
        h_new, a_ps, a_ev, tab_out, post = sem("h_new"), sem("a_ps"), sem("a_ev"), sem("tab_out"), sem("post")
        act_req, act_ans = sem("act_req"), sem("act_ans")
        node_done, acc_zero = sem("node_done"), sem("acc_zero")
        idx_in = sems("idx_in", 2)
        kv_in = [sems(f"kv_in{k}_", NG) for k in range(2)]
        slot_free = [sems(f"slot_free{k}_", NG) for k in range(2)]
        oh_made, oh_turned, oh_copied, q_spread = sem("oh_made"), sem("oh_turned"), sem("oh_copied"), sem("q_spread")
        spread_used, alpha_done, alpha_turned = sem("spread_used"), sem("alpha_done"), sem("alpha_turned")
        rcol_done, fwd_one, bwd_one = sem("rcol_done"), sem("fwd_one"), sem("bwd_one")
        rows_turned, rows_copied, carry_set = sem("rows_turned"), sem("rows_copied"), sem("carry_set")
        carries_packed = sem("carries_packed")
        f_done, b_done, cols_turned, cols_copied = sem("f_done"), sem("b_done"), sem("cols_turned"), sem("cols_copied")
        gap_done, shift_done, shift_spread, scale_done = sem("gap_done"), sem("shift_done"), sem("shift_spread"), sem("scale_done")
        fwd_two, bwd_two, max_done, arg_done = sem("fwd_two"), sem("bwd_two"), sem("max_done"), sem("arg_done")
        ex_done, ex_turned, w_done, part_even = sem("ex_done"), sem("ex_turned"), sem("w_done"), sem("part_even")
        acc_scaled, acc_done = sem("acc_scaled"), sem("acc_done")
        len_in, sq_done, rbf_done = sems("len_in", 2), sem("sq_done"), sem("rbf_done")
        silu_done, one_set = sem("silu_done"), sem("one_set")
        tab_free, out_free = sem("tab_free"), sem("out_free")
        out_ready, out_sent = sem("out_ready"), sem("out_sent")

        counted = [a_ev, a_ps, acc_done, acc_scaled, acc_zero, act_ans, act_req,
                   alpha_done, alpha_turned, arg_done, b_done, bwd_one, bwd_two, carries_packed,
                   carry_set, cols_copied, cols_turned, ex_done, ex_turned, f_done, ffn_act,
                   ffn_ps, fwd_one, fwd_two, gap_done, h_new, m_ev, m_ps,
                   max_done, node_done, oh_copied, oh_made, oh_turned, one_set, out_free,
                   out_ready, post, q_spread, rbf_done, rcol_done, rows_copied, rows_turned,
                   scale_done, shift_done, shift_spread, silu_done, spread_used, sq_done, t_in,
                   t_out, t_ps, tab_free, w_done,
                   part_even, *slot_free[0], *slot_free[1]]
        LN_A, LN_B = NI + 2 * NI * L, NI + 2 * NI * L + 2 * NI
        N_CONST = 14

        def bc(ap, n):
            return ap.unsqueeze(1).to_broadcast([ap.shape[0], n, ap.shape[1]])

        def bcl(ap, n):
            return ap.unsqueeze(len(ap.shape)).to_broadcast([*ap.shape, n])

        block = ctx.enter_context(nc.Block())

        @block.sync
        def _(sp):
            sp.dma_start(su_i, a["dst_t"].rearrange("t e -> (t e)").rearrange("(p t) -> p t", p=P)).then_inc(ld_dst, 16)
            for dst, name in ((ident[:, :], "ident"), (iota[:, :], "iota"), (place[:, :, :], "place"),
                              (centers[:, :], "centers"), (w_i[:, :], "w_i"), (w_o[:, :], "w_o"),
                              (m_1[:, :], "m_1"), (m_1c[:, :], "m_1c"), (m_2[:, :], "m_2"),
                              (u_1[:, :], "u_1"), (u_2[:, :], "u_2")):
                sp.dma_start(dst, a[name]).then_inc(ld_const, 16)
            sp.dma_start(vec1[:, :], a["vec1"].to_broadcast([P, VEC1_W])).then_inc(ld_const, 16)
            sp.dma_start(xn[:, :, :], a["x"].rearrange("(b p) k -> p b k", p=P)).then_inc(ld_const, 16)
            sp.wait_ge(su_rows, 16 * 3 * VC)
            sp.dma_start(flat_len.rearrange("(c p e) -> p c e", p=P, e=P), rows_l).then_inc(su_len, 16)
            sp.wait_ge(su_flat, 1)
            sp.dma_start(flat_dst[1:1 + VC * P * P].rearrange("(c p e) -> p c e", p=P, e=P), r_dst).then_inc(su_dstd, 16)
            sp.dma_start(flat_dst[0:1].rearrange("(a b) -> a b", a=1), edge_word[:, 0:1]).then_inc(su_dstd, 16)
            sp.dma_start(flat_blk.rearrange("(c p) -> p c", p=P), vti[:, 1, :], allow_slow_non_contiguous=True).then_inc(su_dstd, 16)
            sp.wait_ge(su_dstd, 48)
            sp.dma_start(r_prev, flat_dst[0:VC * P * P].rearrange("(c p e) -> p c e", p=P, e=P)).then_inc(su_prev, 16)
            sp.dma_start(blk[:, :], flat_blk.rearrange("(a b) -> a b", a=1)).then_inc(su_prev, 16)
            sp.wait_ge(su_rst, 1)
            sp.dma_start(flat_rst[0:VC * P * P].rearrange("(c p e) -> p c e", p=P, e=P), r_bf[:, :, :]).then_inc(su_rstd, 16)
            sp.dma_start(flat_rst[VC * P * P:VC * P * P + 1].rearrange("(a b) -> a b", a=1), edge_bf[:, 0:1]).then_inc(su_rstd, 16)
            sp.wait_ge(su_rstd, 32)
            for k in range(HEADS):
                for dst, off in ((rst, 0), (rst_r, 1)):
                    sp.dma_start(dst[k * CH:(k + 1) * CH, :, :],
                                 flat_rst[off:off + V * P].rearrange("(c t e) -> t c e", t=CH, e=P)).then_inc(su_tabs, 16)

            def stage_indices(par, gi, i):
                sp.wait_ge(spread_used, START + NG * (2 * gi + par - 1))
                sp.dma_start(idx[:, par, :], src_e[:, bass.ds((2 * i + par) * CH, CH)]).then_inc(idx_in[par], 16)

            sp.wait_ge(su_done, VC * 2)
            with sp.Fori(0, L) as l:
                sp.wait_ge(h_new, START + NI * (l + 1))
                for dst, name in ((w_qs, "w_qs"), (w_kv, "w_kv"), (w_1, "w_1"), (b_1, "b_1")):
                    sp.dma_start(dst[:, :], a[name][bass.ds(l * P, P), :]).then_inc(ld_layer, 16)
                sp.dma_start(w_2[:, :, :].rearrange("p a b -> p (a b)"), a["w_2"][bass.ds(l * P, P), :]).then_inc(ld_layer, 16)
                sp.dma_start(vec0[:, :], a["vec0"][bass.ds(l, 1), :].to_broadcast([P, VEC0_W])).then_inc(ld_layer, 16)
                with sp.Fori(0, NI) as i:
                    sp.wait_ge(a_ev, START + 2 * BW * (l * NI + i + 1))
                    sp.dma_start(kv_table[bass.ds(i * BW * P, BW * P), :].rearrange("(b p) k -> p b k", p=P),
                                 kvst).then_inc(tab_out, 16)
                    sp.wait_ge(tab_out, 16 * (l * NI + i + 1))
                    sp.sem_inc(tab_free, 1)
                with sp.Fori(0, PAIRS) as i:
                    for par in range(2):
                        stage_indices(par, l * PAIRS + i, i)
            with sp.Fori(0, NI) as i:
                sp.wait_ge(a_ev, START + 2 * BW * (L * NI + i + 1))
                sp.dma_start(src_table[bass.ds(i * BW * P, BW * P), :].rearrange("(b p) k -> p b k", p=P),
                             kvst[:, :, 0:HID]).then_inc(tab_out, 16)
                sp.wait_ge(tab_out, 16 * (L * NI + i + 1))
                sp.sem_inc(tab_free, 1)
            with sp.Fori(0, PAIRS) as i:
                for par in range(2):
                    stage_indices(par, L * PAIRS + i, i)
                    sp.wait_ge(sq_done, START + 2 * i + par)
                    sp.dma_start(rbf[:, par, :],
                                 flat_len[bass.ds((2 * i + par) * CH * P, CH * P)].rearrange("(a b) -> a b", a=1)
                                 .to_broadcast([NBASIS, CH * P])).then_inc(len_in[par], 16)
            with sp.Fori(0, NI - 1) as i:
                sp.wait_ge(out_ready, START + i + 1)
                sp.dma_start(out[bass.ds(i * BW * P, BW * P), :].rearrange("(b p) k -> p b k", p=P),
                             dx[:, :, 0:64]).then_inc(out_sent, 16)
                sp.wait_ge(out_sent, 16 * (i + 1))
                sp.sem_inc(out_free, 1)
            sp.wait_ge(out_ready, START + NI)
            full = (N // P) % BW
            lo = (NI - 1) * BW * P
            sp.dma_start(out[lo:lo + full * P, :].rearrange("(b p) k -> p b k", p=P), dx[:, 0:full, 0:64]).then_inc(out_sent, 16)
            sp.dma_start(out[lo + full * P:N, :], dx[0:N - lo - full * P, full, 0:64]).then_inc(out_sent, 16)
            sp.wait_ge(out_sent, 16 * (NI + 1))

        @block.gpsimd
        def _(pool):
            for s in counted:
                pool.sem_inc(s, START)
            pool.wait_ge(su_idx, 1)
            for c in range(VC):
                for dst, name in ((rows_i, "src_t"), (rows_d, "dst_t"), (rows_l, "len_t")):
                    pool.indirect_dma_start(dst[:, c, :], None, a[name],
                                            bass.IndirectOffsetOnAxis(ap=vti[:, 0, c:c + 1], axis=0)).then_inc(su_rows, 16)
            uses = [[pool.alloc_register(f"uses{par}_{j}") for j in range(NG)] for par in range(2)]
            for par in range(2):
                for j in range(NG):
                    pool.reg_mov(uses[par][j], 0)

            def gather_chunk(par, gi, l, table, width):
                used = [pool.snap(uses[par][j]) for j in range(NG)]
                pool.wait_ge(tab_out, 16 * NI * (l + 1))
                pool.wait_ge(acc_zero, START + l + 1)
                pool.wait_ge(idx_in[par], 16 * (gi + 1))
                for j in range(NG):
                    pool.wait_ge(slot_free[par][j], START + used[j])
                    pool.reg_add(uses[par][j], uses[par][j], 1)
                    for t in range(j * G, (j + 1) * G):
                        pool.indirect_dma_start(slots[:, par, t, 0:width], None, table,
                                                bass.IndirectOffsetOnAxis(ap=idx[:, par, t:t + 1], axis=0))\
                            .then_inc(kv_in[par][j], 16)

            with pool.Fori(0, L) as l:
                with pool.Fori(0, PAIRS) as i:
                    for par in range(2):
                        gather_chunk(par, l * PAIRS + i, l, kv_table, KVW)
            with pool.Fori(0, PAIRS) as i:
                for par in range(2):
                    gather_chunk(par, L * PAIRS + i, L, src_table, HID)

        @block.scalar
        def _(act):
            def turned(n):
                act.wait_ge(t_ps, START + n + 1)
                act.copy(hT[:, 0:4 * P], bank[0][:, :]).then_inc(t_out, 1)
                act.copy(hT[:, 4 * P:BW * P], bank[1][:, 0:P]).then_inc(t_out, 1)

            def copy_onehots(g):
                for j in range(NG):
                    act.wait_ge(oh_turned, START + NG * g + j + 1)
                    act.wait_ge(q_spread, START + NG * g + max(j - 1, 0))
                    act.copy(ohT[:, j % 2, :, :].rearrange("p a b -> p (a b)"), bank[j % 2][:, :]).then_inc(oh_copied, 1)

            act.wait_ge(ld_const, 16 * 13)
            with act.Fori(0, NI) as i:
                turned(i)
                act.wait_ge(post, START + i + 1)
                act.activation(h[:, bass.ds(i * BW, BW), :], t1, ACT.Gelu).then_inc(h_new, 1)
            with act.Fori(0, L) as l:
                act.wait_ge(h_new, START + NI * (l + 1))
                with act.Fori(0, NI) as i:
                    n = NI + 2 * NI * l + i
                    act.wait_ge(t_ps, START + n)
                    act.copy(tsrc, h[:, bass.ds(i * BW, BW), :]).then_inc(t_in, 1)
                    turned(n)
                with act.Fori(0, PAIRS) as i:
                    for par in range(2):
                        g = 2 * (l * PAIRS + i) + par
                        copy_onehots(g)
                        act.wait_ge(rows_turned, START + g + 1)
                        act.wait_ge(f_done, START + g)
                        act.wait_ge(gap_done, START + g)
                        act.copy(f_in[:, :, :, 1:CH + 1], bank[5][0:1, 0:2 * P].rearrange("p (a h t) -> p a h t", a=2, t=CH))\
                            .then_inc(rows_copied, 1)
                        act.wait_ge(b_done, START + g)
                        act.copy(b_in[:, :, :, 0:CH], bank[5][0:1, 2 * P:4 * P].rearrange("p (a h t) -> p a h t", a=2, t=CH))\
                            .then_inc(rows_copied, 1)
                        act.wait_ge(cols_turned, START + g + 1)
                        act.wait_ge(bwd_two, START + g)
                        act.copy(icol[:, :], bank[5][:, 0:2]).then_inc(cols_copied, 1)
                        act.wait_ge(shift_spread, START + g + 1)
                        act.wait_ge(acc_scaled, START + g)
                        act.activation(scale[:, :], bank[5][:, 8:16], ACT.Exp, scale=0.25).then_inc(scale_done, 1)
                        act.wait_ge(arg_done, START + g + 1)
                        act.wait_ge(ex_turned, START + g)
                        act.activation(ex[:, :], bwd[:, :], ACT.Exp, scale=0.25).then_inc(ex_done, 1)
                with act.Fori(0, NI) as i:
                    act.wait_ge(act_req, START + 2 * (l * NI + i) + 1)
                    act.activation(st[1][:, :], st[0][:, :], ACT.Sigmoid).then_inc(act_ans, 1)
                    act.wait_ge(act_req, START + 2 * (l * NI + i) + 2)
                    act.activation(st[4][:, :], st[3][:, :], ACT.Sqrt).then_inc(act_ans, 1)
                    turned(NI + 2 * NI * l + NI + i)
                    for f in range(4):
                        for s in range(2):
                            act.wait_ge(ffn_ps, START + 8 * (l * NI + i) + 2 * f + s + 1)
                            act.activation(g1[:, f, s * 320:(s + 1) * 320], bank[2 + (2 * f + s) % 4][:, 0:320], ACT.Gelu,
                                           bias=b_1[:, f:f + 1]).then_inc(ffn_act, 1)
            act.wait_ge(h_new, START + NI * (L + 1))
            with act.Fori(0, NI) as i:
                act.wait_ge(t_ps, START + LN_A + 2 * i)
                act.copy(tsrc, h[:, bass.ds(i * BW, BW), :]).then_inc(t_in, 1)
                turned(LN_A + 2 * i)
                act.wait_ge(act_req, START + 2 * L * NI + i + 1)
                act.activation(st[4][:, :], st[3][:, :], ACT.Sqrt).then_inc(act_ans, 1)
                turned(LN_A + 2 * i + 1)
            with act.Fori(0, PAIRS) as i:
                for par in range(2):
                    c = 2 * i + par
                    g = 2 * (L * PAIRS + i) + par
                    act.wait_ge(len_in[par], 16 * (i + 1))
                    act.wait_ge(q_spread, START + NG * g)
                    act.activation(rbf[:, par, :], rbf[:, par, :], ACT.Square, bias=centers[:, 0:1]).then_inc(sq_done, 1)
                    act.wait_ge(sq_done, START + c + 1)
                    act.activation(rbf[:, par, :], rbf[:, par, :], ACT.Exp, scale=RBF_SCALE).then_inc(rbf_done, 1)
                    copy_onehots(g)
                    for j in range(NG):
                        act.wait_ge(spread_used, START + NG * g + j + 1)
                        s = slots[:, par, j * G:(j + 1) * G, HID:2 * HID]
                        act.activation(s, s, ACT.Silu).then_inc(silu_done, 1)
            with act.Fori(0, NI) as i:
                turned(LN_B + 3 * i)
                turned(LN_B + 3 * i + 1)
                act.wait_ge(act_req, START + 2 * L * NI + NI + 3 * i + 1)
                act.wait_ge(t_ps, START + LN_B + 3 * i + 2)
                act.activation(tsrc[:, :, 0:64], t1[:, :, 0:64], ACT.Silu).then_inc(t_in, 1)
                turned(LN_B + 3 * i + 2)
                for k in range(2):
                    act.wait_ge(act_req, START + 2 * L * NI + NI + 3 * i + 2 + k)
                    act.activation(st[4][:, :], st[3][:, :], ACT.Sqrt).then_inc(act_ans, 1)

        @block.tensor
        def _(pe):
            def turn_blocks(n):
                pe.wait_ge(t_in, START + n + 1)
                pe.wait_ge(t_out, START + 2 * n)
                for b in range(BW):
                    mm = pe.transpose(bank[b // 4][:, (b % 4) * P:(b % 4 + 1) * P], tsrc[:, b, :], ident[:, :])
                mm.then_inc(t_ps, 1)

            def times(n, m, weights, width, K=P):
                pe.wait_ge(t_out, START + 2 * n + 2)
                pe.wait_ge(m_ev, START + m)
                for b in range(BW):
                    mm = pe.matmul(bank[2 + b // 4][:, (b % 4) * P:(b % 4) * P + width], hT[0:K, b * P:(b + 1) * P], weights,
                                   start=True, stop=True)
                mm.then_inc(m_ps, 1)

            def spread(g, blocks, par, basis=None):
                def turn(j):
                    pe.wait_ge(oh_copied, START + NG * g + max(j - 1, 0))
                    for t in range(G):
                        mm = pe.transpose(bank[j % 2][:, t * P:(t + 1) * P], oh[:, par, j * G + t, :], ident[:, :])
                    mm.then_inc(oh_turned, 1)

                def rows(j):
                    pe.wait_ge(oh_copied, START + NG * g + j + 1)
                    pe.wait_ge(spread_used, START + NG * g + max(j - 1, 0))
                    for t in range(G):
                        o = bank[2 + j % 2][:, t * P:(t + 1) * P]
                        mm = pe.matmul(o, ohT[:, j % 2, t, :], qs[:, blocks[(j * G + t) // 2], 0:HID],
                                       start=True, stop=basis is None)
                        if basis is not None:
                            mm = pe.matmul(o, rbf[:, par, (j * G + t) * P:(j * G + t + 1) * P], m_1c[:, :],
                                           start=False, stop=True)
                    mm.then_inc(q_spread, 1)

                pe.wait_ge(oh_made, START + g + 1)
                turn(0)
                turn(1)
                for j in range(NG):
                    rows(j)
                    if j + 2 < NG:
                        turn(j + 2)

            def add_up(g, gi, par, width, done, base):
                for s in range(CH // 2):
                    pe.wait_ge(done, START + NG * base + s // 2 + 1)
                    pe.wait_ge(acc_done, START + (CH // 2) * g + max(s - 1, 0))
                    for t in (2 * s, 2 * s + 1):
                        mm = pe.matmul(bank[6 + s % 2][:, 0:width], oh[:, par, t, :], slots[:, par, t, HID:HID + width],
                                       start=(t % 2 == 0), stop=(t % 2 == 1))
                    mm.then_inc(part_even if s % 2 == 0 else slot_free[par][s // 2], 1)

            def block_numbers(c):
                return [pe.value_load(blk[0:1, bass.ds(c * CH + 2 * s, 1)], min_val=0, max_val=NB - 1) for s in range(CH // 2)]

            pe.wait_ge(su_count, 1)
            pe.matmul(bank[7][:, 0:NB + 1], ones[:, :], row[:, 0, :], start=True, stop=True).then_inc(su_count, 1)
            pe.wait_ge(ld_const, 16 * 13)
            pe.wait_ge(su_turn, 1)
            for n, rows_x in enumerate([r_src, r_rel]):
                for c in range(VC):
                    k = n * VC + c
                    if k >= 2:
                        pe.wait_ge(su_taken, k - 1)
                    pe.transpose(bank[4 + k % 2][:, 0:P], rows_x[:, c, :], ident[:, :]).then_inc(su_turned, 1)
            with pe.Fori(0, NI) as i:
                turn_blocks(i)
                times(i, i, w_i[:, :], HID, 64)
            pe.wait_ge(su_prev, 32)
            with pe.Fori(0, L) as l:
                with pe.Fori(0, NI) as i:
                    n = NI + 2 * NI * l + i
                    turn_blocks(n)
                    pe.wait_ge(ld_layer, 96 * (l + 1))
                    pe.wait_ge(t_out, START + 2 * n + 2)
                    for b in range(BW):
                        pe.wait_ge(a_ev, START + 2 * BW * (l * NI + i) + max(2 * b - 2, 0))
                        pe.matmul(bank[2 + b % 2][:, 0:QS], hT[:, b * P:(b + 1) * P], w_qs[:, :], start=True, stop=True)\
                            .then_inc(a_ps, 1)
                        pe.matmul(bank[4 + b % 2][:, 0:BAND], hT[:, b * P:(b + 1) * P], w_kv[:, :], start=True, stop=True)\
                            .then_inc(a_ps, 1)
                with pe.Fori(0, PAIRS) as i:
                    for par in range(2):
                        gi = l * PAIRS + i
                        g = 2 * gi + par
                        spread(g, block_numbers(2 * i + par), par)
                        pe.wait_ge(alpha_done, START + NG * g + NG)
                        pe.wait_ge(w_done, START + NG * g)
                        pe.transpose(bank[4][:, 0:P], alpha[:, :, :].rearrange("p h t -> p (h t)"), ident[:, :])\
                            .then_inc(alpha_turned, 1)
                        pe.wait_ge(bwd_one, START + g + 1)
                        pe.wait_ge(scale_done, START + g)
                        for k, col in enumerate((fwd[:, P - 1:P], rcol[:, 0:1], bwd[:, 0:1], rcol[:, 1:2])):
                            mm = pe.transpose(bank[5][0:1, k * P:(k + 1) * P], col, ident[:, :])
                        mm.then_inc(rows_turned, 1)
                        pe.wait_ge(carries_packed, START + 2 * g + 2)
                        pe.wait_ge(cols_copied, START + g)
                        pe.matmul(bank[5][:, 0:1], c_row[:, 0, :], ones[0:1, 0:1], start=True, stop=True)
                        pe.matmul(bank[5][:, 1:2], c_row[:, 1, :], ones[0:1, 0:1], start=True, stop=True)\
                            .then_inc(cols_turned, 1)
                        pe.wait_ge(shift_done, START + g + 1)
                        pe.wait_ge(cols_copied, START + g + 1)
                        pe.matmul(bank[5][:, 8:16], oh[:, par, 0, :], shift[:, :], start=True, stop=True)\
                            .then_inc(shift_spread, 1)
                        pe.wait_ge(ex_done, START + g + 1)
                        pe.wait_ge(w_done, START + NG * g)
                        pe.transpose(bank[4][:, P:2 * P], ex[:, :], ident[:, :]).then_inc(ex_turned, 1)
                        add_up(g, gi, par, HEADS * VW, w_done, g)
                with pe.Fori(0, NI) as i:
                    n = NI + 2 * NI * l + NI + i
                    r = l * NI + i
                    turn_blocks(n)
                    pe.wait_ge(t_out, START + 2 * n + 2)
                    for f in range(4):
                        for s in range(2):
                            k = 2 * f + s
                            pe.wait_ge(ffn_act, START + 8 * r + max(k - 3, 0))
                            pe.matmul(bank[2 + k % 4][:, 0:320], w_1[:, f * HID:(f + 1) * HID], hT[:, s * 320:(s + 1) * 320],
                                      start=True, stop=True).then_inc(ffn_ps, 1)
                    pe.wait_ge(ffn_act, START + 8 * r + 8)
                    pe.wait_ge(m_ev, START + NI + r)
                    for b in range(BW):
                        for f in range(4):
                            mm = pe.matmul(bank[6 + b // 4][:, (b % 4) * P:(b % 4 + 1) * P], g1[:, f, b * P:(b + 1) * P],
                                           w_2[:, f, :], start=(f == 0), stop=(f == 3))
                    mm.then_inc(m_ps, 1)
            M0 = NI + NI * L
            with pe.Fori(0, NI) as i:
                turn_blocks(LN_A + 2 * i)
                times(LN_A + 2 * i, M0 + i, w_o[:, :], 64)
                turn_blocks(LN_A + 2 * i + 1)
                pe.wait_ge(t_out, START + 2 * (LN_A + 2 * i + 1) + 2)
                for b in range(BW):
                    pe.wait_ge(a_ev, START + 2 * BW * (L * NI + i) + max(2 * b - 2, 0))
                    pe.matmul(bank[4 + b % 2][:, 0:2 * HID], hT[0:64, b * P:(b + 1) * P], m_1[:, :], start=True, stop=True)\
                        .then_inc(a_ps, 1)
            with pe.Fori(0, PAIRS) as i:
                for par in range(2):
                    gi = L * PAIRS + i
                    g = 2 * gi + par
                    c = 2 * i + par
                    blocks = block_numbers(c)
                    pe.wait_ge(rbf_done, START + c + 1)
                    spread(g, blocks, par, c)
                    add_up(g, gi, par, HID + 1, silu_done, c)
            with pe.Fori(0, NI) as i:
                for k, (weights, width) in enumerate(((m_2, P), (u_1, P), (u_2, 64))):
                    turn_blocks(LN_B + 3 * i + k)
                    times(LN_B + 3 * i + k, M0 + NI + 3 * i + k, weights[:, :], 64, width)

        @block.vector
        def _(dve):
            class Steps:
                def __init__(self, s, base=0):
                    self.s, self.base, self.n = s, base, 0

                def __call__(self, ins):
                    self.n += 1
                    ins.then_inc(self.s, 1)
                    dve.wait_ge(self.s, self.base + self.n)

            step = Steps(su_step, 0)
            dve.memset(ones[:, :], 1.0)
            dve.memset(row[:, :, :], 0.0)
            dve.memset(shift[:, :], 0.0)
            dve.memset(f_in[:, :, :, :], -BIG)
            dve.memset(b_in[:, :, :, :], -BIG)
            dve.memset(edge_word[:, :], -5.0)
            step(dve.memset(edge_bf[:, :], -BIG))
            dve.wait_ge(ld_dst, 16)
            step(dve.tensor_copy(su_f, su_i))
            for b in range(1, NB + 1):
                step(dve.tensor_scalar(su_o, su_f, float(b * P), None, ALU.is_lt, ALU.add, accum_out=row[:, 0, b:b + 1]))
            dve.memset(vt[:, 0, :], 0.0).then_inc(su_count, 1)
            dve.wait_ge(su_count, 2)
            rp = row[:, 1, :]
            step(dve.tensor_copy(rp, bank[7][:, 0:NB + 1]))
            step(dve.tensor_copy(rowi[:, 0, :], rp))
            step(dve.tensor_scalar(rowi[:, 1, :], rowi[:, 0, :], 7, None, ALU.arith_shift_right))
            step(dve.tensor_copy(row[:, 2, :], rowi[:, 1, :]))
            step(dve.tensor_scalar(row[:, 3, :], rp, float(P - 1), None, ALU.add))
            step(dve.tensor_copy(rowi[:, 0, :], row[:, 3, :]))
            step(dve.tensor_scalar(rowi[:, 1, :], rowi[:, 0, :], 7, None, ALU.arith_shift_right))
            step(dve.tensor_copy(row[:, 4, :], rowi[:, 1, :]))
            step(dve.tensor_tensor(row[:, 5, 0:NB], row[:, 4, 1:NB + 1], row[:, 2, 0:NB], ALU.subtract))
            step(dve.tensor_scalar(row[:, 3, 0:NB], row[:, 5, 0:NB], 1.0, None, ALU.add))
            step(dve.tensor_copy(rowi[:, 0, :], row[:, 3, :]))
            step(dve.tensor_scalar(rowi[:, 1, :], rowi[:, 0, :], 1, None, ALU.arith_shift_right))
            step(dve.tensor_copy(row[:, 6, 0:NB], rowi[:, 1, 0:NB]))
            step(dve.tensor_tensor_scan(row[:, 7, 0:NB], ones[:, 0:NB], row[:, 6, 0:NB], 0.0, op0=ALU.mult, op1=ALU.add))
            step(dve.tensor_tensor(row[:, 8, 0:NB], row[:, 7, 0:NB], row[:, 6, 0:NB], ALU.subtract))
            step(dve.scalar_tensor_tensor(out=row[:, 9, 0:NB], in0=row[:, 8, 0:NB], scalar=-2.0, in1=row[:, 2, 0:NB],
                                          op0=ALU.mult, op1=ALU.add))
            step(dve.tensor_tensor(row[:, 10, 0:NB - 1], row[:, 9, 1:NB], row[:, 9, 0:NB - 1], ALU.subtract))
            dve.wait_ge(ld_const, 16 * 13)
            for c in range(VC):
                for k, w in ((0, ones[:, 0:NB]), (1, row[:, 10, 0:NB])):
                    step(dve.scalar_tensor_tensor(out=row[:, 11, 0:NB], in0=row[:, 7, 0:NB], scalar=place[:, 1, c:c + 1], in1=w,
                                                  op0=ALU.is_le, op1=ALU.mult, accum_out=vt[:, k, c:c + 1]))
            step(dve.tensor_tensor(vt[:, 2, :], vt[:, 1, :], place[:, 0, :], ALU.add))
            step(dve.tensor_scalar(vt[:, 2, :], vt[:, 2, :], float(TILES - 1), None, ALU.min))
            step(dve.tensor_scalar(vt[:, 3, :], vt[:, 0, :], float(NB - 1), None, ALU.min))
            step(dve.tensor_copy(vti[:, 1, :], vt[:, 3, :]))
            dve.tensor_copy(vti[:, 0, :], vt[:, 2, :]).then_inc(su_idx, 1)
            step(dve.tensor_scalar(vt[:, 1, :], vt[:, 0, :], float(P), None, ALU.mult))
            dve.wait_ge(su_rows, 16 * 3 * VC)
            step(dve.tensor_copy(rows_f, rows_d))
            for c in range(VC):
                step(dve.tensor_scalar(r_rel[:, c, :], rows_f[:, c, :], vt[:, 1, c:c + 1], None, ALU.subtract))
            step(dve.tensor_scalar(r_ok, r_rel, 0.0, None, ALU.is_ge))
            step(dve.tensor_scalar(r_dst, r_rel, float(P), None, ALU.is_lt))
            step(dve.tensor_tensor(r_ok, r_ok, r_dst, ALU.mult))
            step(dve.scalar_tensor_tensor(out=r_dst, in0=rows_f, scalar=1.0, in1=r_ok, op0=ALU.add, op1=ALU.mult))
            step(dve.tensor_scalar(r_dst, r_dst, -1.0, None, ALU.add))
            dve.tensor_copy(vt[:, 3, 0:1], vt[:, 2, 0:1]).then_inc(su_flat, 1)
            step(dve.tensor_copy(r_src, rows_i))
            dve.tensor_copy(vt[:, 3, 1:2], vt[:, 2, 1:2]).then_inc(su_turn, 1)
            for k in range(2 * VC):
                c = k % VC
                dve.wait_ge(su_turned, k + 1)
                dst = src_e if k < VC else rel_e
                dve.tensor_copy(dst[:, c * P:(c + 1) * P], bank[4 + k % 2][:, 0:P]).then_inc(su_taken, 1)
                dve.wait_ge(su_taken, k + 1)
                dve.tensor_copy(vt[:, 3, 2:3], vt[:, 2, 2:3]).then_inc(su_done, 1)
            dve.wait_ge(su_prev, 32)
            step(dve.tensor_tensor(r_dst, r_dst, r_prev, ALU.not_equal))
            step(dve.tensor_scalar(r_bf[:, :, :], r_dst, -BIG, None, ALU.mult))
            dve.tensor_copy(vt[:, 3, 3:4], vt[:, 2, 3:4]).then_inc(su_rst, 1)
            dve.wait_ge(su_tabs, 16 * 2 * HEADS)
            step(dve.tensor_reduce(rst_sum[:, :, 0], rst[:, :, :], axis=X, op=ALU.add))
            step(dve.tensor_copy(rst_b[:, :, :], rst_r[:, :, ::-1]))
            step(dve.tensor_reduce(rst_sum[:, :, 1], rst_b[:, :, :], axis=X, op=ALU.add))
            step(dve.tensor_scalar(cont[:, :], rst[0:1, :, 0], -1.0, None, ALU.is_ge))

            step(dve.memset(tsrc, 0.0))
            with dve.Fori(0, NI) as i:
                dve.wait_ge(t_ps, START + i)
                dve.tensor_scalar(tsrc[:, :, 0:64], xn[:, bass.ds(i * BW, BW), :], 0.0, None, ALU.add).then_inc(t_in, 1)
                dve.wait_ge(m_ps, START + i + 1)
                dve.wait_ge(h_new, START + i)
                dve.tensor_tensor(t1[:, 0:4, :], bank[2][:, :].rearrange("p (b k) -> p b k", b=4),
                                  bc(vec1[:, VEC1["bi"]:VEC1["bi"] + P], 4), ALU.add).then_inc(node_done, 1)
                dve.tensor_tensor(t1[:, 4, :], bank[3][:, 0:P], vec1[:, VEC1["bi"]:VEC1["bi"] + P], ALU.add).then_inc(m_ev, 1)
                dve.wait_ge(m_ev, START + i + 1)
                dve.wait_ge(node_done, START + i + 1)
                dve.tensor_copy(st[5][:, :], ones[:, 0:BW]).then_inc(post, 1)

            def norm(step, width, request):
                y, z = t1[:, :, 0:width], t2[:, :, 0:width]
                step(dve.tensor_reduce(st[2][:, :], y, axis=X, op=ALU.add))
                step(dve.tensor_scalar(st[2][:, :], st[2][:, :], 1.0 / width, None, ALU.mult))
                step(dve.tensor_tensor(y, y, bcl(st[2][:, :], width), ALU.subtract))
                step(dve.tensor_tensor(z, y, y, ALU.mult))
                step(dve.tensor_reduce(st[5][:, :], z, axis=X, op=ALU.add))
                dve.tensor_scalar(st[3][:, :], st[5][:, :], 1.0 / width, 1e-5, ALU.mult, ALU.add).then_inc(act_req, 1)
                dve.wait_ge(act_ans, START + request)
                step(dve.reciprocal(st[6][:, :], st[4][:, :]))
                step(dve.tensor_tensor(y, y, bcl(st[6][:, :], width), ALU.mult))

            def onehots(g, gi, par, c):
                dve.wait_ge(slot_free[par][NG - 1], START + gi)
                dve.tensor_tensor(oh[:, par, :, :], bc(iota[:, :], CH), bcl(rel_e[:, bass.ds(c * CH, CH)], P),
                                  ALU.is_equal).then_inc(oh_made, 1)

            def add_parts(g, gi, par, blocks, width):
                for s in range(CH // 2):
                    if s % 2 == 0:
                        dve.wait_ge(part_even, START + (CH // 4) * g + s // 2 + 1)
                    else:
                        dve.wait_ge(slot_free[par][s // 2], START + gi + 1)
                    dve.wait_ge(acc_done, START + (CH // 2) * g + s)
                    a_s = acc[:, blocks[s], 0:width]
                    dve.tensor_tensor(a_s, a_s, bank[6 + s % 2][:, 0:width], ALU.add).then_inc(acc_done, 1)

            def block_numbers(c):
                return [dve.value_load(blk[0:1, bass.ds(c * CH + 2 * s, 1)], min_val=0, max_val=NB - 1) for s in range(CH // 2)]

            with dve.Fori(0, L) as l:
                with dve.Fori(0, NI) as i:
                    ga = l * NI + i
                    dve.wait_ge(ld_layer, 96 * (l + 1))
                    dve.wait_ge(tab_free, START + ga)
                    for b in range(BW):
                        dve.wait_ge(a_ps, START + 2 * BW * ga + 2 * b + 1)
                        dve.tensor_tensor(qs[:, i * BW + b, :], bank[2 + b % 2][:, 0:QS], vec0[:, VEC0["qs"]:VEC0["qs"] + QS],
                                          ALU.add).then_inc(a_ev, 1)
                        dve.wait_ge(a_ps, START + 2 * BW * ga + 2 * b + 2)
                        dve.tensor_tensor(kvst[:, b, :], bank[4 + b % 2][:, 0:BAND], vec0[:, VEC0["kv"]:VEC0["kv"] + BAND],
                                          ALU.add).then_inc(a_ev, 1)
                dve.wait_ge(tab_out, 16 * NI * (l + 1))
                dve.wait_ge(a_ev, START + 2 * BW * NI * (l + 1))
                dve.memset(f_out[:, :, :], -BIG).then_inc(node_done, 1)
                dve.memset(acc[:, :, :], 0.0).then_inc(acc_zero, 1)
                with dve.Fori(0, PAIRS) as i:
                    for par in range(2):
                        dve.wait_ge(acc_zero, START + l + 1)
                        dve.wait_ge(node_done, START + NI + l + 1)
                        gi = l * PAIRS + i
                        g = 2 * gi + par
                        c = 2 * i + par
                        blocks = block_numbers(c)
                        onehots(g, gi, par, c)
                        dve.wait_ge(rows_turned, START + g)
                        dve.tensor_scalar(rcol[:, :], rst_sum[:, c, :], 0.0, None, ALU.add).then_inc(rcol_done, 1)
                        for j in range(NG):
                            dve.wait_ge(kv_in[par][j], 16 * G * (gi + 1))
                            dve.wait_ge(q_spread, START + NG * g + j + 1)
                            keys = slots[:, par, j * G:(j + 1) * G, 0:HID]
                            dve.tensor_tensor(keys, keys, bank[2 + j % 2][:, :].rearrange("p (t k) -> p t k", t=G),
                                              ALU.mult).then_inc(spread_used, 1)
                            dve.wait_ge(spread_used, START + NG * g + j + 1)
                            dve.tensor_reduce(alpha[:, :, j * G:(j + 1) * G].rearrange("p h t -> p t h"),
                                              keys.rearrange("p t (h d) -> p t h d", h=HEADS), axis=X, op=ALU.add)\
                                .then_inc(alpha_done, 1)
                        dve.wait_ge(alpha_turned, START + g + 1)
                        aT = bank[4][:, 0:P]
                        R, Rb = rst[:, c, :], rst_b[:, c, :]
                        dve.tensor_tensor_scan(fwd[:, :], R, aT, -BIG, op0=ALU.add, op1=ALU.max).then_inc(fwd_one, 1)
                        dve.wait_ge(fwd_one, START + g + 1)
                        dve.wait_ge(rcol_done, START + g + 1)
                        dve.tensor_tensor_scan(bwd[:, ::-1], Rb, aT[:, ::-1], -BIG, op0=ALU.add, op1=ALU.max)\
                            .then_inc(bwd_one, 1)
                        dve.tensor_copy(f_in[:, 0, :, 0:1], f_out[:, :, CH:CH + 1]).then_inc(carry_set, 1)
                        dve.wait_ge(carry_set, START + g + 1)
                        dve.wait_ge(rows_copied, START + 2 * g + 2)
                        dve.tensor_tensor_scan(f_out[:, :, :].rearrange("p h t -> p (h t)"),
                                               f_in[:, 1, :, :].rearrange("p h t -> p (h t)"),
                                               f_in[:, 0, :, :].rearrange("p h t -> p (h t)"), -BIG, op0=ALU.add, op1=ALU.max)\
                            .then_inc(f_done, 1)
                        dve.wait_ge(f_done, START + g + 1)
                        dve.tensor_tensor_scan(b_out[:, :, :].rearrange("p h t -> p (h t)")[:, ::-1],
                                               b_in[:, 1, :, :].rearrange("p h t -> p (h t)")[:, ::-1],
                                               b_in[:, 0, :, :].rearrange("p h t -> p (h t)")[:, ::-1], -BIG,
                                               op0=ALU.add, op1=ALU.max).then_inc(b_done, 1)
                        dve.wait_ge(b_done, START + g + 1)
                        dve.wait_ge(cols_turned, START + g)
                        dve.tensor_copy(c_row[:, 0, :].rearrange("p (h t) -> p h t", h=HEADS), f_out[:, :, 0:CH])\
                            .then_inc(carries_packed, 1)
                        dve.tensor_copy(c_row[:, 1, :].rearrange("p (h t) -> p h t", h=HEADS), b_out[:, :, 1:CH + 1])\
                            .then_inc(carries_packed, 1)
                        dve.tensor_tensor(gap[:, :], f_in[:, 0, :, 0], b_out[:, :, 0], ALU.subtract).then_inc(gap_done, 1)
                        dve.wait_ge(gap_done, START + g + 1)
                        dve.wait_ge(shift_spread, START + g)
                        dve.tensor_scalar(shift[0:1, :], gap[:, :], 0.0, cont[:, bass.ds(c, 1)], ALU.min, ALU.mult)\
                            .then_inc(shift_done, 1)
                        dve.wait_ge(cols_copied, START + g + 1)
                        dve.tensor_tensor_scan(fwd[:, :], R, aT, icol[:, 0:1], op0=ALU.add, op1=ALU.max).then_inc(fwd_two, 1)
                        dve.wait_ge(bwd_one, START + g + 1)
                        dve.tensor_tensor_scan(bwd[:, ::-1], Rb, aT[:, ::-1], icol[:, 1:2], op0=ALU.add, op1=ALU.max)\
                            .then_inc(bwd_two, 1)
                        dve.wait_ge(fwd_two, START + g + 1)
                        dve.wait_ge(bwd_two, START + g + 1)
                        dve.tensor_tensor(fwd[:, :], fwd[:, :], bwd[:, :], ALU.max).then_inc(max_done, 1)
                        dve.wait_ge(max_done, START + g + 1)
                        dve.tensor_tensor(bwd[:, :], aT, fwd[:, :], ALU.subtract).then_inc(arg_done, 1)
                        dve.wait_ge(scale_done, START + g + 1)
                        dve.wait_ge(acc_done, START + (CH // 2) * g)
                        a_0 = acc[:, blocks[0], :].rearrange("p (h k) -> p h k", h=HEADS)
                        dve.tensor_tensor(a_0, a_0, bcl(scale[:, :], VW), ALU.mult).then_inc(acc_scaled, 1)
                        dve.wait_ge(ex_turned, START + g + 1)
                        exs = bank[4][:, P:2 * P].rearrange("p (h t) -> p t h", h=HEADS)
                        for j in range(NG):
                            vals = slots[:, par, j * G:(j + 1) * G, HID:KVW].rearrange("p t (h k) -> p t h k", h=HEADS)
                            dve.tensor_tensor(vals, vals, bcl(exs[:, j * G:(j + 1) * G, :], VW), ALU.mult).then_inc(w_done, 1)
                        dve.wait_ge(acc_scaled, START + g + 1)
                        add_parts(g, gi, par, blocks, HEADS * VW)
                with dve.Fori(0, NI) as i:
                    r = l * NI + i
                    dve.wait_ge(acc_done, START + (CH // 2) * CHUNKS * (l + 1))
                    K = 25
                    step = Steps(post, START + NI + K * r)
                    bs = bass.ds(i * BW, BW)
                    a5 = acc[:, bs, :].rearrange("p b (h k) -> p b h k", h=HEADS)
                    xr = qs[:, bs, HID:2 * HID]
                    v = lambda name: bc(vec0[:, VEC0[name]:VEC0[name] + P], BW)
                    step(dve.tensor_scalar(den[:, :, :], a5[:, :, :, DH], 1e-16, None, ALU.add))
                    step(dve.reciprocal(rden[:, :, :], den[:, :, :]))
                    for b in range(BW):
                        step(dve.tensor_tensor(o_t[:, b, :].rearrange("p (h k) -> p h k", h=HEADS),
                                               acc[:, i * BW + b, :].rearrange("p (h k) -> p h k", h=HEADS)[:, :, 0:DH],
                                               bcl(rden[:, b, :], DH), ALU.mult))
                    step(dve.tensor_tensor(dx[:, :, :], o_t, xr, ALU.subtract))
                    step(dve.tensor_tensor(t1, o_t, v("w0"), ALU.mult))
                    step(dve.tensor_tensor(t2[:, :, :], xr, v("w1"), ALU.mult))
                    step(dve.tensor_tensor(t1, t1, t2[:, :, :], ALU.add))
                    step(dve.tensor_tensor(t2[:, :, :], dx[:, :, :], v("w2"), ALU.mult))
                    step(dve.tensor_tensor(t1, t1, t2[:, :, :], ALU.add))
                    dve.tensor_reduce(st[0][:, :], t1, axis=X, op=ALU.add).then_inc(act_req, 1)
                    dve.wait_ge(act_ans, START + 2 * r + 1)
                    step(dve.tensor_tensor(t2[:, :, :], dx[:, :, :], bcl(st[1][:, :], P), ALU.mult))
                    step(dve.tensor_tensor(t1, o_t, t2[:, :, :], ALU.subtract))
                    step(dve.tensor_tensor(t1, t1, h[:, bs, :], ALU.add))
                    norm(step, HID, 2 * r + 2)
                    step(dve.tensor_tensor(t1, t1, v("g"), ALU.mult))
                    assert step.n == K - 1 - 0, step.n
                    dve.wait_ge(t_ps, START + NI + 2 * NI * l + NI + i)
                    dve.tensor_tensor(tsrc, t1, v("b"), ALU.add).then_inc(t_in, 1)
                    dve.wait_ge(t_in, START + NI + 2 * NI * l + NI + i + 1)
                    step(dve.tensor_tensor(t2[:, :, :], tsrc, v("b2"), ALU.add))
                    dve.wait_ge(m_ps, START + NI + r + 1)
                    dve.tensor_tensor(h[:, bass.ds(i * BW, 4), :], bank[6][:, :].rearrange("p (b k) -> p b k", b=4), t2[:, 0:4, :],
                                      ALU.add).then_inc(m_ev, 1)
                    dve.tensor_tensor(h[:, i * BW + 4, :], bank[7][:, 0:P], t2[:, 4, :], ALU.add).then_inc(h_new, 1)
                    dve.wait_ge(m_ev, START + NI + r + 1)
                    dve.wait_ge(h_new, START + NI * (l + 1) + i + 1)
            P0 = NI + 25 * NI * L
            v1 = lambda name, w=64: bc(vec1[:, VEC1[name]:VEC1[name] + w], BW)
            with dve.Fori(0, NI) as i:
                bs = bass.ds(i * BW, BW)
                K = 11
                step = Steps(post, START + P0 + K * i)
                y = t1[:, :, 0:64]
                dve.wait_ge(m_ps, START + NI + NI * L + i + 1)
                step(dve.tensor_tensor(t1[:, 0:4, 0:64], bank[2][:, :].rearrange("p (b k) -> p b k", b=4)[:, :, 0:64],
                                       bc(vec1[:, VEC1["bo"]:VEC1["bo"] + 64], 4), ALU.add))
                dve.tensor_tensor(t1[:, 4, 0:64], bank[3][:, 0:64], vec1[:, VEC1["bo"]:VEC1["bo"] + 64], ALU.add).then_inc(m_ev, 1)
                dve.wait_ge(m_ev, START + NI + NI * L + i + 1)
                step(dve.tensor_tensor(y, y, xn[:, bs, :], ALU.add))
                norm(step, 64, 2 * L * NI + i + 1)
                step(dve.tensor_scalar(xn[:, bs, :], y, 0.0, None, ALU.add))
                dve.wait_ge(t_ps, START + LN_A + 2 * i + 1)
                dve.tensor_copy(tsrc[:, :, 0:64], y).then_inc(t_in, 1)
                step(dve.tensor_copy(st[5][:, :], ones[:, 0:BW]))
                assert step.n == K, step.n
                dve.wait_ge(tab_free, START + L * NI + i)
                for b in range(BW):
                    dve.wait_ge(a_ps, START + 2 * BW * L * NI + BW * i + b + 1)
                    dve.tensor_tensor(qs[:, i * BW + b, 0:HID], bank[4 + b % 2][:, HID:2 * HID],
                                      vec1[:, VEC1["mb1"]:VEC1["mb1"] + HID], ALU.add).then_inc(a_ev, 1)
                    dve.tensor_copy(kvst[:, b, 0:HID], bank[4 + b % 2][:, 0:HID]).then_inc(a_ev, 1)
            dve.wait_ge(tab_out, 16 * NI * (L + 1))
            dve.wait_ge(a_ev, START + 2 * BW * NI * (L + 1))
            dve.memset(slots[:, :, :, 2 * HID:2 * HID + 1], 1.0).then_inc(one_set, 1)
            dve.memset(acc[:, :, :], 0.0).then_inc(acc_zero, 1)
            dve.wait_ge(one_set, START + 1)
            dve.wait_ge(acc_zero, START + L + 1)
            with dve.Fori(0, PAIRS) as i:
                for par in range(2):
                    gi = L * PAIRS + i
                    g = 2 * gi + par
                    c = 2 * i + par
                    blocks = block_numbers(c)
                    onehots(g, gi, par, c)
                    for j in range(NG):
                        dve.wait_ge(kv_in[par][j], 16 * G * (gi + 1))
                        dve.wait_ge(q_spread, START + NG * g + j + 1)
                        dve.tensor_tensor(slots[:, par, j * G:(j + 1) * G, HID:2 * HID], slots[:, par, j * G:(j + 1) * G, 0:HID],
                                          bank[2 + j % 2][:, :].rearrange("p (t k) -> p t k", t=G), ALU.add)\
                            .then_inc(spread_used, 1)
                    add_parts(g, gi, par, blocks, HID + 1)
            P1 = P0 + 11 * NI
            dve.wait_ge(acc_done, START + (CH // 2) * CHUNKS * (L + 1))
            with dve.Fori(0, NI) as i:
                bs = bass.ds(i * BW, BW)
                K = 26
                step = Steps(post, START + P1 + K * i)
                M1 = NI + NI * L + NI + 3 * i
                T1 = LN_B + 3 * i
                R1 = 2 * L * NI + NI + 3 * i
                Q1 = 2 * L * NI + NI + 2 * i
                cnt = acc[:, bs, HID]
                step(dve.tensor_scalar(st[0][:, :], cnt, 1.0, None, ALU.max))
                step(dve.reciprocal(st[1][:, :], st[0][:, :]))
                step(dve.tensor_tensor(st[2][:, :], cnt, st[1][:, :], ALU.mult))
                dve.wait_ge(t_ps, START + T1)
                dve.tensor_tensor(tsrc, acc[:, bs, 0:HID], bcl(st[1][:, :], HID), ALU.mult).then_inc(t_in, 1)
                step(dve.tensor_tensor(t2[:, :, 0:64], v1("mb2"), bcl(st[2][:, :], 64), ALU.mult))

                def evac(m, other4, other1, out4, out1):
                    dve.wait_ge(m_ps, START + m + 1)
                    step(dve.tensor_tensor(out4, bank[2][:, :].rearrange("p (b k) -> p b k", b=4)[:, :, 0:64], other4, ALU.add))
                    dve.tensor_tensor(out1, bank[3][:, 0:64], other1, ALU.add).then_inc(m_ev, 1)
                    dve.wait_ge(m_ev, START + m + 1)

                bias = lambda name: (bc(vec1[:, VEC1[name]:VEC1[name] + 64], 4), vec1[:, VEC1[name]:VEC1[name] + 64])
                evac(M1, t2[:, 0:4, 0:64], t2[:, 4, 0:64], t1[:, 0:4, 64:128], t1[:, 4, 64:128])
                step(dve.tensor_scalar(t1[:, :, 0:64], xn[:, bs, :], 0.0, None, ALU.add))
                dve.wait_ge(t_ps, START + T1 + 1)
                dve.tensor_copy(tsrc, t1).then_inc(t_in, 1)
                evac(M1 + 1, *bias("ub1"), t1[:, 0:4, 0:64], t1[:, 4, 0:64])
                step(dve.tensor_copy(st[5][:, :], ones[:, 0:BW]))
                dve.tensor_copy(st[6][:, :], ones[:, 0:BW]).then_inc(act_req, 1)
                evac(M1 + 2, *bias("ub2"), t1[:, 0:4, 0:64], t1[:, 4, 0:64])
                y = t1[:, :, 0:64]
                norm(step, 64, Q1 + 1)
                step(dve.tensor_tensor(y, y, v1("g"), ALU.mult))
                step(dve.tensor_tensor(y, y, v1("b"), ALU.add))
                step(dve.tensor_tensor(y, y, xn[:, bs, :], ALU.add))
                norm(step, 64, Q1 + 2)
                dve.wait_ge(out_free, START + i)
                dve.tensor_copy(dx[:, :, 0:64], y).then_inc(out_ready, 1)
                assert step.n == K, step.n


RBF_WIDTH = (10.0 / (NBASIS - 1)) * 0.5
RBF_SCALE = -1.0 / (2.0 * RBF_WIDTH ** 2)


def lay_out(inp):
    f = {k: np.asarray(v) for k, v in inp.items()}
    z = lambda *s: np.zeros(s, np.float32)
    a = {}
    a["x"] = np.concatenate([f["x"], z(NPAD - N, 64)])
    pad = TILES * P - E
    a["src_t"] = np.concatenate([f["src"], np.zeros(pad, np.int32)]).reshape(TILES, P)
    a["dst_t"] = np.concatenate([f["dst"], np.full(pad, 2 * NPAD, np.int32)]).reshape(TILES, P)
    a["len_t"] = np.concatenate([f["edge_weight1"][:, 0], z(pad)]).reshape(TILES, P)
    n = {k[7:]: v for k, v in f.items() if k.startswith("L0_gnn_")}
    m = {k[7:]: v for k, v in f.items() if k.startswith("L1_gnn_")}
    T = lambda w: w.transpose(0, 2, 1)
    a["w_qs"] = np.concatenate([T(n["Wq"]), T(n["Ws"])], 2).reshape(L * P, QS)
    wide = lambda v, fill: np.concatenate([v.reshape(*v.shape[:-1], HEADS, DH), np.full((*v.shape[:-1], HEADS, 1), fill, np.float32)],
                                          -1).reshape(*v.shape[:-1], HEADS * VW)
    a["w_kv"] = np.concatenate([T(n["Wk"]), wide(T(n["Wv"]), 0.0)], 2).reshape(L * P, BAND)
    a["w_1"] = T(n["W1"]).reshape(L * P, 4 * HID)
    a["b_1"] = n["b1"].reshape(L, 4, HID).transpose(0, 2, 1).reshape(L * P, 4)
    a["w_2"] = T(n["W2"]).reshape(L, 4, HID, HID).transpose(0, 2, 1, 3).reshape(L * P, 4 * HID)
    a["vec0"] = np.concatenate([n["Wbeta"][:, 0, :], n["ln_g"], n["ln_b"], n["b2"], n["bq"], n["bs"], n["bk"], wide(n["bv"], 1.0)], 1)
    a["vec1"] = np.concatenate([n["bi"], n["bo"], m["mb1"], m["mb2"], m["ub1"], m["ub2"], m["ln_g"], m["ln_b"]])[None]
    a["w_i"], a["w_o"] = n["Wi"].T, n["Wo"].T
    a["m_1"] = np.concatenate([m["mw1"][0:64], m["mw1"][64:128]], 1)
    a["m_1c"], a["m_2"], a["u_1"], a["u_2"] = m["mw1"][128:], m["mw2"], m["uw1"], m["uw2"]
    a["ident"] = np.eye(P, dtype=np.float32)
    a["iota"] = np.tile(np.arange(P, dtype=np.float32), (P, 1))
    v = np.arange(VC * P, dtype=np.float32).reshape(VC, P).T
    a["place"] = np.stack([v, np.floor(v / 2)], 1).astype(np.float32)
    a["centers"] = -np.linspace(0.0, 10.0, NBASIS, dtype=np.float32)[:, None]
    return {k: np.ascontiguousarray(v) for k, v in a.items()}


def kernel(**inputs):
    import concourse.bacc as bacc
    from concourse.bass_utils import run_bass_kernel_spmd

    nc = bacc.Bacc("TRN2", target_bir_lowering=False, num_devices=1)
    laid = lay_out(inputs)
    arrays = {f"in_{k}": v for k, v in laid.items()}
    aps = {k: nc.dram_tensor(f"in_{k}", v.shape, mybir.dt.from_np(v.dtype), kind="ExternalInput").ap() for k, v in laid.items()}
    out = nc.dram_tensor("out_0", (N, 64), F32, kind="ExternalOutput").ap()
    build_program(nc, aps, out)
    r = run_bass_kernel_spmd(nc, [arrays], core_ids=[0])
    return r.results[0]["out_0"]
```

```python
from contextlib import ExitStack

import numpy as np

import concourse.bass as bass
from concourse import mybir

F32 = mybir.dt.float32
BF16 = mybir.dt.bfloat16
I32 = mybir.dt.int32
ALU = mybir.AluOpType
ACT = mybir.ActivationFunctionType
X = mybir.AxisListType.X

P = 128
N = 3125
E = 100000
L = 4
HEADS, DH = 8, 16
HID = HEADS * DH
NB = -(-N // P)
NPAD = NB * P
TILES = -(-E // P) + 2
SUPERS = (-(-E // P) + NB - 1 + NB) // 2 + 1
CH = 16
RING = 4
CHUNKS = RING * (-(-2 * SUPERS // (RING * CH)))
V = CHUNKS * CH
VC = -(-V // P)
TURNS = CHUNKS // RING
G = 4
NG = CH // G
VW = DH + 1
KVW = HID + HEADS * VW
BW = 5
NI = NB // BW
BIG = 1.0e30
START = (RING - 1) * NG + 1
NBASIS = 16
QS, BAND = 2 * HID, KVW
VEC0 = {"w0": 0, "w1": 128, "w2": 256, "g": 384, "b": 512, "b2": 640, "qs": 768, "kv": 1024}
VEC0_W = 1024 + KVW
VEC1 = {"bi": 0, "bo": 128, "mb1": 192, "mb2": 320, "ub1": 384, "ub2": 448, "g": 512, "b": 576}
VEC1_W = 640
assert NB % BW == 0 and V >= 2 * SUPERS


def build_program(nc, a, out):
    with ExitStack() as ctx:
        def sb(name, shape, dt=F32):
            return ctx.enter_context(nc.sbuf_tensor(name, shape, dt))

        def sem(name):
            return ctx.enter_context(nc.semaphore(name))

        def sems(name, n):
            return [sem(f"{name}{k}") for k in range(n)]

        bank = [ctx.enter_context(nc.psum_tensor(f"bank{k}", [P, 512], F32)) for k in range(8)]

        kv_table = nc.dram_tensor("kv_table", [NPAD, KVW], F32, kind="Internal").ap()
        src_table = nc.dram_tensor("src_table", [NPAD, HID], F32, kind="Internal").ap()
        flat_dst = nc.dram_tensor("flat_dst", [VC * P * P + P], F32, kind="Internal").ap()
        flat_rst = nc.dram_tensor("flat_rst", [VC * P * P + P], BF16, kind="Internal").ap()
        flat_len = nc.dram_tensor("flat_len", [VC * P * P], F32, kind="Internal").ap()
        flat_blk = nc.dram_tensor("flat_blk", [VC * P], I32, kind="Internal").ap()

        ident = sb("ident", [P, P])
        iota = sb("iota", [P, P])
        place = sb("place", [P, 2, VC])
        centers = sb("centers", [NBASIS, 1])
        ones = sb("ones", [P, P])
        h = sb("h", [P, NB, HID])
        xn = sb("xn", [P, NB, 64])
        qs = sb("qs", [P, NB, QS])
        acc = sb("acc", [P, NB, HEADS * VW])
        src_e = sb("src_e", [P, VC * P], I32)
        rel_e = sb("rel_e", [P, VC * P])
        super_blk = sb("super_blk", [1, VC * P // 2], I32)
        resets = sb("resets", [P, 2, CHUNKS, P], BF16)
        rst = resets[:, 0, :, :]
        rst_b = resets[:, 1, :, :]
        rst_sum = sb("rst_sum", [P, CHUNKS, 2])
        cont = sb("cont", [1, CHUNKS])
        w_qs = sb("w_qs", [P, QS])
        w_kv = sb("w_kv", [P, BAND])
        w_1 = sb("w_1", [P, 4 * HID])
        b_1 = sb("b_1", [P, 4])
        w_2 = sb("w_2", [P, 4, HID])
        vec0 = sb("vec0", [P, VEC0_W])
        vec1 = sb("vec1", [P, VEC1_W])
        w_i = sb("w_i", [64, HID])
        w_o = sb("w_o", [P, 64])
        m_1 = sb("m_1", [64, 2 * HID])
        m_1c = sb("m_1c", [NBASIS, HID])
        m_2 = sb("m_2", [P, 64])
        u_1 = sb("u_1", [P, 64])
        u_2 = sb("u_2", [64, 64])
        slots = sb("slots", [P, RING, CH, KVW])
        flat_slots = slots[:, :, :, :].rearrange("p a c k -> p (a c k)")
        idx = sb("idx", [P, RING, CH], I32)
        oh = sb("oh", [P, 2, CH, P])
        ohT = sb("ohT", [P, 2, G, P])
        alpha = sb("alpha", [P, HEADS, CH])
        rcol = sb("rcol", [P, 2])
        fwd = sb("fwd", [P, P])
        bwd = sb("bwd", [P, P])
        ex = sb("ex", [P, P])
        f_in = sb("f_in", [1, 2, HEADS, CH + 1])
        b_in = sb("b_in", [1, 2, HEADS, CH + 1])
        f_out = sb("f_out", [1, HEADS, CH + 1])
        b_out = sb("b_out", [1, HEADS, CH + 1])
        c_row = sb("c_row", [1, 2, P])
        icol = sb("icol", [P, 2])
        gap = sb("gap", [1, HEADS])
        shift = sb("shift", [P, HEADS])
        scale = sb("scale", [P, HEADS])
        rbf = resets[0:NBASIS, :, :, :].rearrange("p a c e -> p (a c e)")[:, 0:4 * CH * P].bitcast(F32)\
            .rearrange("p (a k) -> p a k", a=2)
        at = [0]

        def node_tile(width):
            s = at[0]
            at[0] += width
            assert at[0] <= RING * CH * KVW
            return flat_slots[:, s:s + width]

        tsrc = node_tile(BW * P).rearrange("p (b k) -> p b k", b=BW)
        hT = node_tile(BW * P)
        kvst = node_tile(BW * KVW).rearrange("p (b k) -> p b k", b=BW)
        g1 = node_tile(4 * BW * P).rearrange("p (f k) -> p f k", f=4)
        at[0] = BW * P * 2
        o_t = node_tile(BW * P).rearrange("p (b k) -> p b k", b=BW)
        at[0] = BW * P * 2 + BW * KVW + 4 * BW * P
        t1 = node_tile(BW * P).rearrange("p (b k) -> p b k", b=BW)
        t2 = node_tile(BW * P).rearrange("p (b k) -> p b k", b=BW)
        dx = node_tile(BW * P).rearrange("p (b k) -> p b k", b=BW)
        den = sb("den", [P, BW, HEADS])
        rden = sb("rden", [P, BW, HEADS])
        st = [sb(f"st{k}", [P, BW]) for k in range(7)]
        su_f = flat_slots[:, 0:TILES]
        su_i = flat_slots[:, TILES:2 * TILES].bitcast(I32)
        su_o = flat_slots[:, 2 * TILES:3 * TILES]
        row = flat_slots[:, 9000:9000 + 12 * (NB + 1)].rearrange("p (a b) -> p a b", a=12)
        rowi = sb("rowi", [P, 4, NB + 1], I32)
        vt = sb("vt", [P, 4, VC])
        vti = sb("vti", [P, 2, VC], I32)
        rows_i = flat_slots[:, 3000:3000 + VC * P].rearrange("p (c e) -> p c e", c=VC).bitcast(I32)
        rows_d = flat_slots[:, 4000:4000 + VC * P].rearrange("p (c e) -> p c e", c=VC).bitcast(I32)
        rows_l = flat_slots[:, 5000:5000 + VC * P].rearrange("p (c e) -> p c e", c=VC)
        rows_f = flat_slots[:, 6000:6000 + VC * P].rearrange("p (c e) -> p c e", c=VC)
        rst_r = flat_slots[:, 0:CHUNKS * P // 2].bitcast(BF16).rearrange("p (c e) -> p c e", c=CHUNKS)
        oh_f = oh[:, :, :, :].rearrange("p a c k -> p (a c k)")
        r_dst = oh_f[:, 0:VC * P].rearrange("p (c e) -> p c e", c=VC)
        r_rel = oh_f[:, 900:900 + VC * P].rearrange("p (c e) -> p c e", c=VC)
        r_ok = oh_f[:, 1800:1800 + VC * P].rearrange("p (c e) -> p c e", c=VC)
        r_prev = oh_f[:, 2700:2700 + VC * P].rearrange("p (c e) -> p c e", c=VC)
        blk = flat_slots[0:1, 10000:10000 + VC * P].bitcast(I32)
        r_bf = flat_slots[:, 8000:8000 + VC * P // 2].bitcast(BF16).rearrange("p (c e) -> p c e", c=VC)
        r_src = flat_slots[:, 7000:7000 + VC * P].rearrange("p (c e) -> p c e", c=VC)
        edge_word = sb("edge_word", [1, 2])
        edge_bf = sb("edge_bf", [1, 2], BF16)

        ld_const, ld_w1, ld_layer, ld_dst = sem("ld_const"), sem("ld_w1"), sem("ld_layer"), sem("ld_dst")
        su_step, su_count, su_idx, su_rows = sem("su_step"), sem("su_count"), sem("su_idx"), sem("su_rows")
        su_flat, su_prev, su_rst, su_tabs = sem("su_flat"), sem("su_prev"), sem("su_rst"), sem("su_tabs")
        su_turn, su_turned, su_taken, su_done = sem("su_turn"), sem("su_turned"), sem("su_taken"), sem("su_done")
        su_pool, su_len, su_rstd, su_dstd = sem("su_pool"), sem("su_len"), sem("su_rstd"), sem("su_dstd")
        t_in, t_ps, t_out = sem("t_in"), sem("t_ps"), sem("t_out")
        m_ps, m_ev, ffn_ps, ffn_act = sem("m_ps"), sem("m_ev"), sem("ffn_ps"), sem("ffn_act")
        h_new, a_ps, a_ev, tab_out, post = sem("h_new"), sem("a_ps"), sem("a_ev"), sem("tab_out"), sem("post")
        act_req, act_ans = sem("act_req"), sem("act_ans")
        node_done, acc_zero = sem("node_done"), sem("acc_zero")
        idx_in = sems("idx_in", RING)
        kv_in = [sems(f"kv_in{k}_", NG) for k in range(RING)]
        slot_free = [sems(f"slot_free{k}_", NG) for k in range(RING)]
        oh_made, oh_turned, oh_copied, q_spread = sem("oh_made"), sem("oh_turned"), sem("oh_copied"), sem("q_spread")
        spread_used, alpha_done, alpha_turned = sem("spread_used"), sem("alpha_done"), sem("alpha_turned")
        rcol_done, fwd_one, bwd_one = sem("rcol_done"), sem("fwd_one"), sem("bwd_one")
        rows_turned, rows_copied, carry_set = sem("rows_turned"), sem("rows_copied"), sem("carry_set")
        carries_packed = sem("carries_packed")
        f_done, b_done, cols_turned, cols_copied = sem("f_done"), sem("b_done"), sem("cols_turned"), sem("cols_copied")
        gap_done, shift_done, shift_spread, scale_done = sem("gap_done"), sem("shift_done"), sem("shift_spread"), sem("scale_done")
        fwd_two, bwd_two, max_done, arg_done = sem("fwd_two"), sem("bwd_two"), sem("max_done"), sem("arg_done")
        ex_done, ex_turned, w_done = sem("ex_done"), sem("ex_turned"), sem("w_done")
        acc_scaled, acc_done = sem("acc_scaled"), sem("acc_done")
        len_in, sq_done, rbf_done = sems("len_in", 2), sem("sq_done"), sem("rbf_done")
        silu_done, one_set = sem("silu_done"), sem("one_set")
        tab_free, out_free = sem("tab_free"), sem("out_free")
        out_ready, out_sent = sem("out_ready"), sem("out_sent")

        counted = [a_ev, a_ps, acc_done, acc_scaled, acc_zero, act_ans, act_req,
                   alpha_done, alpha_turned, arg_done, b_done, bwd_one, bwd_two, carries_packed,
                   carry_set, cols_copied, cols_turned, ex_done, ex_turned, f_done, ffn_act,
                   ffn_ps, fwd_one, fwd_two, gap_done, h_new, m_ev, m_ps,
                   max_done, node_done, oh_copied, oh_made, oh_turned, one_set, out_free,
                   out_ready, post, q_spread, rbf_done, rcol_done, rows_copied, rows_turned,
                   scale_done, shift_done, shift_spread, silu_done, spread_used, sq_done, t_in,
                   t_out, t_ps, tab_free, w_done,
                   *[s for ring in slot_free for s in ring]]
        LN_A, LN_B = NI + 2 * NI * L, NI + 2 * NI * L + 2 * NI
        N_CONST = 14

        def bc(ap, n):
            return ap.unsqueeze(1).to_broadcast([ap.shape[0], n, ap.shape[1]])

        def bcl(ap, n):
            return ap.unsqueeze(len(ap.shape)).to_broadcast([*ap.shape, n])

        def loaded(c, engine):
            _, values = nc.values_load_multi_w_load_instructions(
                super_blk[0:1, bass.ds(c * (CH // 2), CH // 2)], [engine], min_val=0, max_val=NB - 1,
                skip_runtime_bounds_check_because="setup takes the minimum of every place's block and NB - 1, and counts from 0")
            return values

        block = ctx.enter_context(nc.Block())

        @block.sync
        def _(sp):
            sp.dma_start(su_i, a["dst_t"].rearrange("t e -> (t e)").rearrange("(p t) -> p t", p=P)).then_inc(ld_dst, 16)
            for dst, name in ((ident[:, :], "ident"), (iota[:, :], "iota"), (place[:, :, :], "place"),
                              (centers[:, :], "centers"), (w_i[:, :], "w_i"), (w_o[:, :], "w_o"),
                              (m_1[:, :], "m_1"), (m_1c[:, :], "m_1c"), (m_2[:, :], "m_2"),
                              (u_1[:, :], "u_1"), (u_2[:, :], "u_2")):
                sp.dma_start(dst, a[name]).then_inc(ld_const, 16)
            sp.dma_start(vec1[:, :], a["vec1"].to_broadcast([P, VEC1_W])).then_inc(ld_const, 16)
            sp.dma_start(xn[:, :, :], a["x"].rearrange("(b p) k -> p b k", p=P)).then_inc(ld_const, 16)
            sp.wait_ge(su_rows, 16 * 3 * VC)
            sp.dma_start(flat_len.rearrange("(c p e) -> p c e", p=P, e=P), rows_l).then_inc(su_len, 16)
            sp.wait_ge(su_flat, 1)
            sp.dma_start(flat_dst[1:1 + VC * P * P].rearrange("(c p e) -> p c e", p=P, e=P), r_dst).then_inc(su_dstd, 16)
            sp.dma_start(flat_dst[0:1].rearrange("(a b) -> a b", a=1), edge_word[:, 0:1]).then_inc(su_dstd, 16)
            sp.dma_start(flat_blk.rearrange("(c p) -> p c", p=P), vti[:, 1, :], allow_slow_non_contiguous=True).then_inc(su_dstd, 16)
            sp.wait_ge(su_dstd, 48)
            sp.dma_start(r_prev, flat_dst[0:VC * P * P].rearrange("(c p e) -> p c e", p=P, e=P)).then_inc(su_prev, 16)
            sp.dma_start(blk[:, :], flat_blk.rearrange("(a b) -> a b", a=1)).then_inc(su_prev, 16)
            sp.wait_ge(su_rst, 1)
            sp.dma_start(flat_rst[0:VC * P * P].rearrange("(c p e) -> p c e", p=P, e=P), r_bf[:, :, :]).then_inc(su_rstd, 16)
            sp.dma_start(flat_rst[VC * P * P:VC * P * P + 1].rearrange("(a b) -> a b", a=1), edge_bf[:, 0:1]).then_inc(su_rstd, 16)
            sp.wait_ge(su_rstd, 32)
            for k in range(HEADS):
                for dst, off in ((rst, 0), (rst_r, 1)):
                    sp.dma_start(dst[k * CH:(k + 1) * CH, :, :],
                                 flat_rst[off:off + V * P].rearrange("(c t e) -> t c e", t=CH, e=P)).then_inc(su_tabs, 16)

            def stage_indices(k, l, i):
                c = RING * i + k
                sp.wait_ge(spread_used, START + NG * (l * CHUNKS + c - RING + 1))
                sp.dma_start(idx[:, k, :], src_e[:, bass.ds(c * CH, CH)]).then_inc(idx_in[k], 16)

            sp.wait_ge(su_done, VC * 2)
            with sp.Fori(0, L) as l:
                sp.wait_ge(h_new, START + NI * (l + 1))
                for dst, name in ((w_qs, "w_qs"), (w_kv, "w_kv"), (w_1, "w_1"), (b_1, "b_1")):
                    sp.dma_start(dst[:, :], a[name][bass.ds(l * P, P), :]).then_inc(ld_layer, 16)
                sp.dma_start(w_2[:, :, :].rearrange("p a b -> p (a b)"), a["w_2"][bass.ds(l * P, P), :]).then_inc(ld_layer, 16)
                sp.dma_start(vec0[:, :], a["vec0"][bass.ds(l, 1), :].to_broadcast([P, VEC0_W])).then_inc(ld_layer, 16)
                with sp.Fori(0, NI) as i:
                    sp.wait_ge(a_ev, START + 2 * BW * (l * NI + i + 1))
                    sp.dma_start(kv_table[bass.ds(i * BW * P, BW * P), :].rearrange("(b p) k -> p b k", p=P),
                                 kvst).then_inc(tab_out, 16)
                    sp.wait_ge(tab_out, 16 * (l * NI + i + 1))
                    sp.sem_inc(tab_free, 1)
                with sp.Fori(0, TURNS) as i:
                    for k in range(RING):
                        stage_indices(k, l, i)
            with sp.Fori(0, NI) as i:
                sp.wait_ge(a_ev, START + 2 * BW * (L * NI + i + 1))
                sp.dma_start(src_table[bass.ds(i * BW * P, BW * P), :].rearrange("(b p) k -> p b k", p=P),
                             kvst[:, :, 0:HID]).then_inc(tab_out, 16)
                sp.wait_ge(tab_out, 16 * (L * NI + i + 1))
                sp.sem_inc(tab_free, 1)
            with sp.Fori(0, TURNS) as i:
                for k in range(RING):
                    stage_indices(k, L, i)
            with sp.Fori(0, NI - 1) as i:
                sp.wait_ge(out_ready, START + i + 1)
                sp.dma_start(out[bass.ds(i * BW * P, BW * P), :].rearrange("(b p) k -> p b k", p=P),
                             dx[:, :, 0:64]).then_inc(out_sent, 16)
                sp.wait_ge(out_sent, 16 * (i + 1))
                sp.sem_inc(out_free, 1)
            sp.wait_ge(out_ready, START + NI)
            full = (N // P) % BW
            lo = (NI - 1) * BW * P
            sp.dma_start(out[lo:lo + full * P, :].rearrange("(b p) k -> p b k", p=P), dx[:, 0:full, 0:64]).then_inc(out_sent, 16)
            sp.dma_start(out[lo + full * P:N, :], dx[0:N - lo - full * P, full, 0:64]).then_inc(out_sent, 16)
            sp.wait_ge(out_sent, 16 * (NI + 1))

        @block.gpsimd
        def _(pool):
            for s in counted:
                pool.sem_inc(s, START)
            pool.wait_ge(su_idx, 1)
            for c in range(VC):
                for dst, name in ((rows_i, "src_t"), (rows_d, "dst_t"), (rows_l, "len_t")):
                    pool.indirect_dma_start(dst[:, c, :], None, a[name],
                                            bass.IndirectOffsetOnAxis(ap=vti[:, 0, c:c + 1], axis=0)).then_inc(su_rows, 16)
            uses = [[pool.alloc_register(f"uses{k}_{j}") for j in range(NG)] for k in range(RING)]
            for k in range(RING):
                for j in range(NG):
                    pool.reg_mov(uses[k][j], 0)

            def gather_chunk(k, turn, l, table, width):
                used = [pool.snap(uses[k][j]) for j in range(NG)]
                pool.wait_ge(tab_out, 16 * NI * (l + 1))
                pool.wait_ge(acc_zero, START + l + 1)
                pool.wait_ge(idx_in[k], 16 * (turn + 1))
                for j in range(NG):
                    pool.wait_ge(slot_free[k][j], START + used[j])
                    pool.reg_add(uses[k][j], uses[k][j], 1)
                    for t in range(j * G, (j + 1) * G):
                        pool.indirect_dma_start(slots[:, k, t, 0:width], None, table,
                                                bass.IndirectOffsetOnAxis(ap=idx[:, k, t:t + 1], axis=0))\
                            .then_inc(kv_in[k][j], 16)

            with pool.Fori(0, L) as l:
                with pool.Fori(0, TURNS) as i:
                    for k in range(RING):
                        gather_chunk(k, l * TURNS + i, l, kv_table, KVW)
            with pool.Fori(0, TURNS) as i:
                for k in range(RING):
                    gather_chunk(k, L * TURNS + i, L, src_table, HID)

        @block.scalar
        def _(act):
            def turned(n):
                act.wait_ge(t_ps, START + n + 1)
                act.copy(hT[:, 0:4 * P], bank[0][:, :]).then_inc(t_out, 1)
                act.copy(hT[:, 4 * P:BW * P], bank[1][:, 0:P]).then_inc(t_out, 1)

            def copy_onehots(g, j):
                act.wait_ge(oh_turned, START + NG * g + j + 1)
                act.wait_ge(q_spread, START + NG * g + max(j - 1, 0))
                act.copy(ohT[:, j % 2, :, :].rearrange("p a b -> p (a b)"), bank[j % 2][:, :]).then_inc(oh_copied, 1)

            def attend_step(l, i, k, ahead):
                g = l * CHUNKS + RING * i + k
                act.wait_ge(rows_turned, START + g + 1)
                act.wait_ge(f_done, START + g)
                act.wait_ge(gap_done, START + g)
                act.copy(f_in[:, :, :, 1:CH + 1], bank[5][0:1, 0:2 * P].rearrange("p (a h t) -> p a h t", a=2, t=CH))\
                    .then_inc(rows_copied, 1)
                act.wait_ge(b_done, START + g)
                act.copy(b_in[:, :, :, 0:CH], bank[5][0:1, 2 * P:4 * P].rearrange("p (a h t) -> p a h t", a=2, t=CH))\
                    .then_inc(rows_copied, 1)
                if ahead:
                    copy_onehots(g + 1, 0)
                    copy_onehots(g + 1, 1)
                act.wait_ge(cols_turned, START + g + 1)
                act.wait_ge(bwd_two, START + g)
                act.copy(icol[:, :], bank[5][:, 0:2]).then_inc(cols_copied, 1)
                act.wait_ge(shift_spread, START + g + 1)
                act.wait_ge(acc_scaled, START + g)
                act.activation(scale[:, :], bank[5][:, 8:16], ACT.Exp, scale=0.25).then_inc(scale_done, 1)
                act.wait_ge(arg_done, START + g + 1)
                act.wait_ge(ex_turned, START + g)
                act.activation(ex[:, :], bwd[:, :], ACT.Exp, scale=0.25).then_inc(ex_done, 1)
                if ahead:
                    copy_onehots(g + 1, 2)
                    copy_onehots(g + 1, 3)

            def load_lengths(c, k):
                act.wait_ge(q_spread, START + NG * (L * CHUNKS + c - 1))
                act.dma_start(rbf[:, k % 2, :],
                              flat_len[bass.ds(c * CH * P, CH * P)].rearrange("(a b) -> a b", a=1)
                              .to_broadcast([NBASIS, CH * P])).then_inc(len_in[k % 2], 16)

            def message_front(nth, c, k, ahead):
                g = L * CHUNKS + c
                act.wait_ge(len_in[k % 2], 16 * nth)
                act.activation(rbf[:, k % 2, :], rbf[:, k % 2, :], ACT.Square, bias=centers[:, 0:1]).then_inc(sq_done, 1)
                act.wait_ge(sq_done, START + c + 1)
                act.activation(rbf[:, k % 2, :], rbf[:, k % 2, :], ACT.Exp, scale=RBF_SCALE).then_inc(rbf_done, 1)
                if ahead:
                    load_lengths(c + 1, k + 1)
                for j in range(NG):
                    copy_onehots(g, j)
                    if j >= 1:
                        silu(g, k, j - 1)
                silu(g, k, NG - 1)

            def silu(g, k, j):
                act.wait_ge(spread_used, START + NG * g + j + 1)
                s = slots[:, k, j * G:(j + 1) * G, HID:2 * HID]
                act.activation(s, s, ACT.Silu).then_inc(silu_done, 1)

            act.wait_ge(ld_const, 16 * 13)
            with act.Fori(0, NI) as i:
                turned(i)
                act.wait_ge(post, START + i + 1)
                act.activation(h[:, bass.ds(i * BW, BW), :], t1, ACT.Gelu).then_inc(h_new, 1)
            with act.Fori(0, L) as l:
                act.wait_ge(h_new, START + NI * (l + 1))
                with act.Fori(0, NI) as i:
                    n = NI + 2 * NI * l + i
                    act.wait_ge(t_ps, START + n)
                    act.copy(tsrc, h[:, bass.ds(i * BW, BW), :]).then_inc(t_in, 1)
                    turned(n)
                for j in range(NG):
                    copy_onehots(l * CHUNKS, j)
                with act.Fori(0, TURNS - 1) as i:
                    for k in range(RING):
                        attend_step(l, i, k, True)
                for k in range(RING):
                    attend_step(l, TURNS - 1, k, k < RING - 1)
                with act.Fori(0, NI) as i:
                    act.wait_ge(act_req, START + 2 * (l * NI + i) + 1)
                    act.activation(st[1][:, :], st[0][:, :], ACT.Sigmoid).then_inc(act_ans, 1)
                    act.wait_ge(act_req, START + 2 * (l * NI + i) + 2)
                    act.activation(st[4][:, :], st[3][:, :], ACT.Sqrt).then_inc(act_ans, 1)
                    turned(NI + 2 * NI * l + NI + i)
                    for f in range(4):
                        for s in range(2):
                            act.wait_ge(ffn_ps, START + 8 * (l * NI + i) + 2 * f + s + 1)
                            act.activation(g1[:, f, s * 320:(s + 1) * 320], bank[2 + (2 * f + s) % 4][:, 0:320], ACT.Gelu,
                                           bias=b_1[:, f:f + 1]).then_inc(ffn_act, 1)
            act.wait_ge(h_new, START + NI * (L + 1))
            with act.Fori(0, NI) as i:
                act.wait_ge(t_ps, START + LN_A + 2 * i)
                act.copy(tsrc, h[:, bass.ds(i * BW, BW), :]).then_inc(t_in, 1)
                turned(LN_A + 2 * i)
                act.wait_ge(act_req, START + 2 * L * NI + i + 1)
                act.activation(st[4][:, :], st[3][:, :], ACT.Sqrt).then_inc(act_ans, 1)
                turned(LN_A + 2 * i + 1)
            load_lengths(0, 0)
            with act.Fori(0, TURNS - 1) as i:
                for k in range(RING):
                    message_front(RING // 2 * i + k // 2 + 1, RING * i + k, k, True)
            for k in range(RING):
                message_front(RING // 2 * (TURNS - 1) + k // 2 + 1, RING * (TURNS - 1) + k, k, k < RING - 1)
            with act.Fori(0, NI) as i:
                turned(LN_B + 3 * i)
                turned(LN_B + 3 * i + 1)
                act.wait_ge(act_req, START + 2 * L * NI + NI + 3 * i + 1)
                act.wait_ge(t_ps, START + LN_B + 3 * i + 2)
                act.activation(tsrc[:, :, 0:64], t1[:, :, 0:64], ACT.Silu).then_inc(t_in, 1)
                turned(LN_B + 3 * i + 2)
                for k in range(2):
                    act.wait_ge(act_req, START + 2 * L * NI + NI + 3 * i + 2 + k)
                    act.activation(st[4][:, :], st[3][:, :], ACT.Sqrt).then_inc(act_ans, 1)

        @block.tensor
        def _(pe):
            def turn_blocks(n):
                pe.wait_ge(t_in, START + n + 1)
                pe.wait_ge(t_out, START + 2 * n)
                for b in range(BW):
                    mm = pe.transpose(bank[b // 4][:, (b % 4) * P:(b % 4 + 1) * P], tsrc[:, b, :], ident[:, :])
                mm.then_inc(t_ps, 1)

            def times(n, m, weights, width, K=P):
                pe.wait_ge(t_out, START + 2 * n + 2)
                pe.wait_ge(m_ev, START + m)
                for b in range(BW):
                    mm = pe.matmul(bank[2 + b // 4][:, (b % 4) * P:(b % 4) * P + width], hT[0:K, b * P:(b + 1) * P], weights,
                                   start=True, stop=True)
                mm.then_inc(m_ps, 1)

            def turn(g, k, j):
                pe.wait_ge(oh_made, START + 2 * g + j // 2 + 1)
                pe.wait_ge(oh_copied, START + NG * g + max(j - 1, 0))
                for t in range(G):
                    mm = pe.transpose(bank[j % 2][:, t * P:(t + 1) * P], oh[:, k % 2, j * G + t, :], ident[:, :])
                mm.then_inc(oh_turned, 1)

            def rows(g, k, j, blocks, basis=None):
                pe.wait_ge(oh_copied, START + NG * g + j + 1)
                pe.wait_ge(spread_used, START + NG * g + max(j - 1, 0))
                for t in range(G):
                    o = bank[2 + j % 2][:, t * P:(t + 1) * P]
                    mm = pe.matmul(o, ohT[:, j % 2, t, :], qs[:, blocks[(j * G + t) // 2], 0:HID],
                                   start=True, stop=basis is None)
                    if basis is not None:
                        mm = pe.matmul(o, rbf[:, k % 2, (j * G + t) * P:(j * G + t + 1) * P], m_1c[:, :],
                                       start=False, stop=True)
                mm.then_inc(q_spread, 1)

            def add_up(g, k, j, width, done, base):
                pe.wait_ge(done, START + NG * base + j + 1)
                pe.wait_ge(acc_done, START + (CH // 2) * g + max(2 * j - 2, 0))
                for t in range(j * G, (j + 1) * G):
                    o = (t % G) // 2 * HEADS * VW
                    mm = pe.matmul(bank[6 + j % 2][:, o:o + width], oh[:, k % 2, t, :], slots[:, k, t, HID:HID + width],
                                   start=(t % 2 == 0), stop=(t % 2 == 1))
                mm.then_inc(slot_free[k][j], 1)

            def block_numbers(c):
                return loaded(c, mybir.EngineType.PE)

            def turn_alpha(g):
                pe.wait_ge(alpha_done, START + NG * g + NG)
                pe.wait_ge(w_done, START + NG * g)
                pe.transpose(bank[4][:, 0:P], alpha[:, :, :].rearrange("p h t -> p (h t)"), ident[:, :])\
                    .then_inc(alpha_turned, 1)

            def attend_step(l, i, k, ahead):
                c = RING * i + k
                g = l * CHUNKS + c
                n, kn = g + 1, (k + 1) % RING
                pe.wait_ge(fwd_one, START + g + 1)
                pe.wait_ge(bwd_one, START + g + 1)
                pe.wait_ge(scale_done, START + g)
                for m, col in enumerate((fwd[:, P - 1:P], rcol[:, 0:1], bwd[:, 0:1], rcol[:, 1:2])):
                    mm = pe.transpose(bank[5][0:1, m * P:(m + 1) * P], col, ident[:, :])
                mm.then_inc(rows_turned, 1)
                if ahead:
                    blocks = block_numbers(c + 1)
                    turn(n, kn, 0)
                    turn(n, kn, 1)
                pe.wait_ge(carries_packed, START + 2 * g + 2)
                pe.wait_ge(rows_copied, START + 2 * g + 2)
                pe.matmul(bank[5][:, 0:1], c_row[:, 0, :], ones[0:1, 0:1], start=True, stop=True)
                pe.matmul(bank[5][:, 1:2], c_row[:, 1, :], ones[0:1, 0:1], start=True, stop=True)\
                    .then_inc(cols_turned, 1)
                if ahead:
                    rows(n, kn, 0, blocks)
                pe.wait_ge(shift_done, START + g + 1)
                pe.wait_ge(cols_copied, START + g + 1)
                pe.matmul(bank[5][:, 8:16], oh[:, k % 2, 0, :], shift[:, :], start=True, stop=True)\
                    .then_inc(shift_spread, 1)
                if ahead:
                    turn(n, kn, 2)
                    rows(n, kn, 1, blocks)
                pe.wait_ge(ex_done, START + g + 1)
                pe.transpose(bank[4][:, P:2 * P], ex[:, :], ident[:, :]).then_inc(ex_turned, 1)
                if ahead:
                    turn(n, kn, 3)
                    rows(n, kn, 2, blocks)
                add_up(g, k, 0, HEADS * VW, w_done, g)
                add_up(g, k, 1, HEADS * VW, w_done, g)
                if ahead:
                    rows(n, kn, 3, blocks)
                add_up(g, k, 2, HEADS * VW, w_done, g)
                add_up(g, k, 3, HEADS * VW, w_done, g)
                if ahead:
                    turn_alpha(n)

            def front(g, k, blocks, basis=None):
                turn(g, k, 0)
                turn(g, k, 1)
                for j in range(NG):
                    rows(g, k, j, blocks, basis)
                    if j + 2 < NG:
                        turn(g, k, j + 2)

            def message_step(i, k, ahead):
                c = RING * i + k
                g = L * CHUNKS + c
                n, kn = g + 1, (k + 1) % RING
                if ahead:
                    blocks = block_numbers(c + 1)
                    turn(n, kn, 0)
                    turn(n, kn, 1)
                    pe.wait_ge(rbf_done, START + c + 2)
                for j in range(NG):
                    add_up(g, k, j, HID + 1, silu_done, c)
                    if ahead:
                        rows(n, kn, j, blocks, c)
                        if j + 2 < NG:
                            turn(n, kn, j + 2)

            pe.wait_ge(su_count, 1)
            pe.matmul(bank[7][:, 0:NB + 1], ones[:, :], row[:, 0, :], start=True, stop=True).then_inc(su_count, 1)
            pe.wait_ge(ld_const, 16 * 13)
            pe.wait_ge(su_turn, 1)
            for n, rows_x in enumerate([r_src, r_rel]):
                for c in range(VC):
                    k = n * VC + c
                    if k >= 2:
                        pe.wait_ge(su_taken, k - 1)
                    pe.transpose(bank[4 + k % 2][:, 0:P], rows_x[:, c, :], ident[:, :]).then_inc(su_turned, 1)
            with pe.Fori(0, NI) as i:
                turn_blocks(i)
                times(i, i, w_i[:, :], HID, 64)
            pe.wait_ge(su_prev, 32)
            with pe.Fori(0, L) as l:
                with pe.Fori(0, NI) as i:
                    n = NI + 2 * NI * l + i
                    turn_blocks(n)
                    pe.wait_ge(ld_layer, 96 * (l + 1))
                    pe.wait_ge(t_out, START + 2 * n + 2)
                    for b in range(BW):
                        pe.wait_ge(a_ev, START + 2 * BW * (l * NI + i) + max(2 * b - 2, 0))
                        pe.matmul(bank[2 + b % 2][:, 0:QS], hT[:, b * P:(b + 1) * P], w_qs[:, :], start=True, stop=True)\
                            .then_inc(a_ps, 1)
                        pe.matmul(bank[4 + b % 2][:, 0:BAND], hT[:, b * P:(b + 1) * P], w_kv[:, :], start=True, stop=True)\
                            .then_inc(a_ps, 1)
                front(l * CHUNKS, 0, block_numbers(0))
                turn_alpha(l * CHUNKS)
                with pe.Fori(0, TURNS - 1) as i:
                    for k in range(RING):
                        attend_step(l, i, k, True)
                for k in range(RING):
                    attend_step(l, TURNS - 1, k, k < RING - 1)
                with pe.Fori(0, NI) as i:
                    n = NI + 2 * NI * l + NI + i
                    r = l * NI + i
                    turn_blocks(n)
                    pe.wait_ge(t_out, START + 2 * n + 2)
                    for f in range(4):
                        for s in range(2):
                            k = 2 * f + s
                            pe.wait_ge(ffn_act, START + 8 * r + max(k - 3, 0))
                            pe.matmul(bank[2 + k % 4][:, 0:320], w_1[:, f * HID:(f + 1) * HID], hT[:, s * 320:(s + 1) * 320],
                                      start=True, stop=True).then_inc(ffn_ps, 1)
                    pe.wait_ge(ffn_act, START + 8 * r + 8)
                    pe.wait_ge(m_ev, START + NI + r)
                    for b in range(BW):
                        for f in range(4):
                            mm = pe.matmul(bank[6 + b // 4][:, (b % 4) * P:(b % 4 + 1) * P], g1[:, f, b * P:(b + 1) * P],
                                           w_2[:, f, :], start=(f == 0), stop=(f == 3))
                    mm.then_inc(m_ps, 1)
            M0 = NI + NI * L
            with pe.Fori(0, NI) as i:
                turn_blocks(LN_A + 2 * i)
                times(LN_A + 2 * i, M0 + i, w_o[:, :], 64)
                turn_blocks(LN_A + 2 * i + 1)
                pe.wait_ge(t_out, START + 2 * (LN_A + 2 * i + 1) + 2)
                for b in range(BW):
                    pe.wait_ge(a_ev, START + 2 * BW * (L * NI + i) + max(2 * b - 2, 0))
                    pe.matmul(bank[4 + b % 2][:, 0:2 * HID], hT[0:64, b * P:(b + 1) * P], m_1[:, :], start=True, stop=True)\
                        .then_inc(a_ps, 1)
            blocks = block_numbers(0)
            pe.wait_ge(rbf_done, START + 1)
            front(L * CHUNKS, 0, blocks, 0)
            with pe.Fori(0, TURNS - 1) as i:
                for k in range(RING):
                    message_step(i, k, True)
            for k in range(RING):
                message_step(TURNS - 1, k, k < RING - 1)
            with pe.Fori(0, NI) as i:
                for k, (weights, width) in enumerate(((m_2, P), (u_1, P), (u_2, 64))):
                    turn_blocks(LN_B + 3 * i + k)
                    times(LN_B + 3 * i + k, M0 + NI + 3 * i + k, weights[:, :], 64, width)

        @block.vector
        def _(dve):
            class Steps:
                def __init__(self, s, base=0):
                    self.s, self.base, self.n = s, base, 0

                def __call__(self, ins):
                    self.n += 1
                    ins.then_inc(self.s, 1)
                    dve.wait_ge(self.s, self.base + self.n)

            step = Steps(su_step, 0)
            dve.memset(ones[:, :], 1.0)
            dve.memset(row[:, :, :], 0.0)
            dve.memset(shift[:, :], 0.0)
            dve.memset(f_in[:, :, :, :], -BIG)
            dve.memset(b_in[:, :, :, :], -BIG)
            dve.memset(edge_word[:, :], -5.0)
            step(dve.memset(edge_bf[:, :], -BIG))
            dve.wait_ge(ld_dst, 16)
            step(dve.tensor_copy(su_f, su_i))
            for b in range(1, NB + 1):
                step(dve.tensor_scalar(su_o, su_f, float(b * P), None, ALU.is_lt, ALU.add, accum_out=row[:, 0, b:b + 1]))
            dve.memset(vt[:, 0, :], 0.0).then_inc(su_count, 1)
            dve.wait_ge(su_count, 2)
            rp = row[:, 1, :]
            step(dve.tensor_copy(rp, bank[7][:, 0:NB + 1]))
            step(dve.tensor_copy(rowi[:, 0, :], rp))
            step(dve.tensor_scalar(rowi[:, 1, :], rowi[:, 0, :], 7, None, ALU.arith_shift_right))
            step(dve.tensor_copy(row[:, 2, :], rowi[:, 1, :]))
            step(dve.tensor_scalar(row[:, 3, :], rp, float(P - 1), None, ALU.add))
            step(dve.tensor_copy(rowi[:, 0, :], row[:, 3, :]))
            step(dve.tensor_scalar(rowi[:, 1, :], rowi[:, 0, :], 7, None, ALU.arith_shift_right))
            step(dve.tensor_copy(row[:, 4, :], rowi[:, 1, :]))
            step(dve.tensor_tensor(row[:, 5, 0:NB], row[:, 4, 1:NB + 1], row[:, 2, 0:NB], ALU.subtract))
            step(dve.tensor_scalar(row[:, 3, 0:NB], row[:, 5, 0:NB], 1.0, None, ALU.add))
            step(dve.tensor_copy(rowi[:, 0, :], row[:, 3, :]))
            step(dve.tensor_scalar(rowi[:, 1, :], rowi[:, 0, :], 1, None, ALU.arith_shift_right))
            step(dve.tensor_copy(row[:, 6, 0:NB], rowi[:, 1, 0:NB]))
            step(dve.tensor_tensor_scan(row[:, 7, 0:NB], ones[:, 0:NB], row[:, 6, 0:NB], 0.0, op0=ALU.mult, op1=ALU.add))
            step(dve.tensor_tensor(row[:, 8, 0:NB], row[:, 7, 0:NB], row[:, 6, 0:NB], ALU.subtract))
            step(dve.scalar_tensor_tensor(out=row[:, 9, 0:NB], in0=row[:, 8, 0:NB], scalar=-2.0, in1=row[:, 2, 0:NB],
                                          op0=ALU.mult, op1=ALU.add))
            step(dve.tensor_tensor(row[:, 10, 0:NB - 1], row[:, 9, 1:NB], row[:, 9, 0:NB - 1], ALU.subtract))
            dve.wait_ge(ld_const, 16 * 13)
            for c in range(VC):
                for k, w in ((0, ones[:, 0:NB]), (1, row[:, 10, 0:NB])):
                    step(dve.scalar_tensor_tensor(out=row[:, 11, 0:NB], in0=row[:, 7, 0:NB], scalar=place[:, 1, c:c + 1], in1=w,
                                                  op0=ALU.is_le, op1=ALU.mult, accum_out=vt[:, k, c:c + 1]))
            step(dve.tensor_tensor(vt[:, 2, :], vt[:, 1, :], place[:, 0, :], ALU.add))
            step(dve.tensor_scalar(vt[:, 2, :], vt[:, 2, :], float(TILES - 1), None, ALU.min))
            step(dve.tensor_scalar(vt[:, 3, :], vt[:, 0, :], float(NB - 1), None, ALU.min))
            step(dve.tensor_copy(vti[:, 1, :], vt[:, 3, :]))
            dve.tensor_copy(vti[:, 0, :], vt[:, 2, :]).then_inc(su_idx, 1)
            step(dve.tensor_scalar(vt[:, 1, :], vt[:, 0, :], float(P), None, ALU.mult))
            dve.wait_ge(su_rows, 16 * 3 * VC)
            step(dve.tensor_copy(rows_f, rows_d))
            for c in range(VC):
                step(dve.tensor_scalar(r_rel[:, c, :], rows_f[:, c, :], vt[:, 1, c:c + 1], None, ALU.subtract))
            step(dve.tensor_scalar(r_ok, r_rel, 0.0, None, ALU.is_ge))
            step(dve.tensor_scalar(r_dst, r_rel, float(P), None, ALU.is_lt))
            step(dve.tensor_tensor(r_ok, r_ok, r_dst, ALU.mult))
            step(dve.scalar_tensor_tensor(out=r_dst, in0=rows_f, scalar=1.0, in1=r_ok, op0=ALU.add, op1=ALU.mult))
            step(dve.tensor_scalar(r_dst, r_dst, -1.0, None, ALU.add))
            dve.tensor_copy(vt[:, 3, 0:1], vt[:, 2, 0:1]).then_inc(su_flat, 1)
            step(dve.tensor_copy(r_src, rows_i))
            dve.tensor_copy(vt[:, 3, 1:2], vt[:, 2, 1:2]).then_inc(su_turn, 1)
            for k in range(2 * VC):
                c = k % VC
                dve.wait_ge(su_turned, k + 1)
                dst = src_e if k < VC else rel_e
                dve.tensor_copy(dst[:, c * P:(c + 1) * P], bank[4 + k % 2][:, 0:P]).then_inc(su_taken, 1)
                dve.wait_ge(su_taken, k + 1)
                dve.tensor_copy(vt[:, 3, 2:3], vt[:, 2, 2:3]).then_inc(su_done, 1)
            dve.wait_ge(su_prev, 32)
            step(dve.tensor_tensor(r_dst, r_dst, r_prev, ALU.not_equal))
            step(dve.tensor_scalar(r_bf[:, :, :], r_dst, -BIG, None, ALU.mult))
            dve.tensor_copy(vt[:, 3, 3:4], vt[:, 2, 3:4]).then_inc(su_rst, 1)
            dve.wait_ge(su_tabs, 16 * 2 * HEADS)
            step(dve.tensor_reduce(rst_sum[:, :, 0], rst[:, :, :], axis=X, op=ALU.add))
            step(dve.tensor_copy(rst_b[:, :, :], rst_r[:, :, ::-1]))
            step(dve.tensor_reduce(rst_sum[:, :, 1], rst_b[:, :, :], axis=X, op=ALU.add))
            step(dve.tensor_scalar(cont[:, :], rst[0:1, :, 0], -1.0, None, ALU.is_ge))

            step(dve.tensor_scalar(super_blk[:, :], blk[:, ::2], 0, None, ALU.add))
            step(dve.memset(tsrc, 0.0))
            with dve.Fori(0, NI) as i:
                dve.wait_ge(t_ps, START + i)
                dve.tensor_scalar(tsrc[:, :, 0:64], xn[:, bass.ds(i * BW, BW), :], 0.0, None, ALU.add).then_inc(t_in, 1)
                dve.wait_ge(m_ps, START + i + 1)
                dve.wait_ge(h_new, START + i)
                dve.tensor_tensor(t1[:, 0:4, :], bank[2][:, :].rearrange("p (b k) -> p b k", b=4),
                                  bc(vec1[:, VEC1["bi"]:VEC1["bi"] + P], 4), ALU.add).then_inc(node_done, 1)
                dve.tensor_tensor(t1[:, 4, :], bank[3][:, 0:P], vec1[:, VEC1["bi"]:VEC1["bi"] + P], ALU.add).then_inc(m_ev, 1)
                dve.wait_ge(m_ev, START + i + 1)
                dve.wait_ge(node_done, START + i + 1)
                dve.tensor_copy(st[5][:, :], ones[:, 0:BW]).then_inc(post, 1)

            def norm(step, width, request):
                y, z = t1[:, :, 0:width], t2[:, :, 0:width]
                step(dve.tensor_reduce(st[2][:, :], y, axis=X, op=ALU.add))
                step(dve.tensor_scalar(st[2][:, :], st[2][:, :], 1.0 / width, None, ALU.mult))
                step(dve.tensor_tensor(y, y, bcl(st[2][:, :], width), ALU.subtract))
                step(dve.tensor_tensor(z, y, y, ALU.mult))
                step(dve.tensor_reduce(st[5][:, :], z, axis=X, op=ALU.add))
                dve.tensor_scalar(st[3][:, :], st[5][:, :], 1.0 / width, 1e-5, ALU.mult, ALU.add).then_inc(act_req, 1)
                dve.wait_ge(act_ans, START + request)
                step(dve.reciprocal(st[6][:, :], st[4][:, :]))
                step(dve.tensor_tensor(y, y, bcl(st[6][:, :], width), ALU.mult))

            def onehots(g, k, c, half):
                H = CH // 2
                dve.tensor_tensor(oh[:, k % 2, half * H:(half + 1) * H, :], bc(iota[:, :], H),
                                  bcl(rel_e[:, bass.ds(c * CH + half * H, H)], P), ALU.is_equal).then_inc(oh_made, 1)

            def add_part(g, turn, k, s, blocks, width):
                dve.wait_ge(slot_free[k][s // 2], START + turn + 1)
                dve.wait_ge(acc_done, START + (CH // 2) * g + s)
                a_s, o = acc[:, blocks[s], 0:width], s % 2 * HEADS * VW
                dve.tensor_tensor(a_s, a_s, bank[6 + s // 2 % 2][:, o:o + width], ALU.add).then_inc(acc_done, 1)

            def block_numbers(c):
                return loaded(c, mybir.EngineType.DVE)

            def multiply(g, turn, k, j):
                dve.wait_ge(kv_in[k][j], 16 * G * (turn + 1))
                dve.wait_ge(q_spread, START + NG * g + j + 1)
                keys = slots[:, k, j * G:(j + 1) * G, 0:HID]
                dve.tensor_tensor(keys, keys, bank[2 + j % 2][:, :].rearrange("p (t k) -> p t k", t=G),
                                  ALU.mult).then_inc(spread_used, 1)

            def sum_heads(g, k, j):
                dve.wait_ge(spread_used, START + NG * g + j + 1)
                dve.tensor_reduce(alpha[:, :, j * G:(j + 1) * G].rearrange("p h t -> p t h"),
                                  slots[:, k, j * G:(j + 1) * G, 0:HID].rearrange("p t (h d) -> p t h d", h=HEADS),
                                  axis=X, op=ALU.add).then_inc(alpha_done, 1)

            def attend_step(l, i, k, ahead):
                c = RING * i + k
                turn = l * TURNS + i
                g = l * CHUNKS + c
                n, kn, turn_n = g + 1, (k + 1) % RING, turn + (k + 1) // RING
                dve.wait_ge(rows_turned, START + g)
                dve.tensor_scalar(rcol[:, :], rst_sum[:, c, :], 0.0, None, ALU.add).then_inc(rcol_done, 1)
                dve.wait_ge(alpha_turned, START + g + 1)
                aT = bank[4][:, 0:P]
                R, Rb = rst[:, c, :], rst_b[:, c, :]
                dve.tensor_tensor_scan(fwd[:, :], R, aT, -BIG, op0=ALU.add, op1=ALU.max).then_inc(fwd_one, 1)
                dve.wait_ge(rcol_done, START + g + 1)
                dve.tensor_tensor_scan(bwd[:, ::-1], Rb, aT[:, ::-1], -BIG, op0=ALU.add, op1=ALU.max)\
                    .then_inc(bwd_one, 1)
                dve.tensor_copy(f_in[:, 0, :, 0:1], f_out[:, :, CH:CH + 1]).then_inc(carry_set, 1)
                if ahead:
                    onehots(n, kn, c + 1, 0)
                blocks = block_numbers(c)
                dve.wait_ge(carry_set, START + g + 1)
                dve.wait_ge(rows_copied, START + 2 * g + 1)
                dve.tensor_tensor_scan(f_out[:, :, :].rearrange("p h t -> p (h t)"),
                                       f_in[:, 1, :, :].rearrange("p h t -> p (h t)"),
                                       f_in[:, 0, :, :].rearrange("p h t -> p (h t)"), -BIG, op0=ALU.add, op1=ALU.max)\
                    .then_inc(f_done, 1)
                dve.wait_ge(rows_copied, START + 2 * g + 2)
                dve.tensor_tensor_scan(b_out[:, :, :].rearrange("p h t -> p (h t)")[:, ::-1],
                                       b_in[:, 1, :, :].rearrange("p h t -> p (h t)")[:, ::-1],
                                       b_in[:, 0, :, :].rearrange("p h t -> p (h t)")[:, ::-1], -BIG,
                                       op0=ALU.add, op1=ALU.max).then_inc(b_done, 1)
                dve.wait_ge(f_done, START + g + 1)
                dve.wait_ge(cols_turned, START + g)
                dve.tensor_copy(c_row[:, 0, :].rearrange("p (h t) -> p h t", h=HEADS), f_out[:, :, 0:CH])\
                    .then_inc(carries_packed, 1)
                dve.wait_ge(b_done, START + g + 1)
                dve.tensor_tensor(gap[:, :], f_in[:, 0, :, 0], b_out[:, :, 0], ALU.subtract).then_inc(gap_done, 1)
                dve.tensor_copy(c_row[:, 1, :].rearrange("p (h t) -> p h t", h=HEADS), b_out[:, :, 1:CH + 1])\
                    .then_inc(carries_packed, 1)
                dve.wait_ge(gap_done, START + g + 1)
                dve.wait_ge(shift_spread, START + g)
                dve.tensor_scalar(shift[0:1, :], gap[:, :], 0.0, cont[:, bass.ds(c, 1)], ALU.min, ALU.mult)\
                    .then_inc(shift_done, 1)
                if ahead:
                    onehots(n, kn, c + 1, 1)
                dve.wait_ge(cols_copied, START + g + 1)
                dve.tensor_tensor_scan(fwd[:, :], R, aT, icol[:, 0:1], op0=ALU.add, op1=ALU.max).then_inc(fwd_two, 1)
                dve.wait_ge(bwd_one, START + g + 1)
                dve.tensor_tensor_scan(bwd[:, ::-1], Rb, aT[:, ::-1], icol[:, 1:2], op0=ALU.add, op1=ALU.max)\
                    .then_inc(bwd_two, 1)
                dve.wait_ge(fwd_two, START + g + 1)
                dve.wait_ge(bwd_two, START + g + 1)
                dve.tensor_tensor(fwd[:, :], fwd[:, :], bwd[:, :], ALU.max).then_inc(max_done, 1)
                dve.wait_ge(max_done, START + g + 1)
                dve.tensor_tensor(bwd[:, :], aT, fwd[:, :], ALU.subtract).then_inc(arg_done, 1)
                if ahead:
                    multiply(n, turn_n, kn, 0)
                dve.wait_ge(scale_done, START + g + 1)
                dve.wait_ge(acc_done, START + (CH // 2) * g)
                a_0 = acc[:, blocks[0], :].rearrange("p (h k) -> p h k", h=HEADS)
                dve.tensor_tensor(a_0, a_0, bcl(scale[:, :], VW), ALU.mult).then_inc(acc_scaled, 1)
                if ahead:
                    sum_heads(n, kn, 0)
                dve.wait_ge(ex_turned, START + g + 1)
                exs = bank[4][:, P:2 * P].rearrange("p (h t) -> p t h", h=HEADS)
                for j in range(NG):
                    vals = slots[:, k, j * G:(j + 1) * G, HID:KVW].rearrange("p t (h k) -> p t h k", h=HEADS)
                    dve.tensor_tensor(vals, vals, bcl(exs[:, j * G:(j + 1) * G, :], VW), ALU.mult).then_inc(w_done, 1)
                dve.wait_ge(acc_scaled, START + g + 1)
                for j in range(1, NG):
                    if ahead:
                        multiply(n, turn_n, kn, j)
                    add_part(g, turn, k, 2 * j - 2, blocks, HEADS * VW)
                    if ahead:
                        sum_heads(n, kn, j)
                    add_part(g, turn, k, 2 * j - 1, blocks, HEADS * VW)
                for s in (CH // 2 - 2, CH // 2 - 1):
                    add_part(g, turn, k, s, blocks, HEADS * VW)

            def messages(g, turn, k, j):
                dve.wait_ge(kv_in[k][j], 16 * G * (turn + 1))
                dve.wait_ge(q_spread, START + NG * g + j + 1)
                dve.tensor_tensor(slots[:, k, j * G:(j + 1) * G, HID:2 * HID], slots[:, k, j * G:(j + 1) * G, 0:HID],
                                  bank[2 + j % 2][:, :].rearrange("p (t k) -> p t k", t=G), ALU.add)\
                    .then_inc(spread_used, 1)

            def message_step(i, k, ahead):
                c = RING * i + k
                turn = L * TURNS + i
                g = L * CHUNKS + c
                n, kn, turn_n = g + 1, (k + 1) % RING, turn + (k + 1) // RING
                if ahead:
                    onehots(n, kn, c + 1, 0)
                    onehots(n, kn, c + 1, 1)
                blocks = block_numbers(c)
                for j in range(NG):
                    add_part(g, turn, k, 2 * j, blocks, HID + 1)
                    if ahead:
                        messages(n, turn_n, kn, j)
                    add_part(g, turn, k, 2 * j + 1, blocks, HID + 1)

            with dve.Fori(0, L) as l:
                with dve.Fori(0, NI) as i:
                    ga = l * NI + i
                    dve.wait_ge(ld_layer, 96 * (l + 1))
                    dve.wait_ge(tab_free, START + ga)
                    for b in range(BW):
                        dve.wait_ge(a_ps, START + 2 * BW * ga + 2 * b + 1)
                        dve.tensor_tensor(qs[:, i * BW + b, :], bank[2 + b % 2][:, 0:QS], vec0[:, VEC0["qs"]:VEC0["qs"] + QS],
                                          ALU.add).then_inc(a_ev, 1)
                        dve.wait_ge(a_ps, START + 2 * BW * ga + 2 * b + 2)
                        dve.tensor_tensor(kvst[:, b, :], bank[4 + b % 2][:, 0:BAND], vec0[:, VEC0["kv"]:VEC0["kv"] + BAND],
                                          ALU.add).then_inc(a_ev, 1)
                dve.wait_ge(a_ev, START + 2 * BW * NI * (l + 1))
                dve.memset(f_out[:, :, :], -BIG).then_inc(node_done, 1)
                dve.memset(acc[:, :, :], 0.0).then_inc(acc_zero, 1)
                dve.wait_ge(acc_zero, START + l + 1)
                onehots(l * CHUNKS, 0, 0, 0)
                dve.wait_ge(node_done, START + NI + l + 1)
                onehots(l * CHUNKS, 0, 0, 1)
                for j in range(NG):
                    multiply(l * CHUNKS, l * TURNS, 0, j)
                    sum_heads(l * CHUNKS, 0, j)
                with dve.Fori(0, TURNS - 1) as i:
                    for k in range(RING):
                        attend_step(l, i, k, True)
                for k in range(RING):
                    attend_step(l, TURNS - 1, k, k < RING - 1)
                with dve.Fori(0, NI) as i:
                    r = l * NI + i
                    dve.wait_ge(acc_done, START + (CH // 2) * CHUNKS * (l + 1))
                    K = 25
                    step = Steps(post, START + NI + K * r)
                    bs = bass.ds(i * BW, BW)
                    a5 = acc[:, bs, :].rearrange("p b (h k) -> p b h k", h=HEADS)
                    xr = qs[:, bs, HID:2 * HID]
                    v = lambda name: bc(vec0[:, VEC0[name]:VEC0[name] + P], BW)
                    step(dve.tensor_scalar(den[:, :, :], a5[:, :, :, DH], 1e-16, None, ALU.add))
                    step(dve.reciprocal(rden[:, :, :], den[:, :, :]))
                    for b in range(BW):
                        step(dve.tensor_tensor(o_t[:, b, :].rearrange("p (h k) -> p h k", h=HEADS),
                                               acc[:, i * BW + b, :].rearrange("p (h k) -> p h k", h=HEADS)[:, :, 0:DH],
                                               bcl(rden[:, b, :], DH), ALU.mult))
                    step(dve.tensor_tensor(dx[:, :, :], o_t, xr, ALU.subtract))
                    step(dve.tensor_tensor(t1, o_t, v("w0"), ALU.mult))
                    step(dve.tensor_tensor(t2[:, :, :], xr, v("w1"), ALU.mult))
                    step(dve.tensor_tensor(t1, t1, t2[:, :, :], ALU.add))
                    step(dve.tensor_tensor(t2[:, :, :], dx[:, :, :], v("w2"), ALU.mult))
                    step(dve.tensor_tensor(t1, t1, t2[:, :, :], ALU.add))
                    dve.tensor_reduce(st[0][:, :], t1, axis=X, op=ALU.add).then_inc(act_req, 1)
                    dve.wait_ge(act_ans, START + 2 * r + 1)
                    step(dve.tensor_tensor(t2[:, :, :], dx[:, :, :], bcl(st[1][:, :], P), ALU.mult))
                    step(dve.tensor_tensor(t1, o_t, t2[:, :, :], ALU.subtract))
                    step(dve.tensor_tensor(t1, t1, h[:, bs, :], ALU.add))
                    norm(step, HID, 2 * r + 2)
                    step(dve.tensor_tensor(t1, t1, v("g"), ALU.mult))
                    assert step.n == K - 1 - 0, step.n
                    dve.wait_ge(t_ps, START + NI + 2 * NI * l + NI + i)
                    dve.tensor_tensor(tsrc, t1, v("b"), ALU.add).then_inc(t_in, 1)
                    dve.wait_ge(t_in, START + NI + 2 * NI * l + NI + i + 1)
                    step(dve.tensor_tensor(t2[:, :, :], tsrc, v("b2"), ALU.add))
                    dve.wait_ge(m_ps, START + NI + r + 1)
                    dve.tensor_tensor(h[:, bass.ds(i * BW, 4), :], bank[6][:, :].rearrange("p (b k) -> p b k", b=4), t2[:, 0:4, :],
                                      ALU.add).then_inc(m_ev, 1)
                    dve.tensor_tensor(h[:, i * BW + 4, :], bank[7][:, 0:P], t2[:, 4, :], ALU.add).then_inc(h_new, 1)
                    dve.wait_ge(m_ev, START + NI + r + 1)
                    dve.wait_ge(h_new, START + NI * (l + 1) + i + 1)
            P0 = NI + 25 * NI * L
            v1 = lambda name, w=64: bc(vec1[:, VEC1[name]:VEC1[name] + w], BW)
            with dve.Fori(0, NI) as i:
                bs = bass.ds(i * BW, BW)
                K = 11
                step = Steps(post, START + P0 + K * i)
                y = t1[:, :, 0:64]
                dve.wait_ge(m_ps, START + NI + NI * L + i + 1)
                step(dve.tensor_tensor(t1[:, 0:4, 0:64], bank[2][:, :].rearrange("p (b k) -> p b k", b=4)[:, :, 0:64],
                                       bc(vec1[:, VEC1["bo"]:VEC1["bo"] + 64], 4), ALU.add))
                dve.tensor_tensor(t1[:, 4, 0:64], bank[3][:, 0:64], vec1[:, VEC1["bo"]:VEC1["bo"] + 64], ALU.add).then_inc(m_ev, 1)
                dve.wait_ge(m_ev, START + NI + NI * L + i + 1)
                step(dve.tensor_tensor(y, y, xn[:, bs, :], ALU.add))
                norm(step, 64, 2 * L * NI + i + 1)
                step(dve.tensor_scalar(xn[:, bs, :], y, 0.0, None, ALU.add))
                dve.wait_ge(t_ps, START + LN_A + 2 * i + 1)
                dve.tensor_copy(tsrc[:, :, 0:64], y).then_inc(t_in, 1)
                step(dve.tensor_copy(st[5][:, :], ones[:, 0:BW]))
                assert step.n == K, step.n
                dve.wait_ge(tab_free, START + L * NI + i)
                for b in range(BW):
                    dve.wait_ge(a_ps, START + 2 * BW * L * NI + BW * i + b + 1)
                    dve.tensor_tensor(qs[:, i * BW + b, 0:HID], bank[4 + b % 2][:, HID:2 * HID],
                                      vec1[:, VEC1["mb1"]:VEC1["mb1"] + HID], ALU.add).then_inc(a_ev, 1)
                    dve.tensor_copy(kvst[:, b, 0:HID], bank[4 + b % 2][:, 0:HID]).then_inc(a_ev, 1)
            dve.wait_ge(tab_out, 16 * NI * (L + 1))
            dve.wait_ge(a_ev, START + 2 * BW * NI * (L + 1))
            dve.memset(slots[:, :, :, 2 * HID:2 * HID + 1], 1.0).then_inc(one_set, 1)
            dve.memset(acc[:, :, :], 0.0).then_inc(acc_zero, 1)
            dve.wait_ge(one_set, START + 1)
            dve.wait_ge(acc_zero, START + L + 1)
            onehots(L * CHUNKS, 0, 0, 0)
            onehots(L * CHUNKS, 0, 0, 1)
            for j in range(NG):
                messages(L * CHUNKS, L * TURNS, 0, j)
            with dve.Fori(0, TURNS - 1) as i:
                for k in range(RING):
                    message_step(i, k, True)
            for k in range(RING):
                message_step(TURNS - 1, k, k < RING - 1)
            P1 = P0 + 11 * NI
            dve.wait_ge(acc_done, START + (CH // 2) * CHUNKS * (L + 1))
            with dve.Fori(0, NI) as i:
                bs = bass.ds(i * BW, BW)
                K = 26
                step = Steps(post, START + P1 + K * i)
                M1 = NI + NI * L + NI + 3 * i
                T1 = LN_B + 3 * i
                R1 = 2 * L * NI + NI + 3 * i
                Q1 = 2 * L * NI + NI + 2 * i
                cnt = acc[:, bs, HID]
                step(dve.tensor_scalar(st[0][:, :], cnt, 1.0, None, ALU.max))
                step(dve.reciprocal(st[1][:, :], st[0][:, :]))
                step(dve.tensor_tensor(st[2][:, :], cnt, st[1][:, :], ALU.mult))
                dve.wait_ge(t_ps, START + T1)
                dve.tensor_tensor(tsrc, acc[:, bs, 0:HID], bcl(st[1][:, :], HID), ALU.mult).then_inc(t_in, 1)
                step(dve.tensor_tensor(t2[:, :, 0:64], v1("mb2"), bcl(st[2][:, :], 64), ALU.mult))

                def evac(m, other4, other1, out4, out1):
                    dve.wait_ge(m_ps, START + m + 1)
                    step(dve.tensor_tensor(out4, bank[2][:, :].rearrange("p (b k) -> p b k", b=4)[:, :, 0:64], other4, ALU.add))
                    dve.tensor_tensor(out1, bank[3][:, 0:64], other1, ALU.add).then_inc(m_ev, 1)
                    dve.wait_ge(m_ev, START + m + 1)

                bias = lambda name: (bc(vec1[:, VEC1[name]:VEC1[name] + 64], 4), vec1[:, VEC1[name]:VEC1[name] + 64])
                evac(M1, t2[:, 0:4, 0:64], t2[:, 4, 0:64], t1[:, 0:4, 64:128], t1[:, 4, 64:128])
                step(dve.tensor_scalar(t1[:, :, 0:64], xn[:, bs, :], 0.0, None, ALU.add))
                dve.wait_ge(t_ps, START + T1 + 1)
                dve.tensor_copy(tsrc, t1).then_inc(t_in, 1)
                evac(M1 + 1, *bias("ub1"), t1[:, 0:4, 0:64], t1[:, 4, 0:64])
                step(dve.tensor_copy(st[5][:, :], ones[:, 0:BW]))
                dve.tensor_copy(st[6][:, :], ones[:, 0:BW]).then_inc(act_req, 1)
                evac(M1 + 2, *bias("ub2"), t1[:, 0:4, 0:64], t1[:, 4, 0:64])
                y = t1[:, :, 0:64]
                norm(step, 64, Q1 + 1)
                step(dve.tensor_tensor(y, y, v1("g"), ALU.mult))
                step(dve.tensor_tensor(y, y, v1("b"), ALU.add))
                step(dve.tensor_tensor(y, y, xn[:, bs, :], ALU.add))
                norm(step, 64, Q1 + 2)
                dve.wait_ge(out_free, START + i)
                dve.tensor_copy(dx[:, :, 0:64], y).then_inc(out_ready, 1)
                assert step.n == K, step.n


RBF_WIDTH = (10.0 / (NBASIS - 1)) * 0.5
RBF_SCALE = -1.0 / (2.0 * RBF_WIDTH ** 2)


def lay_out(inp):
    f = {k: np.asarray(v) for k, v in inp.items()}
    z = lambda *s: np.zeros(s, np.float32)
    a = {}
    a["x"] = np.concatenate([f["x"], z(NPAD - N, 64)])
    pad = TILES * P - E
    a["src_t"] = np.concatenate([f["src"], np.zeros(pad, np.int32)]).reshape(TILES, P)
    a["dst_t"] = np.concatenate([f["dst"], np.full(pad, 2 * NPAD, np.int32)]).reshape(TILES, P)
    a["len_t"] = np.concatenate([f["edge_weight1"][:, 0], z(pad)]).reshape(TILES, P)
    n = {k[7:]: v for k, v in f.items() if k.startswith("L0_gnn_")}
    m = {k[7:]: v for k, v in f.items() if k.startswith("L1_gnn_")}
    T = lambda w: w.transpose(0, 2, 1)
    a["w_qs"] = np.concatenate([T(n["Wq"]), T(n["Ws"])], 2).reshape(L * P, QS)
    wide = lambda v, fill: np.concatenate([v.reshape(*v.shape[:-1], HEADS, DH), np.full((*v.shape[:-1], HEADS, 1), fill, np.float32)],
                                          -1).reshape(*v.shape[:-1], HEADS * VW)
    a["w_kv"] = np.concatenate([T(n["Wk"]), wide(T(n["Wv"]), 0.0)], 2).reshape(L * P, BAND)
    a["w_1"] = T(n["W1"]).reshape(L * P, 4 * HID)
    a["b_1"] = n["b1"].reshape(L, 4, HID).transpose(0, 2, 1).reshape(L * P, 4)
    a["w_2"] = T(n["W2"]).reshape(L, 4, HID, HID).transpose(0, 2, 1, 3).reshape(L * P, 4 * HID)
    a["vec0"] = np.concatenate([n["Wbeta"][:, 0, :], n["ln_g"], n["ln_b"], n["b2"], n["bq"], n["bs"], n["bk"], wide(n["bv"], 1.0)], 1)
    a["vec1"] = np.concatenate([n["bi"], n["bo"], m["mb1"], m["mb2"], m["ub1"], m["ub2"], m["ln_g"], m["ln_b"]])[None]
    a["w_i"], a["w_o"] = n["Wi"].T, n["Wo"].T
    a["m_1"] = np.concatenate([m["mw1"][0:64], m["mw1"][64:128]], 1)
    a["m_1c"], a["m_2"], a["u_1"], a["u_2"] = m["mw1"][128:], m["mw2"], m["uw1"], m["uw2"]
    a["ident"] = np.eye(P, dtype=np.float32)
    a["iota"] = np.tile(np.arange(P, dtype=np.float32), (P, 1))
    v = np.arange(VC * P, dtype=np.float32).reshape(VC, P).T
    a["place"] = np.stack([v, np.floor(v / 2)], 1).astype(np.float32)
    a["centers"] = -np.linspace(0.0, 10.0, NBASIS, dtype=np.float32)[:, None]
    return {k: np.ascontiguousarray(v) for k, v in a.items()}


def kernel(**inputs):
    import concourse.bacc as bacc
    from concourse.bass_utils import run_bass_kernel_spmd

    nc = bacc.Bacc("TRN2", target_bir_lowering=False, num_devices=1)
    laid = lay_out(inputs)
    arrays = {f"in_{k}": v for k, v in laid.items()}
    aps = {k: nc.dram_tensor(f"in_{k}", v.shape, mybir.dt.from_np(v.dtype), kind="ExternalInput").ap() for k, v in laid.items()}
    out = nc.dram_tensor("out_0", (N, 64), F32, kind="ExternalOutput").ap()
    build_program(nc, aps, out)
    r = run_bass_kernel_spmd(nc, [arrays], core_ids=[0])
    return r.results[0]["out_0"]
```

```python
from contextlib import ExitStack

import numpy as np

import concourse.bass as bass
from concourse import mybir

F32 = mybir.dt.float32
BF16 = mybir.dt.bfloat16
I32 = mybir.dt.int32
ALU = mybir.AluOpType
ACT = mybir.ActivationFunctionType
X = mybir.AxisListType.X

P = 128
N = 3125
E = 100000
L = 4
HEADS, DH = 8, 16
HID = HEADS * DH
NB = -(-N // P)
NPAD = NB * P
TILES = -(-E // P) + 2
SUPERS = (-(-E // P) + NB - 1 + NB) // 2 + 1
CH = 16
RING = 4
CHUNKS = RING * (-(-2 * SUPERS // (RING * CH)))
V = CHUNKS * CH
VC = -(-V // P)
TURNS = CHUNKS // RING
G = 4
NG = CH // G
VW = DH + 1
KVW = HID + HEADS * VW
BW = 5
NI = NB // BW
BIG = 1.0e30
START = (RING - 1) * NG + 1
NBASIS = 16
STACK = P // NBASIS
QS, BAND = 2 * HID, KVW
VEC0 = {"w0": 0, "w1": 128, "w2": 256, "g": 384, "b": 512, "b2": 640}
VEC0_W = 768
VEC1 = {"bi": 0, "bo": 128, "mb1": 192, "mb2": 320, "ub1": 384, "ub2": 448, "g": 512, "b": 576}
VEC1_W = 640
assert NB % BW == 0 and V >= 2 * SUPERS


def build_program(nc, a, out):
    with ExitStack() as ctx:
        def sb(name, shape, dt=F32):
            return ctx.enter_context(nc.sbuf_tensor(name, shape, dt))

        def sem(name):
            return ctx.enter_context(nc.semaphore(name))

        def sems(name, n):
            return [sem(f"{name}{k}") for k in range(n)]

        bank = [ctx.enter_context(nc.psum_tensor(f"bank{k}", [P, 512], F32)) for k in range(8)]

        kv_table = nc.dram_tensor("kv_table", [NPAD, KVW], F32, kind="Internal").ap()
        src_table = nc.dram_tensor("src_table", [NPAD, HID], F32, kind="Internal").ap()
        flat_dst = nc.dram_tensor("flat_dst", [VC * P * P + P], F32, kind="Internal").ap()
        flat_rst = nc.dram_tensor("flat_rst", [VC * P * P + P], BF16, kind="Internal").ap()
        flat_len = nc.dram_tensor("flat_len", [VC * P * P], F32, kind="Internal").ap()
        flat_blk = nc.dram_tensor("flat_blk", [VC * P], I32, kind="Internal").ap()

        ident = sb("ident", [P, P])
        iota = sb("iota", [P, P])
        eps = sb("eps", [P, 1])
        place = sb("place", [P, 2, VC])
        centers = sb("centers", [P, 1])
        ones = sb("ones", [P, P])
        h = sb("h", [P, NB, HID])
        xn = sb("xn", [P, NB, 64])
        qs = sb("qs", [P, NB, QS])
        acc = sb("acc", [P, NB, HEADS * VW])
        src_e = sb("src_e", [P, VC * P], I32)
        rel_e = sb("rel_e", [P, VC * P])
        super_blk = sb("super_blk", [1, VC * P // 2], I32)
        resets = sb("resets", [P, 2, CHUNKS, P], BF16)
        rst = resets[:, 0, :, :]
        rst_b = resets[:, 1, :, :]
        rst_sum = sb("rst_sum", [P, CHUNKS, 2])
        cont = sb("cont", [1, CHUNKS])
        w_qs = sb("w_qs", [P, QS])
        w_kv = sb("w_kv", [P, BAND])
        w_1 = sb("w_1", [P, 4 * HID])
        b_1 = sb("b_1", [P, 4])
        w_2 = sb("w_2", [P, 4, HID])
        vec0 = sb("vec0", [P, VEC0_W])
        vec_qskv = sb("vec_qskv", [P, QS + KVW])
        vec1 = sb("vec1", [P, VEC1_W])
        w_i = sb("w_i", [64, HID])
        w_o = sb("w_o", [P, 64])
        m_1 = sb("m_1", [64, 2 * HID])
        m_2 = sb("m_2", [P, 64])
        u_1 = sb("u_1", [P, 64])
        u_2 = sb("u_2", [64, 64])
        slots = sb("slots", [P, RING, CH, KVW])
        flat_slots = slots[:, :, :, :].rearrange("p a c k -> p (a c k)")
        idx = sb("idx", [P, RING, CH], I32)
        oh = sb("oh", [P, 2, CH, P])
        ohT = sb("ohT", [P, 2, G, P])
        alpha = sb("alpha", [P, HEADS, CH])
        rcol = sb("rcol", [P, 2])
        fwd = sb("fwd", [P, P])
        bwd = sb("bwd", [P, P])
        ex = sb("ex", [P, P])
        f_in = sb("f_in", [1, 2, HEADS, CH + 1])
        b_in = sb("b_in", [1, 2, HEADS, CH + 1])
        f_out = sb("f_out", [1, HEADS, CH + 1])
        b_out = sb("b_out", [1, HEADS, CH + 1])
        c_row = sb("c_row", [1, 2, P])
        icol = sb("icol", [P, 2])
        gap = sb("gap", [1, HEADS])
        shift = sb("shift", [P, HEADS])
        scale = sb("scale", [P, HEADS])
        late = resets[:, :, :, :].rearrange("p a c e -> p (a c e)").bitcast(F32)
        rbf = late[:, 0:2 * CH // STACK * P].rearrange("p (a j e) -> p a j e", a=2, e=P)
        m_1c = late[:, 2 * CH // STACK * P:2 * CH // STACK * P + STACK * HID].rearrange("p (q k) -> p q k", q=STACK)
        at = [0]

        def node_tile(width):
            s = at[0]
            at[0] += width
            assert at[0] <= RING * CH * KVW
            return flat_slots[:, s:s + width]

        def rows_of(n, width=P):
            return node_tile(n * width).rearrange("p (b k) -> p b k", b=n)

        tsrc = rows_of(BW)
        hT = node_tile(BW * P)
        junk = flat_slots[:, at[0]:at[0] + 2 * NB * P].rearrange("p (b k) -> p b k", k=P)
        kvst = rows_of(NB, KVW)
        t1, t2, dx = rows_of(BW), rows_of(BW), rows_of(BW)
        g1 = node_tile(4 * BW * P).rearrange("p (f k) -> p f k", f=4)
        o_all = rows_of(NB)
        w02, w12 = node_tile(P), node_tile(P)
        den, rden = node_tile(NB * HEADS), node_tile(NB * HEADS)
        logit = rows_of(2, NB)
        beta = node_tile(NB)
        st = [sb(f"st{k}", [P, BW]) for k in range(7)]
        su_f = flat_slots[:, 0:TILES]
        su_i = flat_slots[:, TILES:2 * TILES].bitcast(I32)
        su_o = flat_slots[:, 2 * TILES:3 * TILES]
        row = flat_slots[:, 9000:9000 + 12 * (NB + 1)].rearrange("p (a b) -> p a b", a=12)
        rowi = sb("rowi", [P, 4, NB + 1], I32)
        vt = sb("vt", [P, 4, VC])
        vti = sb("vti", [P, 2, VC], I32)
        rows_i = flat_slots[:, 3000:3000 + VC * P].rearrange("p (c e) -> p c e", c=VC).bitcast(I32)
        rows_d = flat_slots[:, 4000:4000 + VC * P].rearrange("p (c e) -> p c e", c=VC).bitcast(I32)
        rows_l = flat_slots[:, 5000:5000 + VC * P].rearrange("p (c e) -> p c e", c=VC)
        rows_f = flat_slots[:, 6000:6000 + VC * P].rearrange("p (c e) -> p c e", c=VC)
        rst_r = flat_slots[:, 0:CHUNKS * P // 2].bitcast(BF16).rearrange("p (c e) -> p c e", c=CHUNKS)
        oh_f = oh[:, :, :, :].rearrange("p a c k -> p (a c k)")
        r_dst = oh_f[:, 0:VC * P].rearrange("p (c e) -> p c e", c=VC)
        r_rel = oh_f[:, 900:900 + VC * P].rearrange("p (c e) -> p c e", c=VC)
        r_ok = oh_f[:, 1800:1800 + VC * P].rearrange("p (c e) -> p c e", c=VC)
        r_prev = oh_f[:, 2700:2700 + VC * P].rearrange("p (c e) -> p c e", c=VC)
        blk = flat_slots[0:1, 10000:10000 + VC * P].bitcast(I32)
        r_bf = flat_slots[:, 8000:8000 + VC * P // 2].bitcast(BF16).rearrange("p (c e) -> p c e", c=VC)
        r_src = flat_slots[:, 7000:7000 + VC * P].rearrange("p (c e) -> p c e", c=VC)
        edge_word = sb("edge_word", [1, 2])
        edge_bf = sb("edge_bf", [1, 2], BF16)

        ld_const, ld_w1, ld_layer, ld_dst = sem("ld_const"), sem("ld_w1"), sem("ld_layer"), sem("ld_dst")
        su_step, su_count, su_idx, su_rows = sem("su_step"), sem("su_count"), sem("su_idx"), sem("su_rows")
        su_flat, su_prev, su_rst, su_tabs = sem("su_flat"), sem("su_prev"), sem("su_rst"), sem("su_tabs")
        su_turn, su_turned, su_taken, su_done = sem("su_turn"), sem("su_turned"), sem("su_taken"), sem("su_done")
        su_pool, su_len, su_rstd, su_dstd = sem("su_pool"), sem("su_len"), sem("su_rstd"), sem("su_dstd")
        t_in, t_ps, t_out = sem("t_in"), sem("t_ps"), sem("t_out")
        m_ps, m_ev, ffn_ps, ffn_act = sem("m_ps"), sem("m_ev"), sem("ffn_ps"), sem("ffn_act")
        h_new, a_ps, a_ev, tab_out, post = sem("h_new"), sem("a_ps"), sem("a_ev"), sem("tab_out"), sem("post")
        act_req, act_ans = sem("act_req"), sem("act_ans")
        sums_ready, deviations_ready, h_kept = sem("sums_ready"), sem("deviations_ready"), sem("h_kept")
        node_done, acc_zero = sem("node_done"), sem("acc_zero")
        idx_in = sems("idx_in", RING)
        kv_in = [sems(f"kv_in{k}_", NG) for k in range(RING)]
        slot_free = [sems(f"slot_free{k}_", NG) for k in range(RING)]
        oh_made, oh_turned, oh_copied, q_spread = sem("oh_made"), sem("oh_turned"), sem("oh_copied"), sem("q_spread")
        spread_used, alpha_done, alpha_turned = sem("spread_used"), sem("alpha_done"), sem("alpha_turned")
        rcol_done, fwd_one, bwd_one = sem("rcol_done"), sem("fwd_one"), sem("bwd_one")
        rows_turned, rows_copied, carry_set = sem("rows_turned"), sem("rows_copied"), sem("carry_set")
        carries_packed = sem("carries_packed")
        f_done, b_done, cols_turned, cols_copied = sem("f_done"), sem("b_done"), sem("cols_turned"), sem("cols_copied")
        gap_done, shift_done, shift_spread, scale_done = sem("gap_done"), sem("shift_done"), sem("shift_spread"), sem("scale_done")
        fwd_two, bwd_two, max_done, arg_done = sem("fwd_two"), sem("bwd_two"), sem("max_done"), sem("arg_done")
        ex_done, ex_turned, w_done = sem("ex_done"), sem("ex_turned"), sem("w_done")
        acc_scaled, acc_done = sem("acc_scaled"), sem("acc_done")
        ld_proj = sem("ld_proj")
        len_in, sq_done, rbf_done, ld_basis = sems("len_in", 2), sem("sq_done"), sem("rbf_done"), sem("ld_basis")
        silu_done, one_set = sem("silu_done"), sem("one_set")
        out_free = sem("out_free")
        out_ready, out_sent = sem("out_ready"), sem("out_sent")

        counted = [sums_ready, deviations_ready, h_kept, a_ev, a_ps, acc_done, acc_scaled, acc_zero, act_ans, act_req,
                   alpha_done, alpha_turned, arg_done, b_done, bwd_one, bwd_two, carries_packed,
                   carry_set, cols_copied, cols_turned, ex_done, ex_turned, f_done, ffn_act,
                   ffn_ps, fwd_one, fwd_two, gap_done, h_new, m_ev, m_ps,
                   max_done, node_done, oh_copied, oh_made, oh_turned, one_set, out_free,
                   out_ready, post, q_spread, rbf_done, rcol_done, rows_copied, rows_turned,
                   scale_done, shift_done, shift_spread, silu_done, spread_used, sq_done, t_in,
                   t_out, t_ps, w_done,
                   *[s for ring in slot_free for s in ring]]
        LN_A, LN_B = NI + 2 * NI * L, NI + 2 * NI * L + 2 * NI

        def bc(ap, n):
            return ap.unsqueeze(1).to_broadcast([ap.shape[0], n, ap.shape[1]])

        def bcl(ap, n):
            return ap.unsqueeze(len(ap.shape)).to_broadcast([*ap.shape, n])

        def loaded(c, engine):
            _, values = nc.values_load_multi_w_load_instructions(
                super_blk[0:1, bass.ds(c * (CH // 2), CH // 2)], [engine], min_val=0, max_val=NB - 1,
                skip_runtime_bounds_check_because="setup takes the minimum of every place's block and NB - 1, and counts from 0")
            return values

        block = ctx.enter_context(nc.Block())

        @block.sync
        def _(sp):
            sp.dma_start(su_i, a["dst_t"].rearrange("t e -> (t e)").rearrange("(p t) -> p t", p=P)).then_inc(ld_dst, 16)
            for dst, name in ((ident[:, :], "ident"), (iota[:, :], "iota"), (place[:, :, :], "place"),
                              (centers[:, :], "centers"), (w_i[:, :], "w_i"), (w_o[:, :], "w_o"),
                              (m_1[:, :], "m_1"), (m_2[:, :], "m_2"),
                              (u_1[:, :], "u_1"), (u_2[:, :], "u_2")):
                sp.dma_start(dst, a[name]).then_inc(ld_const, 16)
            sp.dma_start(vec1[:, :], a["vec1"].to_broadcast([P, VEC1_W])).then_inc(ld_const, 16)
            sp.dma_start(xn[:, :, :], a["x"].rearrange("(b p) k -> p b k", p=P)).then_inc(ld_const, 16)
            sp.wait_ge(su_rows, 16 * 3 * VC)
            sp.dma_start(flat_len.rearrange("(c p e) -> p c e", p=P, e=P), rows_l).then_inc(su_len, 16)
            sp.wait_ge(su_flat, 1)
            sp.dma_start(flat_dst[1:1 + VC * P * P].rearrange("(c p e) -> p c e", p=P, e=P), r_dst).then_inc(su_dstd, 16)
            sp.dma_start(flat_dst[0:1].rearrange("(a b) -> a b", a=1), edge_word[:, 0:1]).then_inc(su_dstd, 16)
            sp.dma_start(flat_blk.rearrange("(c p) -> p c", p=P), vti[:, 1, :], allow_slow_non_contiguous=True).then_inc(su_dstd, 16)
            sp.wait_ge(su_dstd, 48)
            sp.dma_start(r_prev, flat_dst[0:VC * P * P].rearrange("(c p e) -> p c e", p=P, e=P)).then_inc(su_prev, 16)
            sp.dma_start(blk[:, :], flat_blk.rearrange("(a b) -> a b", a=1)).then_inc(su_prev, 16)
            sp.wait_ge(su_rst, 1)
            sp.dma_start(flat_rst[0:VC * P * P].rearrange("(c p e) -> p c e", p=P, e=P), r_bf[:, :, :]).then_inc(su_rstd, 16)
            sp.dma_start(flat_rst[VC * P * P:VC * P * P + 1].rearrange("(a b) -> a b", a=1), edge_bf[:, 0:1]).then_inc(su_rstd, 16)
            sp.wait_ge(su_rstd, 32)
            for k in range(HEADS):
                for dst, off in ((rst, 0), (rst_r, 1)):
                    sp.dma_start(dst[k * CH:(k + 1) * CH, :, :],
                                 flat_rst[off:off + V * P].rearrange("(c t e) -> t c e", t=CH, e=P)).then_inc(su_tabs, 16)

            def stage_indices(k, l, i):
                c = RING * i + k
                sp.wait_ge(spread_used, START + NG * (l * CHUNKS + c - RING + 1))
                sp.dma_start(idx[:, k, :], src_e[:, bass.ds(c * CH, CH)]).then_inc(idx_in[k], 16)

            def load_projections(l):
                for dst, name in ((w_qs, "w_qs"), (w_kv, "w_kv")):
                    sp.dma_start(dst[:, :], a[name][bass.ds(l * P, P), :]).then_inc(ld_proj, 16)
                sp.dma_start(vec_qskv[:, :], a["vec_qskv"][bass.ds(l, 1), :].to_broadcast([P, QS + KVW])).then_inc(ld_proj, 16)

            load_projections(0)
            sp.wait_ge(su_done, VC * 2)
            with sp.Fori(0, L) as l:
                sp.wait_ge(h_new, START + NI * (l + 1))
                for dst, name in ((w_1, "w_1"), (b_1, "b_1")):
                    sp.dma_start(dst[:, :], a[name][bass.ds(l * P, P), :]).then_inc(ld_layer, 16)
                sp.dma_start(w_2[:, :, :].rearrange("p a b -> p (a b)"), a["w_2"][bass.ds(l * P, P), :]).then_inc(ld_layer, 16)
                sp.dma_start(vec0[:, :], a["vec0"][bass.ds(l, 1), :].to_broadcast([P, VEC0_W])).then_inc(ld_layer, 16)
                with sp.Fori(0, NI) as i:
                    sp.wait_ge(a_ev, START + 2 * BW * (l * NI + i + 1))
                    sp.dma_start(kv_table[bass.ds(i * BW * P, BW * P), :].rearrange("(b p) k -> p b k", p=P),
                                 kvst[:, bass.ds(i * BW, BW), :]).then_inc(tab_out, 16)
                load_projections(l + 1)
                with sp.Fori(0, TURNS) as i:
                    for k in range(RING):
                        stage_indices(k, l, i)
            sp.wait_ge(h_new, START + NI * (L + 1))
            sp.dma_start(m_1c, a["m_1c"].rearrange("p (q k) -> p q k", q=STACK)).then_inc(ld_basis, 16)
            with sp.Fori(0, NI) as i:
                sp.wait_ge(a_ev, START + 2 * BW * (L * NI + i + 1))
                sp.dma_start(src_table[bass.ds(i * BW * P, BW * P), :].rearrange("(b p) k -> p b k", p=P),
                             kvst[:, bass.ds(i * BW, BW), 0:HID]).then_inc(tab_out, 16)
            with sp.Fori(0, TURNS) as i:
                for k in range(RING):
                    stage_indices(k, L, i)
            with sp.Fori(0, NI - 1) as i:
                sp.wait_ge(out_ready, START + i + 1)
                sp.dma_start(out[bass.ds(i * BW * P, BW * P), :].rearrange("(b p) k -> p b k", p=P),
                             dx[:, :, 0:64]).then_inc(out_sent, 16)
                sp.wait_ge(out_sent, 16 * (i + 1))
                sp.sem_inc(out_free, 1)
            sp.wait_ge(out_ready, START + NI)
            full = (N // P) % BW
            lo = (NI - 1) * BW * P
            sp.dma_start(out[lo:lo + full * P, :].rearrange("(b p) k -> p b k", p=P), dx[:, 0:full, 0:64]).then_inc(out_sent, 16)
            sp.dma_start(out[lo + full * P:N, :], dx[0:N - lo - full * P, full, 0:64]).then_inc(out_sent, 16)
            sp.wait_ge(out_sent, 16 * (NI + 1))
            sp.wait_ge(ld_proj, 48 * (L + 1))

        @block.gpsimd
        def _(pool):
            for s in counted:
                pool.sem_inc(s, START)
            pool.wait_ge(su_idx, 1)
            for c in range(VC):
                for dst, name in ((rows_i, "src_t"), (rows_d, "dst_t"), (rows_l, "len_t")):
                    pool.indirect_dma_start(dst[:, c, :], None, a[name],
                                            bass.IndirectOffsetOnAxis(ap=vti[:, 0, c:c + 1], axis=0)).then_inc(su_rows, 16)
            uses = [[pool.alloc_register(f"uses{k}_{j}") for j in range(NG)] for k in range(RING)]
            for k in range(RING):
                for j in range(NG):
                    pool.reg_mov(uses[k][j], 0)

            def gather_chunk(k, turn, l, table, width):
                used = [pool.snap(uses[k][j]) for j in range(NG)]
                pool.wait_ge(tab_out, 16 * NI * (l + 1))
                pool.wait_ge(acc_zero, START + l + 1)
                pool.wait_ge(idx_in[k], 16 * (turn + 1))
                for j in range(NG):
                    pool.wait_ge(slot_free[k][j], START + used[j])
                    pool.reg_add(uses[k][j], uses[k][j], 1)
                    for t in range(j * G, (j + 1) * G):
                        pool.indirect_dma_start(slots[:, k, t, 0:width], None, table,
                                                bass.IndirectOffsetOnAxis(ap=idx[:, k, t:t + 1], axis=0))\
                            .then_inc(kv_in[k][j], 16)

            with pool.Fori(0, L) as l:
                with pool.Fori(0, TURNS) as i:
                    for k in range(RING):
                        gather_chunk(k, l * TURNS + i, l, kv_table, KVW)
            with pool.Fori(0, TURNS) as i:
                for k in range(RING):
                    gather_chunk(k, L * TURNS + i, L, src_table, HID)

        @block.scalar
        def _(act):
            def turned(n):
                act.wait_ge(t_ps, START + n + 1)
                act.copy(hT[:, 0:4 * P], bank[0][:, :]).then_inc(t_out, 1)
                act.copy(hT[:, 4 * P:BW * P], bank[1][:, 0:P]).then_inc(t_out, 1)

            def copy_onehots(g, j):
                act.wait_ge(oh_turned, START + NG * g + j + 1)
                act.wait_ge(q_spread, START + NG * g + max(j - 1, 0))
                act.copy(ohT[:, j % 2, :, :].rearrange("p a b -> p (a b)"), bank[j % 2][:, :]).then_inc(oh_copied, 1)

            def attend_step(l, i, k, ahead):
                g = l * CHUNKS + RING * i + k
                act.wait_ge(rows_turned, START + g + 1)
                act.wait_ge(f_done, START + g)
                act.wait_ge(gap_done, START + g)
                act.copy(f_in[:, :, :, 1:CH + 1], bank[5][0:1, 0:2 * P].rearrange("p (a h t) -> p a h t", a=2, t=CH))\
                    .then_inc(rows_copied, 1)
                act.wait_ge(b_done, START + g)
                act.copy(b_in[:, :, :, 0:CH], bank[5][0:1, 2 * P:4 * P].rearrange("p (a h t) -> p a h t", a=2, t=CH))\
                    .then_inc(rows_copied, 1)
                if ahead:
                    copy_onehots(g + 1, 0)
                act.wait_ge(cols_turned, START + g + 1)
                act.wait_ge(bwd_two, START + g)
                act.copy(icol[:, :], bank[5][:, 0:2]).then_inc(cols_copied, 1)
                if ahead:
                    copy_onehots(g + 1, 1)
                act.wait_ge(shift_spread, START + g + 1)
                act.wait_ge(acc_scaled, START + g)
                act.activation(scale[:, :], bank[5][:, 8:16], ACT.Exp, scale=0.25).then_inc(scale_done, 1)
                act.wait_ge(arg_done, START + g + 1)
                act.wait_ge(ex_turned, START + g)
                act.activation(ex[:, :], bwd[:, :], ACT.Exp, scale=0.25).then_inc(ex_done, 1)
                if ahead:
                    copy_onehots(g + 1, 2)
                    copy_onehots(g + 1, 3)

            def load_lengths(c, k):
                act.wait_ge(q_spread, START + NG * (L * CHUNKS + c - 1))
                act.dma_start(rbf[:, k % 2, :, :],
                              flat_len[bass.ds(c * CH * P, CH * P)].rearrange("(q je) -> q je", q=STACK).unsqueeze(1)
                              .to_broadcast([STACK, NBASIS, CH // STACK * P])).then_inc(len_in[k % 2], 16)

            def distances(nth, c, k):
                act.wait_ge(len_in[k % 2], 16 * nth)
                act.activation(rbf[:, k % 2, :, :], rbf[:, k % 2, :, :], ACT.Square, bias=centers[:, 0:1]).then_inc(sq_done, 1)

            def basis(c, k):
                act.wait_ge(sq_done, START + c + 1)
                act.activation(rbf[:, k % 2, :, :], rbf[:, k % 2, :, :], ACT.Exp, scale=RBF_SCALE).then_inc(rbf_done, 1)

            def message_step(i, k, ahead):
                c = RING * i + k
                g = L * CHUNKS + c
                if ahead:
                    load_lengths(c + 1, k + 1)
                    distances(RING // 2 * i + (k + 1) // 2 + 1, c + 1, k + 1)
                for j in range(NG):
                    silu(g, k, j)
                    if j + 2 < NG:
                        copy_onehots(g, j + 2)
                if ahead:
                    copy_onehots(g + 1, 0)
                    copy_onehots(g + 1, 1)
                    basis(c + 1, k + 1)

            def silu(g, k, j):
                act.wait_ge(spread_used, START + NG * g + j + 1)
                s = slots[:, k, j * G:(j + 1) * G, HID:2 * HID]
                act.activation(s, s, ACT.Silu).then_inc(silu_done, 1)

            def deviation(out, width):
                return act.activation(out[:, :], st[5][:, :], ACT.Sqrt, bias=eps[:, 0:1], scale=1.0 / width)

            act.wait_ge(ld_const, 16 * 12)
            with act.Fori(0, NI) as i:
                turned(i)
                act.wait_ge(post, START + i + 1)
                act.activation(h[:, bass.ds(i * BW, BW), :], t1, ACT.Gelu).then_inc(h_new, 1)
            with act.Fori(0, L) as l:
                act.wait_ge(h_new, START + NI * (l + 1))
                with act.Fori(0, NI) as i:
                    n = NI + 2 * NI * l + i
                    act.wait_ge(t_ps, START + n)
                    act.copy(tsrc, h[:, bass.ds(i * BW, BW), :]).then_inc(t_in, 1)
                    turned(n)
                for j in range(NG):
                    copy_onehots(l * CHUNKS, j)
                with act.Fori(0, TURNS - 1) as i:
                    for k in range(RING):
                        attend_step(l, i, k, True)
                for k in range(RING):
                    attend_step(l, TURNS - 1, k, k < RING - 1)
                act.wait_ge(act_req, START + l + 1)
                act.activation(beta[:, :], logit[:, 0, :], ACT.Sigmoid).then_inc(act_ans, 1)
                with act.Fori(0, NI) as i:
                    r = l * NI + i
                    act.wait_ge(sums_ready, START + r + 1)
                    deviation(st[3], HID).then_inc(deviations_ready, 1)
                    act.wait_ge(t_in, START + NI + 2 * NI * l + NI + i + 1)
                    act.copy(h[:, bass.ds(i * BW, BW), :], tsrc).then_inc(h_kept, 1)
                    turned(NI + 2 * NI * l + NI + i)
                    for f in range(4):
                        for s in range(2):
                            act.wait_ge(ffn_ps, START + 8 * (l * NI + i) + 2 * f + s + 1)
                            act.activation(g1[:, f, s * 320:(s + 1) * 320], bank[2 + (2 * f + s) % 4][:, 0:320], ACT.Gelu,
                                           bias=b_1[:, f:f + 1]).then_inc(ffn_act, 1)
            act.wait_ge(h_new, START + NI * (L + 1))
            with act.Fori(0, NI) as i:
                act.wait_ge(t_ps, START + LN_A + 2 * i)
                act.copy(tsrc, h[:, bass.ds(i * BW, BW), :]).then_inc(t_in, 1)
                turned(LN_A + 2 * i)
                act.wait_ge(act_req, START + L + i + 1)
                deviation(st[4], 64).then_inc(act_ans, 1)
                turned(LN_A + 2 * i + 1)
            load_lengths(0, 0)
            distances(1, 0, 0)
            basis(0, 0)
            copy_onehots(L * CHUNKS, 0)
            copy_onehots(L * CHUNKS, 1)
            with act.Fori(0, TURNS - 1) as i:
                for k in range(RING):
                    message_step(i, k, True)
            for k in range(RING):
                message_step(TURNS - 1, k, k < RING - 1)
            with act.Fori(0, NI) as i:
                turned(LN_B + 3 * i)
                turned(LN_B + 3 * i + 1)
                act.wait_ge(act_req, START + L + NI + 3 * i + 1)
                act.wait_ge(t_ps, START + LN_B + 3 * i + 2)
                act.activation(tsrc[:, :, 0:64], t1[:, :, 0:64], ACT.Silu).then_inc(t_in, 1)
                turned(LN_B + 3 * i + 2)
                for k in range(2):
                    act.wait_ge(act_req, START + L + NI + 3 * i + 2 + k)
                    deviation(st[4], 64).then_inc(act_ans, 1)

        @block.tensor
        def _(pe):
            def turn_blocks(n):
                pe.wait_ge(t_in, START + n + 1)
                pe.wait_ge(t_out, START + 2 * n)
                for b in range(BW):
                    mm = pe.transpose(bank[b // 4][:, (b % 4) * P:(b % 4 + 1) * P], tsrc[:, b, :], ident[:, :])
                mm.then_inc(t_ps, 1)

            def times(n, m, weights, width, K=P):
                pe.wait_ge(t_out, START + 2 * n + 2)
                pe.wait_ge(m_ev, START + m)
                for b in range(BW):
                    mm = pe.matmul(bank[2 + b // 4][:, (b % 4) * P:(b % 4) * P + width], hT[0:K, b * P:(b + 1) * P], weights,
                                   start=True, stop=True)
                mm.then_inc(m_ps, 1)

            def turn(g, k, j):
                pe.wait_ge(oh_made, START + 2 * g + j // 2 + 1)
                pe.wait_ge(oh_copied, START + NG * g + max(j - 1, 0))
                for t in range(G):
                    mm = pe.transpose(bank[j % 2][:, t * P:(t + 1) * P], oh[:, k % 2, j * G + t, :], ident[:, :])
                mm.then_inc(oh_turned, 1)

            def rows(g, k, j, blocks, basis=None):
                pe.wait_ge(oh_copied, START + NG * g + j + 1)
                pe.wait_ge(spread_used, START + NG * g + max(j - 1, 0))
                for t in range(G):
                    o = bank[2 + j % 2][:, t * P:(t + 1) * P]
                    mm = pe.matmul(o, ohT[:, j % 2, t, :], qs[:, blocks[(j * G + t) // 2], 0:HID],
                                   start=True, stop=basis is None)
                    if basis is not None:
                        q, half = (j * G + t) // (CH // STACK), (j * G + t) % (CH // STACK)
                        mm = pe.matmul(o, rbf[:, k % 2, half, :], m_1c[:, q, :],
                                       start=False, stop=True)
                mm.then_inc(q_spread, 1)

            def add_up(g, k, j, width, done, base):
                pe.wait_ge(done, START + NG * base + j + 1)
                pe.wait_ge(acc_done, START + (CH // 2) * g + max(2 * j - 2, 0))
                for t in range(j * G, (j + 1) * G):
                    o = (t % G) // 2 * HEADS * VW
                    mm = pe.matmul(bank[6 + j % 2][:, o:o + width], oh[:, k % 2, t, :], slots[:, k, t, HID:HID + width],
                                   start=(t % 2 == 0), stop=(t % 2 == 1))
                mm.then_inc(slot_free[k][j], 1)

            def block_numbers(c):
                return loaded(c, mybir.EngineType.PE)

            def turn_alpha(g):
                pe.wait_ge(alpha_done, START + NG * g + NG)
                pe.wait_ge(w_done, START + NG * g)
                pe.transpose(bank[4][:, 0:P], alpha[:, :, :].rearrange("p h t -> p (h t)"), ident[:, :])\
                    .then_inc(alpha_turned, 1)

            def attend_step(l, i, k, ahead):
                c = RING * i + k
                g = l * CHUNKS + c
                n, kn = g + 1, (k + 1) % RING
                pe.wait_ge(fwd_one, START + g + 1)
                pe.wait_ge(bwd_one, START + g + 1)
                pe.wait_ge(scale_done, START + g)
                for m, col in enumerate((fwd[:, P - 1:P], rcol[:, 0:1], bwd[:, 0:1], rcol[:, 1:2])):
                    mm = pe.transpose(bank[5][0:1, m * P:(m + 1) * P], col, ident[:, :])
                mm.then_inc(rows_turned, 1)
                if ahead:
                    blocks = block_numbers(c + 1)
                    turn(n, kn, 0)
                pe.wait_ge(carries_packed, START + 2 * g + 2)
                pe.wait_ge(rows_copied, START + 2 * g + 2)
                pe.matmul(bank[5][:, 0:1], c_row[:, 0, :], ones[0:1, 0:1], start=True, stop=True)
                pe.matmul(bank[5][:, 1:2], c_row[:, 1, :], ones[0:1, 0:1], start=True, stop=True)\
                    .then_inc(cols_turned, 1)
                if ahead:
                    turn(n, kn, 1)
                    rows(n, kn, 0, blocks)
                pe.wait_ge(shift_done, START + g + 1)
                pe.wait_ge(cols_copied, START + g + 1)
                pe.matmul(bank[5][:, 8:16], oh[:, k % 2, 0, :], shift[:, :], start=True, stop=True)\
                    .then_inc(shift_spread, 1)
                if ahead:
                    turn(n, kn, 2)
                pe.wait_ge(ex_done, START + g + 1)
                pe.transpose(bank[4][:, P:2 * P], ex[:, :], ident[:, :]).then_inc(ex_turned, 1)
                if ahead:
                    rows(n, kn, 1, blocks)
                    turn(n, kn, 3)
                    rows(n, kn, 2, blocks)
                add_up(g, k, 0, HEADS * VW, w_done, g)
                add_up(g, k, 1, HEADS * VW, w_done, g)
                if ahead:
                    rows(n, kn, 3, blocks)
                add_up(g, k, 2, HEADS * VW, w_done, g)
                add_up(g, k, 3, HEADS * VW, w_done, g)
                if ahead:
                    turn_alpha(n)

            def front(g, k, blocks, basis=None):
                turn(g, k, 0)
                turn(g, k, 1)
                for j in range(NG):
                    rows(g, k, j, blocks, basis)
                    if j + 2 < NG:
                        turn(g, k, j + 2)

            def message_step(i, k, ahead):
                c = RING * i + k
                g = L * CHUNKS + c
                n, kn = g + 1, (k + 1) % RING
                if ahead:
                    blocks = block_numbers(c + 1)
                    turn(n, kn, 0)
                    turn(n, kn, 1)
                add_up(g, k, 0, HID + 1, silu_done, c)
                add_up(g, k, 1, HID + 1, silu_done, c)
                if ahead:
                    pe.wait_ge(rbf_done, START + c + 2)
                    rows(n, kn, 0, blocks, c)
                    turn(n, kn, 2)
                    rows(n, kn, 1, blocks, c)
                    turn(n, kn, 3)
                for j in (2, 3):
                    add_up(g, k, j, HID + 1, silu_done, c)
                    if ahead:
                        rows(n, kn, j, blocks, c)

            pe.wait_ge(su_count, 1)
            pe.matmul(bank[7][:, 0:NB + 1], ones[:, :], row[:, 0, :], start=True, stop=True).then_inc(su_count, 1)
            pe.wait_ge(ld_const, 16 * 12)
            pe.wait_ge(su_turn, 1)
            for n, rows_x in enumerate([r_src, r_rel]):
                for c in range(VC):
                    k = n * VC + c
                    if k >= 2:
                        pe.wait_ge(su_taken, k - 1)
                    pe.transpose(bank[4 + k % 2][:, 0:P], rows_x[:, c, :], ident[:, :]).then_inc(su_turned, 1)
            with pe.Fori(0, NI) as i:
                turn_blocks(i)
                times(i, i, w_i[:, :], HID, 64)
            pe.wait_ge(su_prev, 32)
            with pe.Fori(0, L) as l:
                with pe.Fori(0, NI) as i:
                    n = NI + 2 * NI * l + i
                    turn_blocks(n)
                    pe.wait_ge(ld_proj, 48 * (l + 1))
                    pe.wait_ge(t_out, START + 2 * n + 2)
                    for b in range(BW):
                        pe.wait_ge(a_ev, START + 2 * BW * (l * NI + i) + max(2 * b - 2, 0))
                        pe.matmul(bank[2 + b % 2][:, 0:QS], hT[:, b * P:(b + 1) * P], w_qs[:, :], start=True, stop=True)\
                            .then_inc(a_ps, 1)
                        pe.matmul(bank[4 + b % 2][:, 0:BAND], hT[:, b * P:(b + 1) * P], w_kv[:, :], start=True, stop=True)\
                            .then_inc(a_ps, 1)
                front(l * CHUNKS, 0, block_numbers(0))
                turn_alpha(l * CHUNKS)
                with pe.Fori(0, TURNS - 1) as i:
                    for k in range(RING):
                        attend_step(l, i, k, True)
                for k in range(RING):
                    attend_step(l, TURNS - 1, k, k < RING - 1)
                with pe.Fori(0, NI) as i:
                    n = NI + 2 * NI * l + NI + i
                    r = l * NI + i
                    turn_blocks(n)
                    pe.wait_ge(t_out, START + 2 * n + 2)
                    pe.wait_ge(ld_layer, 64 * (l + 1))
                    for f in range(4):
                        for s in range(2):
                            k = 2 * f + s
                            pe.wait_ge(ffn_act, START + 8 * r + max(k - 3, 0))
                            pe.matmul(bank[2 + k % 4][:, 0:320], w_1[:, f * HID:(f + 1) * HID], hT[:, s * 320:(s + 1) * 320],
                                      start=True, stop=True).then_inc(ffn_ps, 1)
                    pe.wait_ge(ffn_act, START + 8 * r + 8)
                    pe.wait_ge(m_ev, START + NI + r)
                    pe.wait_ge(h_new, START + NI + r)
                    for b in range(BW):
                        o = bank[6 + b // 4][:, (b % 4) * P:(b % 4 + 1) * P]
                        for f in range(4):
                            pe.matmul(o, g1[:, f, b * P:(b + 1) * P], w_2[:, f, :], start=(f == 0), stop=False)
                        mm = pe.matmul(o, ones[0:1, :], vec0[0:1, VEC0["b2"]:VEC0["b2"] + P], start=False, stop=True)
                    mm.then_inc(m_ps, 1)
            M0 = NI + NI * L
            with pe.Fori(0, NI) as i:
                turn_blocks(LN_A + 2 * i)
                times(LN_A + 2 * i, M0 + i, w_o[:, :], 64)
                turn_blocks(LN_A + 2 * i + 1)
                pe.wait_ge(t_out, START + 2 * (LN_A + 2 * i + 1) + 2)
                for b in range(BW):
                    pe.wait_ge(a_ev, START + 2 * BW * (L * NI + i) + max(2 * b - 2, 0))
                    pe.matmul(bank[4 + b % 2][:, 0:2 * HID], hT[0:64, b * P:(b + 1) * P], m_1[:, :], start=True, stop=True)\
                        .then_inc(a_ps, 1)
            blocks = block_numbers(0)
            pe.wait_ge(ld_basis, 16)
            pe.wait_ge(rbf_done, START + 1)
            front(L * CHUNKS, 0, blocks, 0)
            with pe.Fori(0, TURNS - 1) as i:
                for k in range(RING):
                    message_step(i, k, True)
            for k in range(RING):
                message_step(TURNS - 1, k, k < RING - 1)
            with pe.Fori(0, NI) as i:
                for k, (weights, width) in enumerate(((m_2, P), (u_1, P), (u_2, 64))):
                    turn_blocks(LN_B + 3 * i + k)
                    times(LN_B + 3 * i + k, M0 + NI + 3 * i + k, weights[:, :], 64, width)

        @block.vector
        def _(dve):
            class Steps:
                def __init__(self, s, base=0):
                    self.s, self.base, self.n = s, base, 0

                def __call__(self, ins):
                    self.n += 1
                    ins.then_inc(self.s, 1)
                    dve.wait_ge(self.s, self.base + self.n)

            step = Steps(su_step, 0)
            dve.memset(ones[:, :], 1.0)
            dve.memset(eps[:, :], 1e-5)
            dve.memset(row[:, :, :], 0.0)
            dve.memset(shift[:, :], 0.0)
            dve.memset(f_in[:, :, :, :], -BIG)
            dve.memset(b_in[:, :, :, :], -BIG)
            dve.memset(edge_word[:, :], -5.0)
            step(dve.memset(edge_bf[:, :], -BIG))
            dve.wait_ge(ld_dst, 16)
            step(dve.tensor_copy(su_f, su_i))
            for b in range(1, NB + 1):
                step(dve.tensor_scalar(su_o, su_f, float(b * P), None, ALU.is_lt, ALU.add, accum_out=row[:, 0, b:b + 1]))
            dve.memset(vt[:, 0, :], 0.0).then_inc(su_count, 1)
            dve.wait_ge(su_count, 2)
            rp = row[:, 1, :]
            step(dve.tensor_copy(rp, bank[7][:, 0:NB + 1]))
            step(dve.tensor_copy(rowi[:, 0, :], rp))
            step(dve.tensor_scalar(rowi[:, 1, :], rowi[:, 0, :], 7, None, ALU.arith_shift_right))
            step(dve.tensor_copy(row[:, 2, :], rowi[:, 1, :]))
            step(dve.tensor_scalar(row[:, 3, :], rp, float(P - 1), None, ALU.add))
            step(dve.tensor_copy(rowi[:, 0, :], row[:, 3, :]))
            step(dve.tensor_scalar(rowi[:, 1, :], rowi[:, 0, :], 7, None, ALU.arith_shift_right))
            step(dve.tensor_copy(row[:, 4, :], rowi[:, 1, :]))
            step(dve.tensor_tensor(row[:, 5, 0:NB], row[:, 4, 1:NB + 1], row[:, 2, 0:NB], ALU.subtract))
            step(dve.tensor_scalar(row[:, 3, 0:NB], row[:, 5, 0:NB], 1.0, None, ALU.add))
            step(dve.tensor_copy(rowi[:, 0, :], row[:, 3, :]))
            step(dve.tensor_scalar(rowi[:, 1, :], rowi[:, 0, :], 1, None, ALU.arith_shift_right))
            step(dve.tensor_copy(row[:, 6, 0:NB], rowi[:, 1, 0:NB]))
            step(dve.tensor_tensor_scan(row[:, 7, 0:NB], ones[:, 0:NB], row[:, 6, 0:NB], 0.0, op0=ALU.mult, op1=ALU.add))
            step(dve.tensor_tensor(row[:, 8, 0:NB], row[:, 7, 0:NB], row[:, 6, 0:NB], ALU.subtract))
            step(dve.scalar_tensor_tensor(out=row[:, 9, 0:NB], in0=row[:, 8, 0:NB], scalar=-2.0, in1=row[:, 2, 0:NB],
                                          op0=ALU.mult, op1=ALU.add))
            step(dve.tensor_tensor(row[:, 10, 0:NB - 1], row[:, 9, 1:NB], row[:, 9, 0:NB - 1], ALU.subtract))
            dve.wait_ge(ld_const, 16 * 12)
            for c in range(VC):
                for k, w in ((0, ones[:, 0:NB]), (1, row[:, 10, 0:NB])):
                    step(dve.scalar_tensor_tensor(out=row[:, 11, 0:NB], in0=row[:, 7, 0:NB], scalar=place[:, 1, c:c + 1], in1=w,
                                                  op0=ALU.is_le, op1=ALU.mult, accum_out=vt[:, k, c:c + 1]))
            step(dve.tensor_tensor(vt[:, 2, :], vt[:, 1, :], place[:, 0, :], ALU.add))
            step(dve.tensor_scalar(vt[:, 2, :], vt[:, 2, :], float(TILES - 1), None, ALU.min))
            step(dve.tensor_scalar(vt[:, 3, :], vt[:, 0, :], float(NB - 1), None, ALU.min))
            step(dve.tensor_copy(vti[:, 1, :], vt[:, 3, :]))
            dve.tensor_copy(vti[:, 0, :], vt[:, 2, :]).then_inc(su_idx, 1)
            step(dve.tensor_scalar(vt[:, 1, :], vt[:, 0, :], float(P), None, ALU.mult))
            dve.wait_ge(su_rows, 16 * 3 * VC)
            step(dve.tensor_copy(rows_f, rows_d))
            for c in range(VC):
                step(dve.tensor_scalar(r_rel[:, c, :], rows_f[:, c, :], vt[:, 1, c:c + 1], None, ALU.subtract))
            step(dve.tensor_scalar(r_ok, r_rel, 0.0, None, ALU.is_ge))
            step(dve.tensor_scalar(r_dst, r_rel, float(P), None, ALU.is_lt))
            step(dve.tensor_tensor(r_ok, r_ok, r_dst, ALU.mult))
            step(dve.scalar_tensor_tensor(out=r_dst, in0=rows_f, scalar=1.0, in1=r_ok, op0=ALU.add, op1=ALU.mult))
            step(dve.tensor_scalar(r_dst, r_dst, -1.0, None, ALU.add))
            dve.tensor_copy(vt[:, 3, 0:1], vt[:, 2, 0:1]).then_inc(su_flat, 1)
            step(dve.tensor_copy(r_src, rows_i))
            dve.tensor_copy(vt[:, 3, 1:2], vt[:, 2, 1:2]).then_inc(su_turn, 1)
            for k in range(2 * VC):
                c = k % VC
                dve.wait_ge(su_turned, k + 1)
                dst = src_e if k < VC else rel_e
                dve.tensor_copy(dst[:, c * P:(c + 1) * P], bank[4 + k % 2][:, 0:P]).then_inc(su_taken, 1)
                dve.wait_ge(su_taken, k + 1)
                dve.tensor_copy(vt[:, 3, 2:3], vt[:, 2, 2:3]).then_inc(su_done, 1)
            dve.wait_ge(su_prev, 32)
            step(dve.tensor_tensor(r_dst, r_dst, r_prev, ALU.not_equal))
            step(dve.tensor_scalar(r_bf[:, :, :], r_dst, -BIG, None, ALU.mult))
            dve.tensor_copy(vt[:, 3, 3:4], vt[:, 2, 3:4]).then_inc(su_rst, 1)
            dve.wait_ge(su_tabs, 16 * 2 * HEADS)
            step(dve.tensor_reduce(rst_sum[:, :, 0], rst[:, :, :], axis=X, op=ALU.add))
            step(dve.tensor_copy(rst_b[:, :, :], rst_r[:, :, ::-1]))
            step(dve.tensor_reduce(rst_sum[:, :, 1], rst_b[:, :, :], axis=X, op=ALU.add))
            step(dve.tensor_scalar(cont[:, :], rst[0:1, :, 0], -1.0, None, ALU.is_ge))

            step(dve.tensor_scalar(super_blk[:, :], blk[:, ::2], 0, None, ALU.add))
            step(dve.memset(tsrc, 0.0))
            with dve.Fori(0, NI) as i:
                dve.wait_ge(t_ps, START + i)
                dve.tensor_scalar(tsrc[:, :, 0:64], xn[:, bass.ds(i * BW, BW), :], 0.0, None, ALU.add).then_inc(t_in, 1)
                dve.wait_ge(m_ps, START + i + 1)
                dve.wait_ge(h_new, START + i)
                dve.tensor_tensor(t1[:, 0:4, :], bank[2][:, :].rearrange("p (b k) -> p b k", b=4),
                                  bc(vec1[:, VEC1["bi"]:VEC1["bi"] + P], 4), ALU.add).then_inc(node_done, 1)
                dve.tensor_tensor(t1[:, 4, :], bank[3][:, 0:P], vec1[:, VEC1["bi"]:VEC1["bi"] + P], ALU.add).then_inc(m_ev, 1)
                dve.wait_ge(m_ev, START + i + 1)
                dve.wait_ge(node_done, START + i + 1)
                dve.tensor_copy(st[5][:, :], ones[:, 0:BW]).then_inc(post, 1)

            def norm(step, width, request):
                y, z = t1[:, :, 0:width], t2[:, :, 0:width]
                step(dve.tensor_reduce(st[2][:, :], y, axis=X, op=ALU.add))
                step(dve.tensor_scalar(st[2][:, :], st[2][:, :], 1.0 / width, None, ALU.mult))
                step(dve.tensor_tensor(y, y, bcl(st[2][:, :], width), ALU.subtract))
                step(dve.tensor_tensor(z, y, y, ALU.mult))
                dve.tensor_reduce(st[5][:, :], z, axis=X, op=ALU.add).then_inc(act_req, 1)
                dve.wait_ge(act_ans, START + request)
                step(dve.reciprocal(st[6][:, :], st[4][:, :]))
                step(dve.tensor_tensor(y, y, bcl(st[6][:, :], width), ALU.mult))

            def onehots(g, k, c, half):
                H = CH // 2
                dve.tensor_tensor(oh[:, k % 2, half * H:(half + 1) * H, :], bc(iota[:, :], H),
                                  bcl(rel_e[:, bass.ds(c * CH + half * H, H)], P), ALU.is_equal).then_inc(oh_made, 1)

            def add_part(g, turn, k, s, blocks, width):
                dve.wait_ge(slot_free[k][s // 2], START + turn + 1)
                dve.wait_ge(acc_done, START + (CH // 2) * g + s)
                a_s, o = acc[:, blocks[s], 0:width], s % 2 * HEADS * VW
                dve.tensor_tensor(a_s, a_s, bank[6 + s // 2 % 2][:, o:o + width], ALU.add).then_inc(acc_done, 1)

            def block_numbers(c):
                return loaded(c, mybir.EngineType.DVE)

            def multiply(g, turn, k, j):
                dve.wait_ge(kv_in[k][j], 16 * G * (turn + 1))
                dve.wait_ge(q_spread, START + NG * g + j + 1)
                keys = slots[:, k, j * G:(j + 1) * G, 0:HID]
                dve.tensor_tensor(keys, keys, bank[2 + j % 2][:, :].rearrange("p (t k) -> p t k", t=G),
                                  ALU.mult).then_inc(spread_used, 1)

            def sum_heads(g, k, j):
                dve.wait_ge(spread_used, START + NG * g + j + 1)
                dve.tensor_reduce(alpha[:, :, j * G:(j + 1) * G].rearrange("p h t -> p t h"),
                                  slots[:, k, j * G:(j + 1) * G, 0:HID].rearrange("p t (h d) -> p t h d", h=HEADS),
                                  axis=X, op=ALU.add).then_inc(alpha_done, 1)

            def attend_step(l, i, k, ahead):
                c = RING * i + k
                turn = l * TURNS + i
                g = l * CHUNKS + c
                n, kn, turn_n = g + 1, (k + 1) % RING, turn + (k + 1) // RING
                dve.wait_ge(rows_turned, START + g)
                dve.tensor_scalar(rcol[:, :], rst_sum[:, c, :], 0.0, None, ALU.add).then_inc(rcol_done, 1)
                dve.wait_ge(alpha_turned, START + g + 1)
                aT = bank[4][:, 0:P]
                R, Rb = rst[:, c, :], rst_b[:, c, :]
                dve.tensor_tensor_scan(fwd[:, :], R, aT, -BIG, op0=ALU.add, op1=ALU.max).then_inc(fwd_one, 1)
                dve.wait_ge(rcol_done, START + g + 1)
                dve.tensor_tensor_scan(bwd[:, ::-1], Rb, aT[:, ::-1], -BIG, op0=ALU.add, op1=ALU.max)\
                    .then_inc(bwd_one, 1)
                dve.tensor_copy(f_in[:, 0, :, 0:1], f_out[:, :, CH:CH + 1]).then_inc(carry_set, 1)
                if ahead:
                    onehots(n, kn, c + 1, 0)
                blocks = block_numbers(c)
                dve.wait_ge(carry_set, START + g + 1)
                dve.wait_ge(rows_copied, START + 2 * g + 1)
                dve.tensor_tensor_scan(f_out[:, :, :].rearrange("p h t -> p (h t)"),
                                       f_in[:, 1, :, :].rearrange("p h t -> p (h t)"),
                                       f_in[:, 0, :, :].rearrange("p h t -> p (h t)"), -BIG, op0=ALU.add, op1=ALU.max)\
                    .then_inc(f_done, 1)
                dve.wait_ge(rows_copied, START + 2 * g + 2)
                dve.tensor_tensor_scan(b_out[:, :, :].rearrange("p h t -> p (h t)")[:, ::-1],
                                       b_in[:, 1, :, :].rearrange("p h t -> p (h t)")[:, ::-1],
                                       b_in[:, 0, :, :].rearrange("p h t -> p (h t)")[:, ::-1], -BIG,
                                       op0=ALU.add, op1=ALU.max).then_inc(b_done, 1)
                dve.wait_ge(f_done, START + g + 1)
                dve.wait_ge(cols_turned, START + g)
                dve.tensor_copy(c_row[:, 0, :].rearrange("p (h t) -> p h t", h=HEADS), f_out[:, :, 0:CH])\
                    .then_inc(carries_packed, 1)
                dve.wait_ge(b_done, START + g + 1)
                dve.tensor_tensor(gap[:, :], f_in[:, 0, :, 0], b_out[:, :, 0], ALU.subtract).then_inc(gap_done, 1)
                dve.tensor_copy(c_row[:, 1, :].rearrange("p (h t) -> p h t", h=HEADS), b_out[:, :, 1:CH + 1])\
                    .then_inc(carries_packed, 1)
                dve.wait_ge(gap_done, START + g + 1)
                dve.wait_ge(shift_spread, START + g)
                dve.tensor_scalar(shift[0:1, :], gap[:, :], 0.0, cont[:, bass.ds(c, 1)], ALU.min, ALU.mult)\
                    .then_inc(shift_done, 1)
                if ahead:
                    onehots(n, kn, c + 1, 1)
                dve.wait_ge(cols_copied, START + g + 1)
                dve.tensor_tensor_scan(fwd[:, :], R, aT, icol[:, 0:1], op0=ALU.add, op1=ALU.max).then_inc(fwd_two, 1)
                dve.wait_ge(bwd_one, START + g + 1)
                dve.tensor_tensor_scan(bwd[:, ::-1], Rb, aT[:, ::-1], icol[:, 1:2], op0=ALU.add, op1=ALU.max)\
                    .then_inc(bwd_two, 1)
                dve.wait_ge(fwd_two, START + g + 1)
                dve.wait_ge(bwd_two, START + g + 1)
                dve.tensor_tensor(fwd[:, :], fwd[:, :], bwd[:, :], ALU.max).then_inc(max_done, 1)
                dve.wait_ge(max_done, START + g + 1)
                dve.tensor_tensor(bwd[:, :], aT, fwd[:, :], ALU.subtract).then_inc(arg_done, 1)
                if ahead:
                    multiply(n, turn_n, kn, 0)
                dve.wait_ge(scale_done, START + g + 1)
                dve.wait_ge(acc_done, START + (CH // 2) * g)
                a_0 = acc[:, blocks[0], :].rearrange("p (h k) -> p h k", h=HEADS)
                dve.tensor_tensor(a_0, a_0, bcl(scale[:, :], VW), ALU.mult).then_inc(acc_scaled, 1)
                if ahead:
                    sum_heads(n, kn, 0)
                dve.wait_ge(ex_turned, START + g + 1)
                exs = bank[4][:, P:2 * P].rearrange("p (h t) -> p t h", h=HEADS)
                for j in range(NG):
                    vals = slots[:, k, j * G:(j + 1) * G, HID:KVW].rearrange("p t (h k) -> p t h k", h=HEADS)
                    dve.tensor_tensor(vals, vals, bcl(exs[:, j * G:(j + 1) * G, :], VW), ALU.mult).then_inc(w_done, 1)
                dve.wait_ge(acc_scaled, START + g + 1)
                for j in range(1, NG):
                    if ahead:
                        multiply(n, turn_n, kn, j)
                    add_part(g, turn, k, 2 * j - 2, blocks, HEADS * VW)
                    if ahead:
                        sum_heads(n, kn, j)
                    add_part(g, turn, k, 2 * j - 1, blocks, HEADS * VW)
                for s in (CH // 2 - 2, CH // 2 - 1):
                    add_part(g, turn, k, s, blocks, HEADS * VW)

            def messages(g, turn, k, j):
                dve.wait_ge(kv_in[k][j], 16 * G * (turn + 1))
                dve.wait_ge(q_spread, START + NG * g + j + 1)
                dve.tensor_tensor(slots[:, k, j * G:(j + 1) * G, HID:2 * HID], slots[:, k, j * G:(j + 1) * G, 0:HID],
                                  bank[2 + j % 2][:, :].rearrange("p (t k) -> p t k", t=G), ALU.add)\
                    .then_inc(spread_used, 1)

            def message_step(i, k, ahead):
                c = RING * i + k
                turn = L * TURNS + i
                g = L * CHUNKS + c
                n, kn, turn_n = g + 1, (k + 1) % RING, turn + (k + 1) // RING
                blocks = block_numbers(c)
                for s in range(4):
                    add_part(g, turn, k, s, blocks, HID + 1)
                if ahead > 1:
                    onehots(n + 1, k, c + 2, 0)
                if ahead:
                    messages(n, turn_n, kn, 0)
                    messages(n, turn_n, kn, 1)
                add_part(g, turn, k, 4, blocks, HID + 1)
                add_part(g, turn, k, 5, blocks, HID + 1)
                if ahead:
                    messages(n, turn_n, kn, 2)
                add_part(g, turn, k, 6, blocks, HID + 1)
                add_part(g, turn, k, 7, blocks, HID + 1)
                if ahead > 1:
                    onehots(n + 1, k, c + 2, 1)
                if ahead:
                    messages(n, turn_n, kn, 3)

            K_MIX, K_NORM, K_OUT = 4, 7, 10
            KL = K_MIX + K_NORM * NI
            with dve.Fori(0, L) as l:
                with dve.Fori(0, NI) as i:
                    ga = l * NI + i
                    dve.wait_ge(ld_proj, 48 * (l + 1))
                    for b in range(BW):
                        dve.wait_ge(a_ps, START + 2 * BW * ga + 2 * b + 1)
                        dve.tensor_tensor(qs[:, i * BW + b, :], bank[2 + b % 2][:, 0:QS], vec_qskv[:, 0:QS],
                                          ALU.add).then_inc(a_ev, 1)
                        dve.wait_ge(a_ps, START + 2 * BW * ga + 2 * b + 2)
                        dve.tensor_tensor(kvst[:, i * BW + b, :], bank[4 + b % 2][:, 0:BAND], vec_qskv[:, QS:QS + BAND],
                                          ALU.add).then_inc(a_ev, 1)
                dve.wait_ge(a_ev, START + 2 * BW * NI * (l + 1))
                dve.memset(f_out[:, :, :], -BIG).then_inc(node_done, 1)
                dve.memset(acc[:, :, :], 0.0).then_inc(acc_zero, 1)
                dve.wait_ge(acc_zero, START + l + 1)
                onehots(l * CHUNKS, 0, 0, 0)
                dve.wait_ge(node_done, START + NI + l + 1)
                onehots(l * CHUNKS, 0, 0, 1)
                for j in range(NG):
                    multiply(l * CHUNKS, l * TURNS, 0, j)
                    sum_heads(l * CHUNKS, 0, j)
                with dve.Fori(0, TURNS - 1) as i:
                    for k in range(RING):
                        attend_step(l, i, k, True)
                for k in range(RING):
                    attend_step(l, TURNS - 1, k, k < RING - 1)
                dve.wait_ge(acc_done, START + (CH // 2) * CHUNKS * (l + 1))
                dve.wait_ge(ld_layer, 64 * (l + 1))
                step = Steps(post, START + NI + KL * l)
                w = lambda name: vec0[:, VEC0[name]:VEC0[name] + P]
                dve.tensor_tensor(w02, w("w0"), w("w2"), ALU.add)
                dve.tensor_tensor(w12, w("w1"), w("w2"), ALU.subtract)
                rows17 = acc[:, :, :].rearrange("p b (h k) -> p (b h) k", h=HEADS)
                step(dve.tensor_scalar(den, rows17[:, :, DH], 1e-16, None, ALU.add))
                step(dve.reciprocal(rden, den))
                step(dve.tensor_tensor(o_all.rearrange("p b (h d) -> p (b h) d", h=HEADS), rows17[:, :, 0:DH], bcl(rden, DH),
                                       ALU.mult))
                for b in range(NB):
                    dve.scalar_tensor_tensor(out=junk[:, b, :], in0=o_all[:, b, :], scalar=1.0, in1=w02,
                                             op0=ALU.mult, op1=ALU.mult, accum_out=logit[:, 0, b:b + 1])
                for b in range(NB):
                    ins = dve.scalar_tensor_tensor(out=junk[:, NB + b, :], in0=qs[:, b, HID:2 * HID], scalar=1.0, in1=w12,
                                                   op0=ALU.mult, op1=ALU.mult, accum_out=logit[:, 1, b:b + 1])
                step(ins)
                dve.tensor_tensor(logit[:, 0, :], logit[:, 0, :], logit[:, 1, :], ALU.add).then_inc(act_req, 1)
                assert step.n == K_MIX, step.n

                def mix_and_norm(i, r, update):
                    step = Steps(post, START + NI + KL * l + K_MIX + K_NORM * i)
                    bs = bass.ds(i * BW, BW)
                    dve.wait_ge(t_in, START + NI + 2 * NI * l + NI + i)
                    step(dve.tensor_tensor(dx, qs[:, bs, HID:2 * HID], o_all[:, bs, :], ALU.subtract))
                    dve.wait_ge(deviations_ready, START + r)
                    step(dve.tensor_tensor(t1, o_all[:, bs, :], h[:, bs, :], ALU.add))
                    dve.wait_ge(act_ans, START + l + 1)
                    for b in range(BW):
                        ins = dve.scalar_tensor_tensor(out=t1[:, b, :], in0=dx[:, b, :], scalar=beta[:, bass.ds(i * BW + b, 1)],
                                                       in1=t1[:, b, :], op0=ALU.mult, op1=ALU.add,
                                                       accum_out=st[4][:, b:b + 1])
                    step(ins)
                    step(dve.tensor_scalar(st[2][:, :], st[4][:, :], -1.0 / HID, None, ALU.mult))
                    step(dve.tensor_tensor(dx, t1, bcl(st[2][:, :], P), ALU.add))
                    for b in range(BW):
                        ins = dve.scalar_tensor_tensor(out=t2[:, b, :], in0=dx[:, b, :], scalar=1.0, in1=dx[:, b, :],
                                                       op0=ALU.mult, op1=ALU.mult, accum_out=st[5][:, b:b + 1])
                    ins.then_inc(sums_ready, 1)
                    dve.wait_ge(deviations_ready, START + r + 1)
                    step(dve.reciprocal(st[6][:, :], st[3][:, :]))
                    for b in range(BW):
                        ins = dve.scalar_tensor_tensor(out=dx[:, b, :], in0=dx[:, b, :], scalar=st[6][:, b:b + 1], in1=w("g"),
                                                       op0=ALU.mult, op1=ALU.mult)
                    step(ins)
                    dve.wait_ge(t_ps, START + NI + 2 * NI * l + NI + i)
                    dve.wait_ge(h_kept, START + r)
                    dve.tensor_tensor(tsrc, dx, bc(w("b"), BW), ALU.add).then_inc(t_in, 1)
                    assert step.n == K_NORM, step.n
                    if update:
                        add_feed_forward(i - 1, r - 1)

                def add_feed_forward(i, r):
                    dve.wait_ge(m_ps, START + NI + r + 1)
                    dve.wait_ge(h_kept, START + r + 1)
                    h4, h1 = h[:, bass.ds(i * BW, 4), :], h[:, i * BW + 4, :]
                    dve.tensor_tensor(h4, h4, bank[6][:, :].rearrange("p (b k) -> p b k", b=4), ALU.add).then_inc(m_ev, 1)
                    dve.tensor_tensor(h1, h1, bank[7][:, 0:P], ALU.add).then_inc(h_new, 1)

                mix_and_norm(0, l * NI, False)
                with dve.Fori(1, NI) as i:
                    mix_and_norm(i, l * NI + i, True)
                add_feed_forward(NI - 1, l * NI + NI - 1)
            P0 = NI + KL * L
            v1 = lambda name, w=64: bc(vec1[:, VEC1[name]:VEC1[name] + w], BW)
            with dve.Fori(0, NI) as i:
                bs = bass.ds(i * BW, BW)
                K = K_OUT
                step = Steps(post, START + P0 + K * i)
                y = t1[:, :, 0:64]
                dve.wait_ge(m_ps, START + NI + NI * L + i + 1)
                step(dve.tensor_tensor(t1[:, 0:4, 0:64], bank[2][:, :].rearrange("p (b k) -> p b k", b=4)[:, :, 0:64],
                                       bc(vec1[:, VEC1["bo"]:VEC1["bo"] + 64], 4), ALU.add))
                dve.tensor_tensor(t1[:, 4, 0:64], bank[3][:, 0:64], vec1[:, VEC1["bo"]:VEC1["bo"] + 64], ALU.add).then_inc(m_ev, 1)
                dve.wait_ge(m_ev, START + NI + NI * L + i + 1)
                step(dve.tensor_tensor(y, y, xn[:, bs, :], ALU.add))
                norm(step, 64, L + i + 1)
                step(dve.tensor_scalar(xn[:, bs, :], y, 0.0, None, ALU.add))
                dve.wait_ge(t_ps, START + LN_A + 2 * i + 1)
                dve.tensor_copy(tsrc[:, :, 0:64], y).then_inc(t_in, 1)
                step(dve.tensor_copy(st[5][:, :], ones[:, 0:BW]))
                assert step.n == K, step.n
                for b in range(BW):
                    dve.wait_ge(a_ps, START + 2 * BW * L * NI + BW * i + b + 1)
                    dve.tensor_tensor(qs[:, i * BW + b, 0:HID], bank[4 + b % 2][:, HID:2 * HID],
                                      vec1[:, VEC1["mb1"]:VEC1["mb1"] + HID], ALU.add).then_inc(a_ev, 1)
                    dve.tensor_scalar(kvst[:, i * BW + b, 0:HID], bank[4 + b % 2][:, 0:HID], 0.0, None, ALU.add).then_inc(a_ev, 1)
            dve.wait_ge(tab_out, 16 * NI * (L + 1))
            dve.wait_ge(a_ev, START + 2 * BW * NI * (L + 1))
            dve.memset(slots[:, :, :, 2 * HID:2 * HID + 1], 1.0).then_inc(one_set, 1)
            dve.memset(acc[:, :, :], 0.0).then_inc(acc_zero, 1)
            dve.wait_ge(one_set, START + 1)
            dve.wait_ge(acc_zero, START + L + 1)
            onehots(L * CHUNKS, 0, 0, 0)
            onehots(L * CHUNKS, 0, 0, 1)
            onehots(L * CHUNKS + 1, 1, 1, 0)
            onehots(L * CHUNKS + 1, 1, 1, 1)
            for j in range(NG):
                messages(L * CHUNKS, L * TURNS, 0, j)
            with dve.Fori(0, TURNS - 1) as i:
                for k in range(RING):
                    message_step(i, k, 2)
            for k in range(RING):
                message_step(TURNS - 1, k, RING - 1 - k)
            P1 = P0 + K_OUT * NI
            dve.wait_ge(acc_done, START + (CH // 2) * CHUNKS * (L + 1))
            with dve.Fori(0, NI) as i:
                bs = bass.ds(i * BW, BW)
                K = 24
                Q1 = L + NI + 2 * i
                step = Steps(post, START + P1 + K * i)
                M1 = NI + NI * L + NI + 3 * i
                T1 = LN_B + 3 * i
                cnt = acc[:, bs, HID]
                step(dve.tensor_scalar(st[0][:, :], cnt, 1.0, None, ALU.max))
                step(dve.reciprocal(st[1][:, :], st[0][:, :]))
                step(dve.tensor_tensor(st[2][:, :], cnt, st[1][:, :], ALU.mult))
                dve.wait_ge(t_ps, START + T1)
                dve.tensor_tensor(tsrc, acc[:, bs, 0:HID], bcl(st[1][:, :], HID), ALU.mult).then_inc(t_in, 1)
                step(dve.tensor_tensor(t2[:, :, 0:64], v1("mb2"), bcl(st[2][:, :], 64), ALU.mult))

                def evac(m, other4, other1, out4, out1):
                    dve.wait_ge(m_ps, START + m + 1)
                    step(dve.tensor_tensor(out4, bank[2][:, :].rearrange("p (b k) -> p b k", b=4)[:, :, 0:64], other4, ALU.add))
                    dve.tensor_tensor(out1, bank[3][:, 0:64], other1, ALU.add).then_inc(m_ev, 1)
                    dve.wait_ge(m_ev, START + m + 1)

                bias = lambda name: (bc(vec1[:, VEC1[name]:VEC1[name] + 64], 4), vec1[:, VEC1[name]:VEC1[name] + 64])
                evac(M1, t2[:, 0:4, 0:64], t2[:, 4, 0:64], t1[:, 0:4, 64:128], t1[:, 4, 64:128])
                step(dve.tensor_scalar(t1[:, :, 0:64], xn[:, bs, :], 0.0, None, ALU.add))
                dve.wait_ge(t_ps, START + T1 + 1)
                dve.tensor_copy(tsrc, t1).then_inc(t_in, 1)
                evac(M1 + 1, *bias("ub1"), t1[:, 0:4, 0:64], t1[:, 4, 0:64])
                step(dve.tensor_copy(st[5][:, :], ones[:, 0:BW]))
                dve.tensor_copy(st[6][:, :], ones[:, 0:BW]).then_inc(act_req, 1)
                evac(M1 + 2, *bias("ub2"), t1[:, 0:4, 0:64], t1[:, 4, 0:64])
                y = t1[:, :, 0:64]
                norm(step, 64, Q1 + 1)
                step(dve.tensor_tensor(y, y, v1("g"), ALU.mult))
                step(dve.tensor_tensor(y, y, v1("b"), ALU.add))
                step(dve.tensor_tensor(y, y, xn[:, bs, :], ALU.add))
                norm(step, 64, Q1 + 2)
                dve.wait_ge(out_free, START + i)
                dve.tensor_copy(dx[:, :, 0:64], y).then_inc(out_ready, 1)
                assert step.n == K, step.n


RBF_WIDTH = (10.0 / (NBASIS - 1)) * 0.5
RBF_SCALE = -1.0 / (2.0 * RBF_WIDTH ** 2)


def lay_out(inp):
    f = {k: np.asarray(v) for k, v in inp.items()}
    z = lambda *s: np.zeros(s, np.float32)
    a = {}
    a["x"] = np.concatenate([f["x"], z(NPAD - N, 64)])
    pad = TILES * P - E
    a["src_t"] = np.concatenate([f["src"], np.zeros(pad, np.int32)]).reshape(TILES, P)
    a["dst_t"] = np.concatenate([f["dst"], np.full(pad, 2 * NPAD, np.int32)]).reshape(TILES, P)
    a["len_t"] = np.concatenate([f["edge_weight1"][:, 0], z(pad)]).reshape(TILES, P)
    n = {k[7:]: v for k, v in f.items() if k.startswith("L0_gnn_")}
    m = {k[7:]: v for k, v in f.items() if k.startswith("L1_gnn_")}
    T = lambda w: w.transpose(0, 2, 1)
    more = lambda v: np.concatenate([v, z(1, *v.shape[1:])])
    a["w_qs"] = more(np.concatenate([T(n["Wq"]), T(n["Ws"])], 2)).reshape((L + 1) * P, QS)
    wide = lambda v, fill: np.concatenate([v.reshape(*v.shape[:-1], HEADS, DH), np.full((*v.shape[:-1], HEADS, 1), fill, np.float32)],
                                          -1).reshape(*v.shape[:-1], HEADS * VW)
    a["w_kv"] = more(np.concatenate([T(n["Wk"]), wide(T(n["Wv"]), 0.0)], 2)).reshape((L + 1) * P, BAND)
    a["w_1"] = T(n["W1"]).reshape(L * P, 4 * HID)
    a["b_1"] = n["b1"].reshape(L, 4, HID).transpose(0, 2, 1).reshape(L * P, 4)
    a["w_2"] = T(n["W2"]).reshape(L, 4, HID, HID).transpose(0, 2, 1, 3).reshape(L * P, 4 * HID)
    a["vec0"] = np.concatenate([n["Wbeta"][:, 0, :], n["ln_g"], n["ln_b"], n["b2"]], 1)
    a["vec_qskv"] = more(np.concatenate([n["bq"], n["bs"], n["bk"], wide(n["bv"], 1.0)], 1))
    a["vec1"] = np.concatenate([n["bi"], n["bo"], m["mb1"], m["mb2"], m["ub1"], m["ub2"], m["ln_g"], m["ln_b"]])[None]
    a["w_i"], a["w_o"] = n["Wi"].T, n["Wo"].T
    a["m_1"] = np.concatenate([m["mw1"][0:64], m["mw1"][64:128]], 1)
    a["m_2"], a["u_1"], a["u_2"] = m["mw2"], m["uw1"], m["uw2"]
    m_1c = z(STACK, NBASIS, STACK, HID)
    for q in range(STACK):
        m_1c[q, :, q] = m["mw1"][128:]
    a["m_1c"] = m_1c.reshape(P, STACK * HID)
    a["ident"] = np.eye(P, dtype=np.float32)
    a["iota"] = np.tile(np.arange(P, dtype=np.float32), (P, 1))
    v = np.arange(VC * P, dtype=np.float32).reshape(VC, P).T
    a["place"] = np.stack([v, np.floor(v / 2)], 1).astype(np.float32)
    a["centers"] = np.tile(-np.linspace(0.0, 10.0, NBASIS, dtype=np.float32), STACK)[:, None]
    return {k: np.ascontiguousarray(v) for k, v in a.items()}


def kernel(**inputs):
    import concourse.bacc as bacc
    from concourse.bass_utils import run_bass_kernel_spmd

    nc = bacc.Bacc("TRN2", target_bir_lowering=False, num_devices=1)
    laid = lay_out(inputs)
    arrays = {f"in_{k}": v for k, v in laid.items()}
    aps = {k: nc.dram_tensor(f"in_{k}", v.shape, mybir.dt.from_np(v.dtype), kind="ExternalInput").ap() for k, v in laid.items()}
    out = nc.dram_tensor("out_0", (N, 64), F32, kind="ExternalOutput").ap()
    build_program(nc, aps, out)
    r = run_bass_kernel_spmd(nc, [arrays], core_ids=[0])
    return r.results[0]["out_0"]
```
